# Optimizing a Trainium2 kernel written in Bass

```python
import numpy as np
import jax
import jax.numpy as jnp

def _softmax(x, axis=-1):
    return jax.nn.softmax(x, axis=axis)

def _gelu(x):
    return jax.nn.gelu(x, approximate=True)

def _silu(x):
    return jax.nn.silu(x)

def _sigmoid(x):
    return jax.nn.sigmoid(x)

def _layernorm(x, axis=-1, eps=1e-05):
    m = jnp.mean(x, axis=axis, keepdims=True)
    v = jnp.var(x, axis=axis, keepdims=True)
    return (x - m) / jnp.sqrt(v + eps)

def _scatter_add(tgt, idx, src, axis=0):
    return tgt.at[idx].add(src)

def _segment_sum(src, seg, n):
    return jax.ops.segment_sum(src, seg, n)
kernel_name = 'mk_seq_preln_d2_jaxref_r8_1dcbd8'

def setup_inputs(seed: int=0):
    np.random.seed(seed)
    _w = jnp.asarray

    def _L0_attn_setup():
        import jax, jax.numpy as jnp
        import numpy as np
        D, B, L, E, H, F = (6, 4, 256, 128, 16, 512)
        DH = E // H
        DECAY = 16.0
        CSCALE = 1.0
        EPS = 1e-05

        def _ln(x, w, b):
            m = jnp.mean(x, axis=-1, keepdims=True)
            v = jnp.mean(jnp.square(x - m), axis=-1, keepdims=True)
            return (x - m) * jax.lax.rsqrt(v + EPS) * w + b
        key = jax.random.key(seed)
        ks = jax.random.split(key, 10)
        s = 0.02
        f32 = jnp.float32
        return {'x': jax.random.normal(ks[0], (B, L, E), f32), 'Wq': jax.random.normal(ks[1], (D, E, E), f32) * s, 'Wk': jax.random.normal(ks[2], (D, E, E), f32) * s, 'bq': jnp.zeros((D, E), f32), 'bk': jnp.zeros((D, E), f32), 'ln1_w': jnp.ones((D, E), f32), 'ln1_b': jnp.zeros((D, E), f32), 'ln2_w': jnp.ones((D, E), f32), 'ln2_b': jnp.zeros((D, E), f32), 'ln3_w': jnp.ones((D, E), f32), 'ln3_b': jnp.zeros((D, E), f32), 'W1': jax.random.normal(ks[3], (D, F, E), f32) * s, 'b1': jnp.zeros((D, F), f32), 'W2': jax.random.normal(ks[4], (D, E, F), f32) * s, 'b2': jnp.zeros((D, E), f32)}
    _L0_attn_in = _L0_attn_setup()

    def _L0_ffn_setup():
        import jax, jax.numpy as jnp
        import numpy as np
        B, S, D, E, F, K = (4, 128, 128, 8, 352, 1)
        key = jax.random.key(seed)
        ks = jax.random.split(key, 8)
        sc = 0.02
        return {'x_bsD': jax.random.normal(ks[0], (B, S, D), jnp.float32), 'router_DE': jax.random.normal(ks[1], (D, E), jnp.float32) * sc, 'w1_eDF': jax.random.normal(ks[2], (E, D, F), jnp.float32) * sc, 'w3_eDF': jax.random.normal(ks[3], (E, D, F), jnp.float32) * sc, 'w2_eFD': jax.random.normal(ks[4], (E, F, D), jnp.float32) * sc, 'ws1_DF': jax.random.normal(ks[5], (D, F), jnp.float32) * sc, 'ws3_DF': jax.random.normal(ks[6], (D, F), jnp.float32) * sc, 'ws2_FD': jax.random.normal(ks[7], (F, D), jnp.float32) * sc}
    _L0_ffn_in = _L0_ffn_setup()

    def _L1_attn_setup():
        import jax, jax.numpy as jnp
        import numpy as np
        D_MODEL, D_STATE, D_CONV, EXPAND = (128, 16, 4, 2)
        D_INNER = EXPAND * D_MODEL
        DT_RANK = -(-D_MODEL // 16)
        B_SZ, L_SEQ = (2, 256)

        def _silu(x):
            return x * jax.nn.sigmoid(x)

        def _mamba_block(seq, ln_g, ln_b, in_proj_w, conv_w, conv_b, x_proj_w, dt_proj_w, dt_proj_b, A_log, D, out_proj_w, res_scale):
            B, L, _ = seq.shape
            mu = jnp.mean(seq, -1, keepdims=True)
            var = jnp.mean(jnp.square(seq - mu), -1, keepdims=True)
            xn = (seq - mu) * jax.lax.rsqrt(var + 1e-05) * ln_g + ln_b
            xz = jnp.einsum('bld,ed->ble', xn, in_proj_w)
            x, z = jnp.split(xz, 2, axis=-1)
            x_pad = jnp.pad(x, ((0, 0), (D_CONV - 1, 0), (0, 0)))
            xc = conv_b
            for k in range(D_CONV):
                xc = xc + x_pad[:, k:k + L, :] * conv_w[:, k]
            x = _silu(xc)
            x_dbl = jnp.einsum('bld,ed->ble', x, x_proj_w)
            dt = jax.nn.softplus(jnp.einsum('blr,dr->bld', x_dbl[..., :DT_RANK], dt_proj_w) + dt_proj_b)
            Bm = x_dbl[..., DT_RANK:DT_RANK + D_STATE]
            Cm = x_dbl[..., DT_RANK + D_STATE:]
            A = -jnp.exp(A_log)

            def step(h, inputs):
                dt_t, B_t, C_t, x_t = inputs
                dA = jnp.exp(dt_t[..., None] * A)
                h = h * dA + (dt_t * x_t)[..., None] * B_t[:, None, :]
                y = jnp.einsum('bds,bs->bd', h, C_t)
                return (h, y)
            h0 = jnp.zeros((B, D_INNER, D_STATE), x.dtype)
            _, ys = jax.lax.scan(step, h0, (jnp.swapaxes(dt, 0, 1), jnp.swapaxes(Bm, 0, 1), jnp.swapaxes(Cm, 0, 1), jnp.swapaxes(x, 0, 1)))
            y = jnp.swapaxes(ys, 0, 1) + D * x
            y = y * _silu(z)
            out = jnp.einsum('ble,de->bld', y, out_proj_w)
            return seq + res_scale * out
        key = jax.random.key(seed)
        ks = jax.random.split(key, 12)
        s = lambda k, shp, sc: jax.random.normal(k, shp, dtype=jnp.float32) * sc
        inp = {'seq': s(ks[0], (B_SZ, L_SEQ, D_MODEL), 1.0), 'ln_g': jnp.ones((D_MODEL,), jnp.float32), 'ln_b': jnp.zeros((D_MODEL,), jnp.float32), 'in_proj_w': s(ks[1], (2 * D_INNER, D_MODEL), 0.02), 'conv_w': s(ks[2], (D_INNER, D_CONV), 0.2), 'conv_b': jnp.zeros((D_INNER,), jnp.float32), 'x_proj_w': s(ks[3], (DT_RANK + 2 * D_STATE, D_INNER), 0.02), 'dt_proj_w': s(ks[4], (D_INNER, DT_RANK), 0.1), 'dt_proj_b': jnp.log(jnp.expm1(jax.random.uniform(ks[5], (D_INNER,), jnp.float32, 0.001, 0.1))), 'A_log': jnp.log(jnp.broadcast_to(jnp.arange(1, D_STATE + 1, dtype=jnp.float32), (D_INNER, D_STATE))), 'D': jnp.ones((D_INNER,), jnp.float32), 'out_proj_w': s(ks[6], (D_MODEL, D_INNER), 0.02), 'res_scale': jnp.float32(0.5)}
        return inp
    _L1_attn_in = _L1_attn_setup()

    def _L1_ffn_setup():
        import jax, jax.numpy as jnp
        import numpy as np
        DIM = 128
        DEPTH = 2
        HEADS = 8
        DIM_HEAD = 64
        WINDOW = 64
        INNER = HEADS * DIM_HEAD
        HID = int(DIM * 4 * 2 / 3)
        B, N = (2, 1024)
        QK_SCALE = 8.0

        def shift_token(t):
            t1, t2 = jnp.split(t, 2, axis=-1)
            t2 = jnp.pad(t2, ((0, 0), (1, 0), (0, 0)))[:, :-1]
            return jnp.concatenate([t1, t2], axis=-1)

        def l2norm(t):
            return t / jnp.clip(jnp.linalg.norm(t, axis=-1, keepdims=True), 1e-12)

        def rotate_half(x):
            x1, x2 = jnp.split(x, 2, axis=-1)
            return jnp.concatenate([-x2, x1], axis=-1)

        def rotary_xpos(q, k):
            n = q.shape[-2]
            half_idx = jnp.arange(0, DIM_HEAD, 2, dtype=jnp.float32)
            inv_freq = 1.0 / 10000.0 ** (half_idx / DIM_HEAD)
            t = jnp.arange(n, dtype=jnp.float32)
            freqs = t[:, None] * inv_freq[None, :]
            freqs = jnp.concatenate([freqs, freqs], axis=-1)
            base = (half_idx + 0.4 * DIM_HEAD) / (1.4 * DIM_HEAD)
            power = (t - n // 2) / float(WINDOW // 2)
            scale = base[None, :] ** power[:, None]
            scale = jnp.concatenate([scale, scale], axis=-1)
            cos, sin = (jnp.cos(freqs), jnp.sin(freqs))
            q = q * cos * scale + rotate_half(q) * sin * scale
            k = k * cos / scale + rotate_half(k) * sin / scale
            return (q, k)

        def local_attention(q, k, v):
            b, h, n, d = q.shape
            w = n // WINDOW
            bq = q.reshape(b, h, w, WINDOW, d) * QK_SCALE
            bk = k.reshape(b, h, w, WINDOW, d)
            bv = v.reshape(b, h, w, WINDOW, d)

            def look_around(t):
                p = jnp.pad(t, ((0, 0), (0, 0), (1, 0), (0, 0), (0, 0)))
                return jnp.concatenate([p[:, :, :w], p[:, :, 1:]], axis=3)
            bk, bv = (look_around(bk), look_around(bv))
            bt = jnp.arange(n).reshape(w, WINDOW)
            btp = jnp.pad(bt, ((1, 0), (0, 0)), constant_values=-1)
            btk = jnp.concatenate([btp[:w], btp[1:]], axis=1)
            sim = jnp.einsum('bhwid,bhwjd->bhwij', bq, bk)
            i = bt[:, :, None]
            j = btk[:, None, :]
            mask = (i < j) | (i > j + WINDOW) | (j == -1)
            sim = jnp.where(mask, -jnp.finfo(sim.dtype).max, sim)
            attn = jax.nn.softmax(sim, axis=-1)
            out = jnp.einsum('bhwij,bhwjd->bhwid', attn, bv)
            return out.reshape(b, h, n, d)

        def _layer(x, wqkv, qs, ksc, wo, lg, lb, w1, b1, w2, b2):
            b, n, _ = x.shape
            h = shift_token(x)
            qkv = h @ wqkv
            q, k, v = jnp.split(qkv, 3, axis=-1)
            to_heads = lambda t: t.reshape(b, n, HEADS, DIM_HEAD).transpose(0, 2, 1, 3)
            q, k, v = (to_heads(q), to_heads(k), to_heads(v))
            q = l2norm(q) * qs
            k = l2norm(k) * ksc
            q, k = rotary_xpos(q, k)
            o = local_attention(q, k, v)
            o = o.transpose(0, 2, 1, 3).reshape(b, n, INNER)
            x = x + o @ wo
            h = shift_token(x)
            mu = h.mean(-1, keepdims=True)
            var = h.var(-1, keepdims=True)
            h = (h - mu) / jnp.sqrt(var + 1e-05) * lg + lb
            h = h @ w1 + b1
            a, g = jnp.split(h, 2, axis=-1)
            h = a * jax.nn.gelu(g, approximate=False)
            x = x + h @ w2 + b2
            return x
        key = jax.random.key(seed)
        ks = jax.random.split(key, 6)
        return {'x': jax.random.normal(ks[0], (B, N, DIM), jnp.float32), 'wqkv': jax.random.normal(ks[1], (DEPTH, DIM, 3 * INNER), jnp.float32) * 0.02, 'q_scale': jnp.ones((DEPTH, DIM_HEAD), jnp.float32), 'k_scale': jnp.ones((DEPTH, DIM_HEAD), jnp.float32), 'wo': jax.random.normal(ks[2], (DEPTH, INNER, DIM), jnp.float32) * 0.02, 'ln_g': jnp.ones((DEPTH, DIM), jnp.float32), 'ln_b': jnp.zeros((DEPTH, DIM), jnp.float32), 'w1': jax.random.normal(ks[3], (DEPTH, DIM, 2 * HID), jnp.float32) * 0.02, 'b1': jnp.zeros((DEPTH, 2 * HID), jnp.float32), 'w2': jax.random.normal(ks[4], (DEPTH, HID, DIM), jnp.float32) * 0.02, 'b2': jnp.zeros((DEPTH, DIM), jnp.float32)}
    _L1_ffn_in = _L1_ffn_setup()
    _d = {'L0_attn_x': _L0_attn_in['x'], 'L0_attn_Wq': _L0_attn_in['Wq'], 'L0_attn_Wk': _L0_attn_in['Wk'], 'L0_attn_bq': _L0_attn_in['bq'], 'L0_attn_bk': _L0_attn_in['bk'], 'L0_attn_ln1_w': _L0_attn_in['ln1_w'], 'L0_attn_ln1_b': _L0_attn_in['ln1_b'], 'L0_attn_ln2_w': _L0_attn_in['ln2_w'], 'L0_attn_ln2_b': _L0_attn_in['ln2_b'], 'L0_attn_ln3_w': _L0_attn_in['ln3_w'], 'L0_attn_ln3_b': _L0_attn_in['ln3_b'], 'L0_attn_W1': _L0_attn_in['W1'], 'L0_attn_b1': _L0_attn_in['b1'], 'L0_attn_W2': _L0_attn_in['W2'], 'L0_attn_b2': _L0_attn_in['b2'], 'L0_ffn_router_DE': _L0_ffn_in['router_DE'], 'L0_ffn_w1_eDF': _L0_ffn_in['w1_eDF'], 'L0_ffn_w3_eDF': _L0_ffn_in['w3_eDF'], 'L0_ffn_w2_eFD': _L0_ffn_in['w2_eFD'], 'L0_ffn_ws1_DF': _L0_ffn_in['ws1_DF'], 'L0_ffn_ws3_DF': _L0_ffn_in['ws3_DF'], 'L0_ffn_ws2_FD': _L0_ffn_in['ws2_FD'], 'L1_attn_ln_g': _L1_attn_in['ln_g'], 'L1_attn_ln_b': _L1_attn_in['ln_b'], 'L1_attn_in_proj_w': _L1_attn_in['in_proj_w'], 'L1_attn_conv_w': _L1_attn_in['conv_w'], 'L1_attn_conv_b': _L1_attn_in['conv_b'], 'L1_attn_x_proj_w': _L1_attn_in['x_proj_w'], 'L1_attn_dt_proj_w': _L1_attn_in['dt_proj_w'], 'L1_attn_dt_proj_b': _L1_attn_in['dt_proj_b'], 'L1_attn_A_log': _L1_attn_in['A_log'], 'L1_attn_D': _L1_attn_in['D'], 'L1_attn_out_proj_w': _L1_attn_in['out_proj_w'], 'L1_attn_res_scale': _L1_attn_in['res_scale'], 'L1_ffn_wqkv': _L1_ffn_in['wqkv'], 'L1_ffn_q_scale': _L1_ffn_in['q_scale'], 'L1_ffn_k_scale': _L1_ffn_in['k_scale'], 'L1_ffn_wo': _L1_ffn_in['wo'], 'L1_ffn_ln_g': _L1_ffn_in['ln_g'], 'L1_ffn_ln_b': _L1_ffn_in['ln_b'], 'L1_ffn_w1': _L1_ffn_in['w1'], 'L1_ffn_b1': _L1_ffn_in['b1'], 'L1_ffn_w2': _L1_ffn_in['w2'], 'L1_ffn_b2': _L1_ffn_in['b2']}
    _x0 = _d['L0_attn_x']
    _d['L0_attn_x'] = jax.random.normal(jax.random.fold_in(jax.random.key(seed), 1), (8, 256, 128), dtype=_x0.dtype)
    del _x0
    return _d

def reference(L0_attn_x, L0_attn_Wq, L0_attn_Wk, L0_attn_bq, L0_attn_bk, L0_attn_ln1_w, L0_attn_ln1_b, L0_attn_ln2_w, L0_attn_ln2_b, L0_attn_ln3_w, L0_attn_ln3_b, L0_attn_W1, L0_attn_b1, L0_attn_W2, L0_attn_b2, L0_ffn_router_DE, L0_ffn_w1_eDF, L0_ffn_w3_eDF, L0_ffn_w2_eFD, L0_ffn_ws1_DF, L0_ffn_ws3_DF, L0_ffn_ws2_FD, L1_attn_ln_g, L1_attn_ln_b, L1_attn_in_proj_w, L1_attn_conv_w, L1_attn_conv_b, L1_attn_x_proj_w, L1_attn_dt_proj_w, L1_attn_dt_proj_b, L1_attn_A_log, L1_attn_D, L1_attn_out_proj_w, L1_attn_res_scale, L1_ffn_wqkv, L1_ffn_q_scale, L1_ffn_k_scale, L1_ffn_wo, L1_ffn_ln_g, L1_ffn_ln_b, L1_ffn_w1, L1_ffn_b1, L1_ffn_w2, L1_ffn_b2):

    def _L0_attn_ref(x, Wq, Wk, bq, bk, ln1_w, ln1_b, ln2_w, ln2_b, ln3_w, ln3_b, W1, b1, W2, b2):
        import jax, jax.numpy as jnp
        import numpy as np
        D, B, L, E, H, F = (6, 4, 256, 128, 16, 512)
        DH = E // H
        DECAY = 16.0
        CSCALE = 1.0
        EPS = 1e-05

        def _ln(x, w, b):
            m = jnp.mean(x, axis=-1, keepdims=True)
            v = jnp.mean(jnp.square(x - m), axis=-1, keepdims=True)
            return (x - m) * jax.lax.rsqrt(v + EPS) * w + b
        seq = x.shape[1]
        pos = jnp.arange(seq)
        rel = jnp.exp(-jnp.abs(pos[:, None] - pos[None, :]).astype(x.dtype) / DECAY)
        inv_sqrt_d = 1.0 / np.sqrt(DH)

        def layer(h, p):
            wq, wk, bq_, bk_, l1w, l1b, l2w, l2b, l3w, l3b, w1, b1_, w2, b2_ = p
            bh, sl, _ = h.shape
            q = (h @ wq.T + bq_).reshape(bh, sl, H, DH)
            k = (h @ wk.T + bk_).reshape(bh, sl, H, DH)
            scores = jnp.einsum('blhd,bmhd->bhlm', q, k) * inv_sqrt_d
            w_avg = jax.nn.softmax(scores, axis=-1).mean(axis=1)
            new_w = jax.nn.softmax(CSCALE * w_avg + rel[None], axis=-1)
            sa = jnp.einsum('blm,bme->ble', new_w, h)
            h1 = _ln(h + sa, l1w, l1b)
            h2 = _ln(h1, l2w, l2b)
            ff = jax.nn.relu(h2 @ w1.T + b1_) @ w2.T + b2_
            return (_ln(h2 + ff, l3w, l3b), None)
        out, _ = jax.lax.scan(layer, x, (Wq, Wk, bq, bk, ln1_w, ln1_b, ln2_w, ln2_b, ln3_w, ln3_b, W1, b1, W2, b2))
        return out

    def _L0_ffn_ref(x_bsD, router_DE, w1_eDF, w3_eDF, w2_eFD, ws1_DF, ws3_DF, ws2_FD):
        import jax, jax.numpy as jnp
        import numpy as np
        B, S, D, E, F, K = (4, 128, 128, 8, 352, 1)
        b, s, d = x_bsD.shape
        a = b * s
        x_aD = x_bsD.reshape(a, d)
        scores_aE = x_aD @ router_DE
        vals_aK, idx_aK = jax.lax.top_k(scores_aE, K)
        masked_aE = jnp.full_like(scores_aE, -jnp.inf).at[jnp.arange(a)[:, None], idx_aK].set(vals_aK)
        gates_Ea = jax.nn.sigmoid(masked_aE).T
        routed_in_EaD = jax.lax.stop_gradient(gates_Ea[:, :, None] * x_aD[None, :, :])
        mid_EaF = jax.nn.silu(jnp.einsum('ead,edf->eaf', routed_in_EaD, w1_eDF)) * jnp.einsum('ead,edf->eaf', routed_in_EaD, w3_eDF)
        routed_out_EaD = jnp.einsum('eaf,efd->ead', mid_EaF, w2_eFD)
        shared_aD = jax.nn.silu(x_aD @ ws1_DF) * (x_aD @ ws3_DF) @ ws2_FD
        out_aD = shared_aD + routed_out_EaD.sum(axis=0)
        return out_aD.reshape(b, s, d)

    def _L1_attn_ref(seq, ln_g, ln_b, in_proj_w, conv_w, conv_b, x_proj_w, dt_proj_w, dt_proj_b, A_log, D, out_proj_w, res_scale):
        import jax, jax.numpy as jnp
        import numpy as np
        D_MODEL, D_STATE, D_CONV, EXPAND = (128, 16, 4, 2)
        D_INNER = EXPAND * D_MODEL
        DT_RANK = -(-D_MODEL // 16)
        B_SZ, L_SEQ = (2, 256)

        def _silu(x):
            return x * jax.nn.sigmoid(x)

        def _mamba_block(seq, ln_g, ln_b, in_proj_w, conv_w, conv_b, x_proj_w, dt_proj_w, dt_proj_b, A_log, D, out_proj_w, res_scale):
            B, L, _ = seq.shape
            mu = jnp.mean(seq, -1, keepdims=True)
            var = jnp.mean(jnp.square(seq - mu), -1, keepdims=True)
            xn = (seq - mu) * jax.lax.rsqrt(var + 1e-05) * ln_g + ln_b
            xz = jnp.einsum('bld,ed->ble', xn, in_proj_w)
            x, z = jnp.split(xz, 2, axis=-1)
            x_pad = jnp.pad(x, ((0, 0), (D_CONV - 1, 0), (0, 0)))
            xc = conv_b
            for k in range(D_CONV):
                xc = xc + x_pad[:, k:k + L, :] * conv_w[:, k]
            x = _silu(xc)
            x_dbl = jnp.einsum('bld,ed->ble', x, x_proj_w)
            dt = jax.nn.softplus(jnp.einsum('blr,dr->bld', x_dbl[..., :DT_RANK], dt_proj_w) + dt_proj_b)
            Bm = x_dbl[..., DT_RANK:DT_RANK + D_STATE]
            Cm = x_dbl[..., DT_RANK + D_STATE:]
            A = -jnp.exp(A_log)

            def step(h, inputs):
                dt_t, B_t, C_t, x_t = inputs
                dA = jnp.exp(dt_t[..., None] * A)
                h = h * dA + (dt_t * x_t)[..., None] * B_t[:, None, :]
                y = jnp.einsum('bds,bs->bd', h, C_t)
                return (h, y)
            h0 = jnp.zeros((B, D_INNER, D_STATE), x.dtype)
            _, ys = jax.lax.scan(step, h0, (jnp.swapaxes(dt, 0, 1), jnp.swapaxes(Bm, 0, 1), jnp.swapaxes(Cm, 0, 1), jnp.swapaxes(x, 0, 1)))
            y = jnp.swapaxes(ys, 0, 1) + D * x
            y = y * _silu(z)
            out = jnp.einsum('ble,de->bld', y, out_proj_w)
            return seq + res_scale * out
        return _mamba_block(seq, ln_g, ln_b, in_proj_w, conv_w, conv_b, x_proj_w, dt_proj_w, dt_proj_b, A_log, D, out_proj_w, res_scale)

    def _L1_ffn_ref(x, wqkv, q_scale, k_scale, wo, ln_g, ln_b, w1, b1, w2, b2):
        import jax, jax.numpy as jnp
        import numpy as np
        DIM = 128
        DEPTH = 2
        HEADS = 8
        DIM_HEAD = 64
        WINDOW = 64
        INNER = HEADS * DIM_HEAD
        HID = int(DIM * 4 * 2 / 3)
        B, N = (2, 1024)
        QK_SCALE = 8.0

        def shift_token(t):
            t1, t2 = jnp.split(t, 2, axis=-1)
            t2 = jnp.pad(t2, ((0, 0), (1, 0), (0, 0)))[:, :-1]
            return jnp.concatenate([t1, t2], axis=-1)

        def l2norm(t):
            return t / jnp.clip(jnp.linalg.norm(t, axis=-1, keepdims=True), 1e-12)

        def rotate_half(x):
            x1, x2 = jnp.split(x, 2, axis=-1)
            return jnp.concatenate([-x2, x1], axis=-1)

        def rotary_xpos(q, k):
            n = q.shape[-2]
            half_idx = jnp.arange(0, DIM_HEAD, 2, dtype=jnp.float32)
            inv_freq = 1.0 / 10000.0 ** (half_idx / DIM_HEAD)
            t = jnp.arange(n, dtype=jnp.float32)
            freqs = t[:, None] * inv_freq[None, :]
            freqs = jnp.concatenate([freqs, freqs], axis=-1)
            base = (half_idx + 0.4 * DIM_HEAD) / (1.4 * DIM_HEAD)
            power = (t - n // 2) / float(WINDOW // 2)
            scale = base[None, :] ** power[:, None]
            scale = jnp.concatenate([scale, scale], axis=-1)
            cos, sin = (jnp.cos(freqs), jnp.sin(freqs))
            q = q * cos * scale + rotate_half(q) * sin * scale
            k = k * cos / scale + rotate_half(k) * sin / scale
            return (q, k)

        def local_attention(q, k, v):
            b, h, n, d = q.shape
            w = n // WINDOW
            bq = q.reshape(b, h, w, WINDOW, d) * QK_SCALE
            bk = k.reshape(b, h, w, WINDOW, d)
            bv = v.reshape(b, h, w, WINDOW, d)

            def look_around(t):
                p = jnp.pad(t, ((0, 0), (0, 0), (1, 0), (0, 0), (0, 0)))
                return jnp.concatenate([p[:, :, :w], p[:, :, 1:]], axis=3)
            bk, bv = (look_around(bk), look_around(bv))
            bt = jnp.arange(n).reshape(w, WINDOW)
            btp = jnp.pad(bt, ((1, 0), (0, 0)), constant_values=-1)
            btk = jnp.concatenate([btp[:w], btp[1:]], axis=1)
            sim = jnp.einsum('bhwid,bhwjd->bhwij', bq, bk)
            i = bt[:, :, None]
            j = btk[:, None, :]
            mask = (i < j) | (i > j + WINDOW) | (j == -1)
            sim = jnp.where(mask, -jnp.finfo(sim.dtype).max, sim)
            attn = jax.nn.softmax(sim, axis=-1)
            out = jnp.einsum('bhwij,bhwjd->bhwid', attn, bv)
            return out.reshape(b, h, n, d)

        def _layer(x, wqkv, qs, ksc, wo, lg, lb, w1, b1, w2, b2):
            b, n, _ = x.shape
            h = shift_token(x)
            qkv = h @ wqkv
            q, k, v = jnp.split(qkv, 3, axis=-1)
            to_heads = lambda t: t.reshape(b, n, HEADS, DIM_HEAD).transpose(0, 2, 1, 3)
            q, k, v = (to_heads(q), to_heads(k), to_heads(v))
            q = l2norm(q) * qs
            k = l2norm(k) * ksc
            q, k = rotary_xpos(q, k)
            o = local_attention(q, k, v)
            o = o.transpose(0, 2, 1, 3).reshape(b, n, INNER)
            x = x + o @ wo
            h = shift_token(x)
            mu = h.mean(-1, keepdims=True)
            var = h.var(-1, keepdims=True)
            h = (h - mu) / jnp.sqrt(var + 1e-05) * lg + lb
            h = h @ w1 + b1
            a, g = jnp.split(h, 2, axis=-1)
            h = a * jax.nn.gelu(g, approximate=False)
            x = x + h @ w2 + b2
            return x
        for l in range(DEPTH):
            x = _layer(x, wqkv[l], q_scale[l], k_scale[l], wo[l], ln_g[l], ln_b[l], w1[l], b1[l], w2[l], b2[l])
        return x
    x = L0_attn_x
    x = x + _L0_attn_ref(_layernorm(x, axis=-1), L0_attn_Wq, L0_attn_Wk, L0_attn_bq, L0_attn_bk, L0_attn_ln1_w, L0_attn_ln1_b, L0_attn_ln2_w, L0_attn_ln2_b, L0_attn_ln3_w, L0_attn_ln3_b, L0_attn_W1, L0_attn_b1, L0_attn_W2, L0_attn_b2)
    x = x + _L0_ffn_ref(_layernorm(x, axis=-1), L0_ffn_router_DE, L0_ffn_w1_eDF, L0_ffn_w3_eDF, L0_ffn_w2_eFD, L0_ffn_ws1_DF, L0_ffn_ws3_DF, L0_ffn_ws2_FD)
    x = x + _L1_attn_ref(_layernorm(x, axis=-1), L1_attn_ln_g, L1_attn_ln_b, L1_attn_in_proj_w, L1_attn_conv_w, L1_attn_conv_b, L1_attn_x_proj_w, L1_attn_dt_proj_w, L1_attn_dt_proj_b, L1_attn_A_log, L1_attn_D, L1_attn_out_proj_w, L1_attn_res_scale)
    x = x + _L1_ffn_ref(_layernorm(x, axis=-1), L1_ffn_wqkv, L1_ffn_q_scale, L1_ffn_k_scale, L1_ffn_wo, L1_ffn_ln_g, L1_ffn_ln_b, L1_ffn_w1, L1_ffn_b1, L1_ffn_w2, L1_ffn_b2)
    return x

_drawn_inputs = setup_inputs


def setup_inputs(seed=0):
    import zlib

    import numpy as np

    out = dict(_drawn_inputs(seed))
    spreads = {'L0_attn_bq': (0.0, 0.1),
     'L0_attn_bk': (0.0, 0.1),
     'L0_attn_ln1_w': (1.0, 0.2),
     'L0_attn_ln1_b': (0.0, 0.1),
     'L0_attn_ln2_w': (1.0, 0.2),
     'L0_attn_ln2_b': (0.0, 0.1),
     'L0_attn_ln3_w': (1.0, 0.2),
     'L0_attn_ln3_b': (0.0, 0.1),
     'L0_attn_b1': (0.0, 0.1),
     'L0_attn_b2': (0.0, 0.1),
     'L1_attn_ln_g': (1.0, 0.2),
     'L1_attn_ln_b': (0.0, 0.1),
     'L1_attn_conv_b': (0.0, 0.1),
     'L1_attn_D': (1.0, 0.2),
     'L1_ffn_q_scale': (1.0, 0.2),
     'L1_ffn_k_scale': (1.0, 0.2),
     'L1_ffn_ln_g': (1.0, 0.2),
     'L1_ffn_ln_b': (0.0, 0.1),
     'L1_ffn_b1': (0.0, 0.1),
     'L1_ffn_b2': (0.0, 0.1)}
    factors = {}
    for name, (base, spread) in spreads.items():
        noise = np.random.default_rng([zlib.crc32(name.encode()), seed]).standard_normal(out[name].shape)
        drawn = base * np.exp(spread * noise) if base else spread * noise
        out[name] = jnp.asarray(drawn.astype(out[name].dtype))
    for name, factor in factors.items():
        out[name] = (out[name] * factor).astype(out[name].dtype)
    return out
```

```python
from contextlib import ExitStack

import numpy as np
import concourse.bass as bass
from concourse import mybir

ALU = mybir.AluOpType
ACT = mybir.ActivationFunctionType
AX = mybir.AxisListType
F32 = mybir.dt.float32
BF16 = mybir.dt.bfloat16

P = 128
SEQS, L, E = 8, 256, 128
T = SEQS * L // P
TPS = L // P
NTOK = SEQS * L
EPS = 1e-5
GRP = 512
NG = NTOK // GRP
TPG = GRP // P

LAYERS, HEADS, HID_A = 6, 16, 512
DH = E // HEADS
CH = 4
HG = HEADS // CH
FC = HID_A // P
DECAY = 16.0
C_BQ, C_BK, C_B1, C_B2, C_L2W, C_L2B, C_L3W, C_L3B, NCOL = 0, 1, 2, 6, 7, 8, 9, 10, 11


class Chain:

    def __init__(self, eng, sem, base=0):
        self.eng, self.sem, self.base, self.n = eng, sem, base, 0

    def link(self, ins):
        self.n += 1
        ins.then_inc(self.sem, 1)
        self.eng.wait_ge(self.sem, self.base + self.n)


def moments(v, chain, b, n):
    st = b["st"][:, 0:n, :]
    sm = b["sm"][:, 0:n, :]
    chain.link(v.tensor_tensor(sm, st[:, :, 1:3], st[:, :, 4:6], ALU.add))
    chain.link(v.tensor_tensor(b["d"][:, 0:n], st[:, :, 1], st[:, :, 4], ALU.subtract))
    chain.link(v.scalar_tensor_tensor(b["dd"][:, 0:n], b["d"][:, 0:n], E / 4.0, b["d"][:, 0:n], ALU.mult, ALU.mult))
    chain.link(v.tensor_tensor(b["dd"][:, 0:n], b["dd"][:, 0:n], sm[:, :, 1], ALU.add))
    chain.link(v.tensor_scalar(b["mean"][:, 0:n], sm[:, :, 0], 0.5, None, ALU.mult))
    return v.tensor_scalar(b["var"][:, 0:n], b["dd"][:, 0:n], 1.0 / E, EPS, ALU.mult, ALU.add)


def moment_buffers(sb, name, n):
    return {k: sb(f"{name}_{k}", [P, n] + ([w] if w else []))
            for k, w in (("st", 6), ("sm", 2), ("d", 0), ("dd", 0), ("mean", 0), ("var", 0), ("rstd", 0))}


def stage_a(nc, d, x_tok, ident, minus_half):
    with ExitStack() as ctx:
        def sb(name, shape):
            return ctx.enter_context(nc.sbuf_tensor("a_" + name, shape, F32))

        def ps(name, shape):
            return ctx.enter_context(nc.psum_tensor("a_" + name, shape, F32))

        def sem(name):
            return ctx.enter_context(nc.semaphore("a_" + name))

        h_tok = sb("h_tok", [P, T, E])
        hT = sb("hT", [P, NTOK])
        r_tok = sb("r_tok", [P, T, E])
        n1 = sb("n1", [P, T, E])
        h2T = sb("h2T", [P, NTOK])
        n3 = [sb(f"n3_{u}", [P, TPG, E]) for u in range(2)]
        qT = sb("qT", [P, L])
        kT = [sb(f"kT{u}", [P, L]) for u in range(2)]
        qm = [sb(f"qm{u}", [P, HEADS, L]) for u in range(2)]
        head_mask = sb("head_mask", [P, HEADS])
        prob = [sb(f"prob{u}", [P, CH, L]) for u in range(2)]
        negmax = [sb(f"negmax{u}", [P, CH]) for u in range(2)]
        rowsum = [sb(f"rowsum{u}", [P, CH]) for u in range(2)]
        rowinv = [sb(f"rowinv{u}", [P, CH]) for u in range(2)]
        acc = [sb(f"acc{u}", [P, TPS, L]) for u in range(2)]
        odd = sb("odd", [P, TPS, L])
        mix = sb("mix", [P, TPS, L])
        mixT = sb("mixT", [P, TPS, L])
        mixsum = sb("mixsum", [P, TPS])
        mixinv = sb("mixinv", [P, TPS])
        ffr = [sb(f"ffr{u}", [P, GRP]) for u in range(2)]
        act = sb("act", [P, FC, GRP])
        rel = sb("rel", [P, TPS, L])
        wq = sb("wq", [P, P])
        wk = sb("wk", [P, P])
        w1 = sb("w1", [P, HID_A])
        w2 = sb("w2", [P, FC, E])
        cols = sb("cols", [P, NCOL])
        rows = sb("rows", [P, 4, E])
        bqs = sb("bqs", [P, 1])
        qscale = sb("qscale", [P, 1])
        mb = [moment_buffers(sb, f"m{u}", T // 2) for u in range(2)]

        psS = [ps(f"scores{u}", [P, CH, L]) for u in range(2)]
        psP = [ps(f"proj{u}", [P, 2, L]) for u in range(2)]
        psT = ps("turn", [P, GRP])
        psA = ps("attn", [P, GRP])
        psF = [psS[0][:, 0:2, :].rearrange("p c m -> p (c m)"), psS[0][:, 2:4, :].rearrange("p c m -> p (c m)")]
        psY = [psS[1][:, 0:2, :].rearrange("p c m -> p (c m)"), psS[1][:, 2:4, :].rearrange("p c m -> p (c m)")]
        psX = [psP[u][:, :, :].rearrange("p c m -> p (c m)") for u in range(2)]

        names = ("const_in", "qk_weights_in", "mlp_weights_in", "q_bias", "proj_ready", "qk_ready", "qm_ready", "odd_ready", "scores_ready",
                 "negmax_ready", "exp_done", "recip_done", "sum_done", "acc_step", "mix_ready", "mix_turned",
                 "mixT_ready", "attn_ready", "r_ready", "chain", "var_ready", "rstd_ready", "norm1_ready",
                 "n1_ready", "gain_done", "n2_ready", "n2_turned", "h2T_ready", "hidden_ready", "relu_even",
                 "relu_odd", "mlp_ready", "ffr_ready", "ffr_turned", "n3_ready", "n3_turned", "hT_ready",
                 "h_tok_ready", "h_ln_ready", "h_turned", "x_ready", "mixinv_done", "stats_done")
        s = {n: sem(n) for n in names}
        GPL = SEQS * 8
        G8 = 8
        chain_sem = s["chain"]
        CHAIN_PER_LAYER = 8 * 5
        SLOTS = 2

        with nc.Block() as block:
            @block.sync
            def _(sp):
                sp.dma_start(rel[:], d["rel"].rearrange("(t p) m -> p t m", p=P)).then_inc(s["const_in"], 16)
                sp.dma_start(head_mask[:], d["a_heads"]).then_inc(s["const_in"], 16)

                def load_qk(l):
                    sp.dma_start(wq[:], d["a_wq"][l]).then_inc(s["qk_weights_in"], 16)
                    sp.dma_start(wk[:], d["a_wk"][l]).then_inc(s["qk_weights_in"], 16)

                def load_mlp(l):
                    sp.dma_start(w1[:], d["a_w1"][l]).then_inc(s["mlp_weights_in"], 16)
                    sp.dma_start(w2[:], d["a_w2"][l]).then_inc(s["mlp_weights_in"], 16)
                    sp.dma_start(cols[:], d["a_cols"][l]).then_inc(s["mlp_weights_in"], 16)
                    sp.dma_start(rows[:], d["a_rows"][l]).then_inc(s["mlp_weights_in"], 16)

                load_mlp(0)
                load_qk(0)
                with sp.Fori(0, LAYERS - 1) as l:
                    sp.wait_ge(s["proj_ready"], (l + 1) * SEQS)
                    load_qk(l + 1)
                    sp.wait_ge(s["h_tok_ready"], (l + 1) * NG + SLOTS)
                    sp.wait_ge(s["hT_ready"], (l + 2) * NG)
                    load_mlp(l + 1)

            def h_affine(g, l, k):
                sl = slice(k * TPG, (k + 1) * TPG)
                g.wait_ge(s["n3_ready"], l * NG + k + 1 + SLOTS)
                g.tensor_tensor(h_tok[:, sl, :], n3[k % 2][:], rows[:, 2:3, :].broadcast_to([P, TPG, E]),
                                ALU.mult).then_inc(s["gain_done"], 1)
                g.wait_ge(s["gain_done"], l * (2 + NG) + 2 + k + 1)
                g.tensor_tensor(h_tok[:, sl, :], h_tok[:, sl, :], rows[:, 3:4, :].broadcast_to([P, TPG, E]),
                                ALU.add).then_inc(s["h_tok_ready"], 1)

            @block.gpsimd
            def _(g):
                g.memset(qscale[:], float(DH) ** -0.5).then_inc(s["q_bias"], 1)

                g.sem_inc(s["h_tok_ready"], SLOTS)
                g.sem_inc(s["qm_ready"], HG)

                def rstd(i, b, n, base):
                    g.wait_ge(s["var_ready"], base + i)
                    g.tensor_tensor(b["rstd"][:, 0:n], b["var"][:, 0:n], minus_half[:, 0:n],
                                    ALU.pow).then_inc(s["rstd_ready"], 1)

                for k in range(NG):
                    rstd(k + 1, mb[k % 2], TPG, 0)
                g.wait_ge(s["q_bias"], 1)
                g.wait_ge(s["const_in"], 32)
                with g.Fori(0, LAYERS) as l:
                    g.wait_ge(s["mlp_weights_in"], (l + 1) * 64)
                    g.tensor_tensor(bqs[:], cols[:, C_BQ:C_BQ + 1], qscale[:], ALU.mult).then_inc(s["q_bias"], 1)
                    for q in range(SEQS):
                        g.wait_ge(s["qk_ready"], l * SEQS * 2 + 2 * q + 1 + SLOTS * 2)
                        g.wait_ge(s["scores_ready"], l * GPL + q * G8 - G8 + SLOTS * G8)
                        for j in range(HG):
                            hs = slice(j * CH, (j + 1) * CH)
                            g.tensor_tensor(qm[q % 2][:, hs, :], qT[:].unsqueeze(1).broadcast_to([P, CH, L]),
                                            head_mask[:, hs].unsqueeze(2).broadcast_to([P, CH, L]), ALU.mult)\
                                .then_inc(s["qm_ready"], 1)
                    base = l * 8 + NG
                    H2 = T // 2
                    for k in range(2):
                        rstd(1 + k, mb[k], H2, base)
                    for k in range(2):
                        sl = slice(k * H2, (k + 1) * H2)
                        g.wait_ge(s["norm1_ready"], l * 2 + k + 1)
                        g.tensor_tensor(n1[:, sl, :], r_tok[:, sl, :], rows[:, 0:1, :].broadcast_to([P, H2, E]),
                                        ALU.mult).then_inc(s["gain_done"], 1)
                        g.wait_ge(s["gain_done"], l * (2 + NG) + k + 1)
                        g.tensor_tensor(n1[:, sl, :], n1[:, sl, :], rows[:, 1:2, :].broadcast_to([P, H2, E]),
                                        ALU.add).then_inc(s["n1_ready"], 1)
                    for k in range(2):
                        rstd(3 + k, mb[k], H2, base)
                    for k in range(NG):
                        rstd(5 + k, mb[k % 2], TPG, base)
                        if k:
                            h_affine(g, l, k - 1)
                    h_affine(g, l, NG - 1)

            @block.scalar
            def _(a):
                a.sem_inc(s["exp_done"], SLOTS)
                a.sem_inc(s["qk_ready"], 2 * SLOTS)
                a.sem_inc(s["mix_ready"], 2 * SLOTS)
                a.sem_inc(s["h2T_ready"], SLOTS)
                a.sem_inc(s["relu_even"], 1)
                for k in range(NG):
                    a.wait_ge(s["h_turned"], k + 1)
                    a.activation(hT[:, k * GRP:(k + 1) * GRP], psX[k % 2], ACT.Copy).then_inc(s["hT_ready"], 1)

                def evac(l, q):
                    a.wait_ge(s["proj_ready"], l * SEQS + q + 1)
                    a.wait_ge(s["qm_ready"], l * SEQS * HG + q * HG + HG)
                    a.activation(qT[:], psP[q % 2][:, 0, :], ACT.Identity, bias=bqs[:],
                                 scale=float(DH) ** -0.5).then_inc(s["qk_ready"], 1)
                    a.activation(kT[q % 2][:], psP[q % 2][:, 1, :], ACT.Identity,
                                 bias=cols[:, C_BK:C_BK + 1]).then_inc(s["qk_ready"], 1)

                def exps(l, q, k):
                    n = q * G8 + k
                    a.wait_ge(s["negmax_ready"], l * GPL + n + 1)
                    a.wait_ge(s["sum_done"], l * GPL + n + 1)
                    for c in range(CH):
                        ins = a.activation(prob[k % 2][:, c, :], psS[k % 2][:, c, :], ACT.Exp,
                                           bias=negmax[k % 2][:, c:c + 1], accum_out=rowsum[k % 2][:, c:c + 1])
                    ins.then_inc(s["exp_done"], 1)

                def mix_exp(l, q):
                    a.wait_ge(s["odd_ready"], l * SEQS * 2 + 2 * q + 2)
                    a.wait_ge(s["mix_turned"], l * SEQS + q + 1)
                    a.wait_ge(s["mixinv_done"], l * SEQS + q + 1)
                    for t in range(TPS):
                        a.activation(mix[:, t, :], acc[q % 2][:, t, :], ACT.Exp, scale=1.0 / HEADS,
                                     accum_out=mixsum[:, t:t + 1]).then_inc(s["mix_ready"], 1)

                def mix_copy(l, q):
                    a.wait_ge(s["mix_turned"], l * SEQS + q + 2)
                    a.wait_ge(s["attn_ready"], l * SEQS + q + 1)
                    a.activation(mixT[:, :, :].rearrange("p t m -> p (t m)"), psT[:], ACT.Copy)\
                        .then_inc(s["mixT_ready"], 1)

                with a.Fori(0, LAYERS) as l:
                    a.wait_ge(s["mlp_weights_in"], (l + 1) * 64)
                    a.wait_ge(s["q_bias"], l + 2)
                    evac(l, 0)
                    for q in range(SEQS):
                        for k in range(G8):
                            exps(l, q, k)
                            if k == 1 and q:
                                mix_exp(l, q - 1)
                            if k == 4 and q:
                                mix_copy(l, q - 1)
                            if k == 2 and q < SEQS - 1:
                                evac(l, q + 1)
                    mix_exp(l, SEQS - 1)
                    mix_copy(l, SEQS - 1)

                    def h2_evac(k):
                        a.wait_ge(s["n2_turned"], l * NG + k + 1)
                        a.activation(h2T[:, k * GRP:(k + 1) * GRP], psX[k % 2], ACT.Identity,
                                     bias=cols[:, C_L2B:C_L2B + 1], scale=cols[:, C_L2W:C_L2W + 1])\
                            .then_inc(s["h2T_ready"], 1)

                    def relu(k, f):
                        a.wait_ge(s["hidden_ready"], l * NG * FC + k * FC + f + 1)
                        a.wait_ge(s["mlp_ready"], l * NG + k + 1)
                        a.activation(act[:, f, :], psF[0], ACT.Relu, bias=cols[:, C_B1 + f:C_B1 + f + 1])\
                            .then_inc(s["relu_even"], 1)

                    def h_evac(k):
                        a.wait_ge(s["n3_turned"], l * NG + k + 1 + SLOTS)
                        a.activation(hT[:, k * GRP:(k + 1) * GRP], psT[:], ACT.Identity,
                                     bias=cols[:, C_L3B:C_L3B + 1], scale=cols[:, C_L3W:C_L3W + 1])\
                            .then_inc(s["hT_ready"], 1)

                    h2_evac(0)
                    h2_evac(1)
                    for k in range(NG):
                        relu(k, 0)
                        relu(k, 2)
                        if k + 2 < NG:
                            h2_evac(k + 2)
                        if k >= 2:
                            h_evac(k - 2)
                    h_evac(NG - 2)
                    h_evac(NG - 1)

            @block.vector
            def _(v):
                v.sem_inc(s["sum_done"], SLOTS)
                v.sem_inc(s["r_ready"], 2)
                v.sem_inc(s["relu_odd"], 1)
                v.sem_inc(s["ffr_ready"], 1)
                v.sem_inc(s["n3_ready"], SLOTS)
                v.sem_inc(s["mixinv_done"], 1)
                chain = Chain(v, chain_sem)

                def stats(src, b, n, signal):
                    for t in range(n):
                        ins = v.bn_stats(b["st"][:, t, :], src(t))
                    signal(ins)

                for k in range(NG):
                    b = mb[k % 2]
                    stats(lambda t: x_tok[:, k * TPG + t, :], b, TPG, chain.link)
                    moments(v, chain, b, TPG).then_inc(s["var_ready"], 1)
                    v.wait_ge(s["rstd_ready"], k + 1)
                    v.wait_ge(s["var_ready"], k + 1)
                    for t in range(TPG):
                        ins = v.tensor_scalar(h_tok[:, k * TPG + t, :], x_tok[:, k * TPG + t, :], b["mean"][:, t:t + 1],
                                              b["rstd"][:, t:t + 1], ALU.subtract, ALU.mult)
                    ins.then_inc(s["h_ln_ready"], 1)
                v.wait_ge(s["const_in"], 32)
                first_chain = chain.n

                with v.Fori(0, LAYERS) as l:
                    def maxima(q, k):
                        n = q * G8 + k
                        v.wait_ge(s["scores_ready"], l * GPL + n + 1 + SLOTS * G8)
                        v.wait_ge(s["exp_done"], l * GPL + n + 1)
                        v.tensor_reduce(negmax[k % 2][:], psS[k % 2][:], AX.X, ALU.max, negate=True)\
                            .then_inc(s["negmax_ready"], 1)

                    def sums(q, k):
                        n = q * G8 + k
                        t, j = k % TPS, k // TPS
                        v.wait_ge(s["exp_done"], l * GPL + n + 1 + SLOTS)
                        v.wait_ge(s["sum_done"], l * GPL + n + SLOTS - 1)
                        v.reciprocal(rowinv[k % 2][:], rowsum[k % 2][:]).then_inc(s["recip_done"], 1)
                        v.wait_ge(s["recip_done"], l * GPL + n + 1)
                        if j == 0:
                            v.wait_ge(s["mix_ready"], l * SEQS * 2 + q * 2 + 2)
                        for c in range(CH):
                            dst = odd[:, t, :] if c % 2 else acc[q % 2][:, t, :]
                            if j == 0 and c == 0:
                                ins = v.scalar_tensor_tensor(dst, prob[k % 2][:, c, :], rowinv[k % 2][:, c:c + 1],
                                                             rel[:, t, :], ALU.mult, ALU.add)
                            elif j == 0 and c == 1:
                                ins = v.tensor_scalar(dst, prob[k % 2][:, c, :], rowinv[k % 2][:, c:c + 1], None,
                                                      ALU.mult)
                            else:
                                if c >= 2:
                                    v.wait_ge(s["acc_step"], l * GPL * 3 + n * 3 + c - 1)
                                ins = v.scalar_tensor_tensor(dst, prob[k % 2][:, c, :], rowinv[k % 2][:, c:c + 1], dst,
                                                             ALU.mult, ALU.add)
                            if c < CH - 1:
                                ins.then_inc(s["acc_step"], 1)
                        ins.then_inc(s["sum_done"], 1)

                    def join(q):
                        for t in range(TPS):
                            v.wait_ge(s["sum_done"], l * GPL + (q + 1) * G8 + SLOTS - 1 + t)
                            v.wait_ge(s["acc_step"], l * GPL * 3 + (q + 1) * G8 * 3 - 3 + 3 * t)
                            v.tensor_tensor(acc[q % 2][:, t, :], acc[q % 2][:, t, :], odd[:, t, :], ALU.add)\
                                .then_inc(s["odd_ready"], 1)

                    def residual(q):
                        v.wait_ge(s["mix_ready"], l * SEQS * 2 + 2 * q + 2 + 2 * SLOTS)
                        v.reciprocal(mixinv[:], mixsum[:]).then_inc(s["mixinv_done"], 1)
                        v.wait_ge(s["mixinv_done"], l * SEQS + q + 2)
                        v.wait_ge(s["attn_ready"], l * SEQS + q + 2)
                        for t in range(TPS):
                            v.scalar_tensor_tensor(r_tok[:, q * TPS + t, :], psA[:, t * E:(t + 1) * E],
                                                   mixinv[:, t:t + 1], h_tok[:, q * TPS + t, :],
                                                   ALU.mult, ALU.add).then_inc(s["r_ready"], 1)

                    for q in range(SEQS):
                        for k in range(G8):
                            maxima(q, k)
                            if k:
                                sums(q, k - 1)
                            elif q:
                                sums(q - 1, G8 - 1)
                                join(q - 1)
                            if k == 7 and q:
                                residual(q - 1)
                    sums(SEQS - 1, G8 - 1)
                    join(SEQS - 1)
                    residual(SEQS - 1)

                    H2 = T // 2
                    chain = Chain(v, chain_sem, l * CHAIN_PER_LAYER + first_chain)
                    vb = l * 8 + NG
                    for k in range(2):
                        v.wait_ge(s["r_ready"], l * 2 * SEQS + (k + 1) * H2 + 2)
                        stats(lambda t: r_tok[:, k * H2 + t, :], mb[k], H2,
                              lambda ins: ins.then_inc(s["stats_done"], 1))
                        v.wait_ge(s["stats_done"], l * 8 + k + 1)
                        moments(v, chain, mb[k], H2).then_inc(s["var_ready"], 1)
                    for k in range(2):
                        v.wait_ge(s["rstd_ready"], vb + k + 1)
                        for t in range(H2):
                            ins = v.tensor_scalar(r_tok[:, k * H2 + t, :], r_tok[:, k * H2 + t, :],
                                                  mb[k]["mean"][:, t:t + 1], mb[k]["rstd"][:, t:t + 1],
                                                  ALU.subtract, ALU.mult)
                        ins.then_inc(s["norm1_ready"], 1)
                    for k in range(2):
                        v.wait_ge(s["n1_ready"], l * 2 + k + 1)
                        stats(lambda t: n1[:, k * H2 + t, :], mb[k], H2,
                              lambda ins: ins.then_inc(s["stats_done"], 1))
                        v.wait_ge(s["stats_done"], l * 8 + 2 + k + 1)
                        moments(v, chain, mb[k], H2).then_inc(s["var_ready"], 1)
                    for k in range(2):
                        v.wait_ge(s["rstd_ready"], vb + 2 + k + 1)
                        for t in range(H2):
                            ins = v.tensor_scalar(n1[:, k * H2 + t, :], n1[:, k * H2 + t, :],
                                                  mb[k]["mean"][:, t:t + 1], mb[k]["rstd"][:, t:t + 1],
                                                  ALU.subtract, ALU.mult)
                            if t % TPG == TPG - 1:
                                ins.then_inc(s["n2_ready"], 1)

                    def relu(k, f):
                        v.wait_ge(s["hidden_ready"], l * NG * FC + k * FC + f + 1)
                        v.wait_ge(s["mlp_ready"], l * NG + k + 1)
                        v.tensor_scalar(act[:, f, :], psF[1], cols[:, C_B1 + f:C_B1 + f + 1], 0.0, ALU.add, ALU.max)\
                            .then_inc(s["relu_odd"], 1)

                    def mlp_residual(k):
                        v.wait_ge(s["mlp_ready"], l * NG + k + 2)
                        v.wait_ge(s["ffr_turned"], l * NG + k + 1)
                        v.wait_ge(s["h2T_ready"], l * NG + k + 1 + SLOTS)
                        v.scalar_tensor_tensor(ffr[k % 2][:], psA[:], cols[:, C_B2:C_B2 + 1],
                                               h2T[:, k * GRP:(k + 1) * GRP], ALU.add, ALU.add)\
                            .then_inc(s["ffr_ready"], 1)

                    def norm3(k):
                        b = mb[k % 2]
                        v.wait_ge(s["ffr_turned"], l * NG + k + 1 + SLOTS)
                        stats(lambda t: psY[k % 2][:, t * E:(t + 1) * E], b, TPG,
                              lambda ins: ins.then_inc(s["stats_done"], 1))
                        v.wait_ge(s["stats_done"], l * 8 + 4 + k + 1)
                        moments(v, chain, b, TPG).then_inc(s["var_ready"], 1)
                        v.wait_ge(s["rstd_ready"], vb + 4 + k + 1)
                        v.wait_ge(s["n3_turned"], l * NG + k + 1 - 2 + SLOTS)
                        v.wait_ge(s["h_tok_ready"], l * NG + k + 1 - 2 + SLOTS)
                        for t in range(TPG):
                            ins = v.tensor_scalar(n3[k % 2][:, t, :], psY[k % 2][:, t * E:(t + 1) * E],
                                                  b["mean"][:, t:t + 1], b["rstd"][:, t:t + 1],
                                                  ALU.subtract, ALU.mult)
                        ins.then_inc(s["n3_ready"], 1)

                    for k in range(NG):
                        relu(k, 1)
                        relu(k, 3)
                        if k:
                            norm3(k - 1)
                        mlp_residual(k)
                    norm3(NG - 1)
                    assert chain.n == CHAIN_PER_LAYER, chain.n
                v.wait_ge(s["h_tok_ready"], LAYERS * NG + SLOTS)
                v.tensor_tensor(x_tok[:], x_tok[:], h_tok[:], ALU.add).then_inc(s["x_ready"], 1)
                v.wait_ge(s["x_ready"], 1)

            @block.tensor
            def _(p):
                p.sem_inc(s["mix_turned"], 1)
                p.sem_inc(s["scores_ready"], SLOTS * G8)
                p.sem_inc(s["attn_ready"], 1)
                p.sem_inc(s["mlp_ready"], 1)
                p.sem_inc(s["ffr_turned"], SLOTS)
                p.sem_inc(s["n3_turned"], SLOTS)
                for k in range(NG):
                    p.wait_ge(s["h_ln_ready"], k + 1)
                    if k >= 2:
                        p.wait_ge(s["hT_ready"], k - 1)
                    for t in range(TPG):
                        ins = p.transpose(psX[k % 2][:, t * P:(t + 1) * P], h_tok[:, k * TPG + t, :], ident[:])
                    ins.then_inc(s["h_turned"], 1)

                with p.Fori(0, LAYERS) as l:
                    def project(q):
                        p.wait_ge(s["qk_ready"], l * SEQS * 2 + 2 * q - 2 + 2 * SLOTS)
                        p.wait_ge(s["hT_ready"], (l + 1) * NG)
                        for k, w in enumerate((wq, wk)):
                            ins = p.matmul(psP[q % 2][:, k, :], w[:], hT[:, q * L:(q + 1) * L], start=True, stop=True)
                        ins.then_inc(s["proj_ready"], 1)

                    def scores(q, k):
                        n = q * G8 + k
                        j, t = k // TPS, k % TPS
                        p.wait_ge(s["qm_ready"], l * SEQS * HG + q * HG + j + 1 + HG)
                        p.wait_ge(s["exp_done"], l * GPL + n + 1)
                        for c in range(CH):
                            ins = p.matmul(psS[k % 2][:, c, :], qm[q % 2][:, j * CH + c, t * P:(t + 1) * P],
                                           kT[q % 2][:], start=True, stop=True)
                        ins.then_inc(s["scores_ready"], 1)

                    def turn_mix(q):
                        p.wait_ge(s["mix_ready"], l * SEQS * 2 + 2 * q + 2 + 2 * SLOTS)
                        for t in range(TPS):
                            for m in range(TPS):
                                ins = p.transpose(psT[:, m * L + t * P:m * L + (t + 1) * P],
                                                  mix[:, t, m * P:(m + 1) * P], ident[:])
                        ins.then_inc(s["mix_turned"], 1)

                    def attend(q):
                        p.wait_ge(s["mixT_ready"], l * SEQS + q + 1)
                        p.wait_ge(s["r_ready"], l * 2 * SEQS + 2 * q + 2)
                        if q == 0:
                            p.wait_ge(s["h_tok_ready"], l * NG + SLOTS)
                        for t in range(TPS):
                            for m in range(TPS):
                                ins = p.matmul(psA[:, t * E:(t + 1) * E], mixT[:, m, t * P:(t + 1) * P],
                                               h_tok[:, q * TPS + m, :], start=(m == 0), stop=(m == TPS - 1))
                        ins.then_inc(s["attn_ready"], 1)

                    p.wait_ge(s["qk_weights_in"], (l + 1) * 32)
                    project(0)
                    for q in range(SEQS):
                        p.wait_ge(s["qk_ready"], l * SEQS * 2 + (q + 1) * 2 + 2 * SLOTS)
                        for k in range(G8):
                            scores(q, k)
                            if k == 1 and q < SEQS - 1:
                                project(q + 1)
                            if k == 4 and q:
                                turn_mix(q - 1)
                            if k == 6 and q:
                                attend(q - 1)
                    turn_mix(SEQS - 1)
                    attend(SEQS - 1)

                    def turn_n2(k):
                        p.wait_ge(s["n2_ready"], l * NG + k + 1)
                        p.wait_ge(s["h2T_ready"], l * NG + k + 1)
                        for t in range(TPG):
                            ins = p.transpose(psX[k % 2][:, t * P:(t + 1) * P], n1[:, k * TPG + t, :], ident[:])
                        ins.then_inc(s["n2_turned"], 1)

                    def hidden(k):
                        p.wait_ge(s["h2T_ready"], l * NG + k + 1 + SLOTS)
                        for f in range(FC):
                            i = k * 2 + f // 2
                            p.wait_ge(s[("relu_even", "relu_odd")[f % 2]], l * NG * 2 + i + 1)
                            p.matmul(psF[f % 2], w1[:, f * P:(f + 1) * P], h2T[:, k * GRP:(k + 1) * GRP],
                                     start=True, stop=True).then_inc(s["hidden_ready"], 1)

                    def mlp_out(k):
                        p.wait_ge(s["ffr_ready"], l * NG + k + 1)
                        for f in range(FC):
                            i = k * 2 + f // 2
                            p.wait_ge(s[("relu_even", "relu_odd")[f % 2]], l * NG * 2 + i + 2)
                            ins = p.matmul(psA[:], w2[:, f, :], act[:, f, :], start=(f == 0), stop=(f == FC - 1))
                        ins.then_inc(s["mlp_ready"], 1)

                    def turn_ffr(k):
                        p.wait_ge(s["ffr_ready"], l * NG + k + 2)
                        p.wait_ge(s["n3_ready"], l * NG + k + 1 - 2 + SLOTS)
                        for t in range(TPG):
                            ins = p.transpose(psY[k % 2][:, t * P:(t + 1) * P], ffr[k % 2][:, t * P:(t + 1) * P],
                                              ident[:])
                        ins.then_inc(s["ffr_turned"], 1)

                    def turn_n3(k):
                        p.wait_ge(s["n3_ready"], l * NG + k + 1 + SLOTS)
                        p.wait_ge(s["hT_ready"], (l + 1) * NG + k)
                        for t in range(TPG):
                            ins = p.transpose(psT[:, t * P:(t + 1) * P], n3[k % 2][:, t, :], ident[:])
                        ins.then_inc(s["n3_turned"], 1)

                    p.wait_ge(s["mlp_weights_in"], (l + 1) * 64)
                    turn_n2(0)
                    turn_n2(1)
                    for k in range(NG):
                        hidden(k)
                        if k:
                            turn_ffr(k - 1)
                        mlp_out(k)
                        if k + 2 < NG:
                            turn_n2(k + 2)
                        if k >= 2:
                            turn_n3(k - 2)
                    turn_ffr(NG - 1)
                    turn_n3(NG - 2)
                    turn_n3(NG - 1)


EXPERTS, HID_B = 8, 352
FB = [(f, min(P, HID_B - f)) for f in range(0, HID_B, P)]
NFB = len(FB)


def stage_b(nc, d, x_tok, ident, minus_half):
    with ExitStack() as ctx:
        def sb(name, shape):
            return ctx.enter_context(nc.sbuf_tensor("b_" + name, shape, F32))

        def ps(name, shape):
            return ctx.enter_context(nc.psum_tensor("b_" + name, shape, F32))

        xn = sb("xn", [P, T, E])
        xg = sb("xg", [P, T, E])
        xnT = sb("xnT", [P, NTOK])
        xgT = sb("xgT", [P, NTOK])
        router = sb("router", [P, EXPERTS])
        rank = sb("rank", [P, EXPERTS])
        top = sb("top", [P, T])
        gate = sb("gate", [P, T])
        score = sb("score", [P, T, EXPERTS])
        ranked = sb("ranked", [P, T, EXPERTS])
        best = sb("best", [P, T])
        own = sb("own", [P, EXPERTS, T])
        mask = [sb(f"mask{u}", [P, T]) for u in range(2)]
        w13 = [sb(f"w13_{u}", [P, 2, HID_B]) for u in range(2)]
        w2 = [sb(f"w2_{u}", [P, NFB, E]) for u in range(2)]
        silu = [sb(f"silu{u}", [P, GRP]) for u in range(2)]
        mid = [sb(f"mid{u}", [P, NFB, GRP]) for u in range(2)]
        mb = [moment_buffers(sb, f"m{u}", T // 2) for u in range(2)]
        psH = [ps(f"h1_{u}", [P, GRP]) for u in range(2)]
        psG = [ps(f"h3_{u}", [P, GRP]) for u in range(2)]
        psO = [ps(f"o{u}", [P, GRP]) for u in range(2)]
        psX = [ps(f"x{u}", [P, GRP]) for u in range(2)]

        names = ("const_in", "weights0_in", "weights1_in", "stats_done", "chain", "var_ready", "rstd_ready", "xn_ready", "turned",
                 "xnT_ready", "xgT_ready", "scores_ready", "top_ready", "gate_ready", "xg_ready", "hidden_ready",
                 "silu_ready", "mid_ready", "out_ready", "acc_done", "mask_ready")
        s = {n: ctx.enter_context(nc.semaphore("b_" + n)) for n in names}
        H2 = T // 2
        SL = 2
        CPS = NG * NFB

        with nc.Block() as block:
            @block.sync
            def _(sp):
                sp.dma_start(router[:], d["b_router"]).then_inc(s["const_in"], 16)
                sp.dma_start(rank[:], d["b_rank"]).then_inc(s["const_in"], 16)

                def load(e, u):
                    sp.dma_start(w13[u][:], d["b_w13"][e]).then_inc(s[f"weights{u}_in"], 16)
                    sp.dma_start(w2[u][:], d["b_w2"][e]).then_inc(s[f"weights{u}_in"], 16)

                load(0, 1)
                load(1, 0)
                with sp.Fori(0, EXPERTS // 2 - 1) as i:
                    for u in range(2):
                        sp.wait_ge(s["out_ready"], (2 * i + u + 1) * NG + SL)
                        load(2 * i + u + 2, 1 - u)
                sp.wait_ge(s["out_ready"], (EXPERTS - 1) * NG + SL)
                load(EXPERTS, 1)

            @block.gpsimd
            def _(g):
                for k in range(2):
                    g.wait_ge(s["var_ready"], k + 1)
                    g.tensor_tensor(mb[k]["rstd"][:], mb[k]["var"][:], minus_half[:, 0:H2], ALU.pow)\
                        .then_inc(s["rstd_ready"], 1)

            @block.scalar
            def _(a):
                for k in range(NG):
                    a.wait_ge(s["turned"], k + 1)
                    a.activation(xnT[:, k * GRP:(k + 1) * GRP], psX[k % 2][:], ACT.Copy).then_inc(s["xnT_ready"], 1)
                a.wait_ge(s["top_ready"], 1)
                a.activation(gate[:], top[:], ACT.Sigmoid).then_inc(s["gate_ready"], 1)
                def step(n):
                    for k in range(NG):
                        for f, (_, w) in enumerate(FB):
                            i = k * NFB + f
                            a.wait_ge(s["hidden_ready"], n * CPS + i + 1)
                            a.wait_ge(s["mid_ready"], n * CPS + i + 1)
                            a.activation(silu[i % 2][0:w, :], psH[i % 2][0:w, :], ACT.Silu)\
                                .then_inc(s["silu_ready"], 1)

                step(0)
                for k in range(NG):
                    a.wait_ge(s["turned"], NG + k + 1)
                    a.activation(xgT[:, k * GRP:(k + 1) * GRP], psX[k % 2][:], ACT.Copy).then_inc(s["xgT_ready"], 1)
                with a.Fori(0, EXPERTS) as e:
                    step(e + 1)

            @block.vector
            def _(v):
                v.sem_inc(s["mid_ready"], SL)
                v.sem_inc(s["acc_done"], SL)
                chain = Chain(v, s["chain"])
                for k in range(2):
                    for t in range(H2):
                        ins = v.bn_stats(mb[k]["st"][:, t, :], x_tok[:, k * H2 + t, :])
                    chain.link(ins)
                    moments(v, chain, mb[k], H2).then_inc(s["var_ready"], 1)
                for k in range(2):
                    v.wait_ge(s["rstd_ready"], k + 1)
                    for t in range(H2):
                        ins = v.tensor_scalar(xn[:, k * H2 + t, :], x_tok[:, k * H2 + t, :], mb[k]["mean"][:, t:t + 1],
                                              mb[k]["rstd"][:, t:t + 1], ALU.subtract, ALU.mult)
                        if t % TPG == TPG - 1:
                            ins.then_inc(s["xn_ready"], 1)
                v.wait_ge(s["const_in"], 32)
                v.wait_ge(s["scores_ready"], 1)
                sc = psO[0][:, 0:T * EXPERTS].rearrange("p (t e) -> p t e", e=EXPERTS)
                chain.link(v.tensor_copy(score[:], sc))
                v.tensor_reduce(top[:], score[:], AX.X, ALU.max).then_inc(s["top_ready"], 1)
                v.wait_ge(s["top_ready"], 1)
                chain.link(v.tensor_tensor(ranked[:], score[:], top[:].unsqueeze(2).broadcast_to([P, T, EXPERTS]),
                                           ALU.is_equal))
                chain.link(v.tensor_tensor(ranked[:], ranked[:],
                                           rank[:].unsqueeze(1).broadcast_to([P, T, EXPERTS]), ALU.mult))
                chain.link(v.tensor_reduce(best[:], ranked[:], AX.X, ALU.max))
                chain.link(v.tensor_tensor(own[:].rearrange("p e t -> p t e"), ranked[:],
                                           best[:].unsqueeze(2).broadcast_to([P, T, EXPERTS]), ALU.is_equal))
                chain.link(v.memset(mask[1][:], 1.0))
                v.wait_ge(s["gate_ready"], 1)
                for t in range(T):
                    ins = v.tensor_scalar(xg[:, t, :], xn[:, t, :], gate[:, t:t + 1], None, ALU.mult)
                    if t % TPG == TPG - 1:
                        ins.then_inc(s["xg_ready"], 1)

                def product(n, k, f):
                    i = k * NFB + f
                    w = FB[f][1]
                    v.wait_ge(s["silu_ready"], n * CPS + i + 1)
                    v.wait_ge(s["out_ready"], n * NG + k - 1 + SL)
                    v.tensor_tensor(mid[k % 2][0:w, f, :], silu[i % 2][0:w, :], psG[i % 2][0:w, :], ALU.mult)\
                        .then_inc(s["mid_ready"], 1)

                def add_out(n, u, k):
                    v.wait_ge(s["out_ready"], n * NG + k + 1 + SL)
                    if not isinstance(n, int) or n:
                        v.wait_ge(s["acc_done"], n * NG + k - NG + 1 + SL)
                    for t in range(TPG):
                        x1 = x_tok[:, k * TPG + t, :]
                        ins = v.scalar_tensor_tensor(x1, psO[k % 2][:, t * E:(t + 1) * E],
                                                     mask[u][:, k * TPG + t:k * TPG + t + 1], x1, ALU.mult, ALU.add)
                    ins.then_inc(s["acc_done"], 1)

                for k in range(NG):
                    for f in range(NFB):
                        product(0, k, f)
                    if k:
                        add_out(0, 1, k - 1)
                with v.Fori(0, EXPERTS // 2) as i:
                    for u in range(2):
                        n = 2 * i + u + 1
                        for k in range(NG):
                            for f in range(NFB):
                                product(n, k, f)
                                if k == 0 and f == 0:
                                    add_out(n - 1, 1 - u, NG - 1)
                                    v.tensor_copy(mask[u][:], own[:, bass.ds(2 * i + u, 1), :]
                                                  .rearrange("p o t -> p (o t)")).then_inc(s["mask_ready"], 1)
                                    v.wait_ge(s["mask_ready"], n)
                            if k:
                                add_out(n, u, k - 1)
                add_out(EXPERTS, 1, NG - 1)
                v.wait_ge(s["acc_done"], (EXPERTS + 1) * NG + SL)

            @block.tensor
            def _(p):
                p.sem_inc(s["out_ready"], SL)

                def turn(src, k, ready, free):
                    p.wait_ge(s[ready], k + 1)
                    if free:
                        p.wait_ge(*free)
                    for t in range(TPG):
                        ins = p.transpose(psX[k % 2][:, t * P:(t + 1) * P], src[:, k * TPG + t, :], ident[:])
                    ins.then_inc(s["turned"], 1)

                for k in range(NG):
                    turn(xn, k, "xn_ready", (s["xnT_ready"], k - 1) if k >= 2 else None)
                p.wait_ge(s["const_in"], 32)
                p.wait_ge(s["xnT_ready"], NG)
                for t in range(T):
                    ins = p.matmul(psO[0][:, t * EXPERTS:(t + 1) * EXPERTS], xnT[:, t * P:(t + 1) * P], router[:],
                                   start=True, stop=True)
                ins.then_inc(s["scores_ready"], 1)

                def hidden(n, u, x, k, f):
                    i = k * NFB + f
                    f0, w = FB[f]
                    p.wait_ge(s["mid_ready"], n * CPS + i + 1)
                    p.matmul(psH[i % 2][0:w, :], w13[u][:, 0, f0:f0 + w], x[:, k * GRP:(k + 1) * GRP],
                             start=True, stop=True)
                    p.matmul(psG[i % 2][0:w, :], w13[u][:, 1, f0:f0 + w], x[:, k * GRP:(k + 1) * GRP],
                             start=True, stop=True).then_inc(s["hidden_ready"], 1)

                def output(n, u, k):
                    p.wait_ge(s["mid_ready"], n * CPS + (k + 1) * NFB + SL)
                    p.wait_ge(s["acc_done"], n * NG + k + 1)
                    for t in range(TPG):
                        for f, (_, w) in enumerate(FB):
                            ins = p.matmul(psO[k % 2][:, t * E:(t + 1) * E], mid[k % 2][0:w, f, t * P:(t + 1) * P],
                                           w2[u][0:w, f, :], start=(f == 0), stop=(f == NFB - 1))
                    ins.then_inc(s["out_ready"], 1)

                def step(n, u, x, loads):
                    p.wait_ge(s[f"weights{u}_in"], loads * 32)
                    for k in range(NG):
                        for f in range(NFB):
                            hidden(n, u, x, k, f)
                            if f == 1 and k:
                                output(n, u, k - 1)
                            if f == 1 and not k and not isinstance(n, int):
                                output(n - 1, 1 - u, NG - 1)

                step(0, 1, xnT, 1)
                for k in range(NG):
                    turn(xg, k, "xg_ready", (s["xgT_ready"], k - 1) if k >= 2 else (s["xnT_ready"], NG))
                p.wait_ge(s["xgT_ready"], NG)
                with p.Fori(0, EXPERTS // 2) as i:
                    for u in range(2):
                        step(2 * i + u + 1, u, xgT, i + 1 + u)
                output(EXPERTS, 1, NG - 1)


def layout_b(i, a):
    w1 = np.concatenate([i["L0_ffn_ws1_DF"][None], i["L0_ffn_w1_eDF"]])
    w3 = np.concatenate([i["L0_ffn_ws3_DF"][None], i["L0_ffn_w3_eDF"]])
    a["b_w13"] = np.ascontiguousarray(np.stack([w1, w3], axis=2))
    w2 = np.zeros((EXPERTS + 1, NFB * P, E), np.float32)
    w2[:, :HID_B] = np.concatenate([i["L0_ffn_ws2_FD"][None], i["L0_ffn_w2_eFD"]])
    a["b_w2"] = np.ascontiguousarray(w2.reshape(EXPERTS + 1, NFB, P, E).transpose(0, 2, 1, 3))
    a["b_router"] = np.ascontiguousarray(i["L0_ffn_router_DE"])
    a["b_rank"] = np.ascontiguousarray(np.broadcast_to(np.arange(EXPERTS, 0, -1, dtype=np.float32), (P, EXPERTS)))


STATES, TAPS, RANK = 16, 4, 8
DT = 2
INNER_C = DT * P
BC = 2 * STATES
HALF = NTOK // 2
HSEQ = SEQS // 2
BANKS = HALF // GRP


def stage_c(nc, d, x_tok, ident, minus_half):
    with ExitStack() as ctx:
        def sb(name, shape, dt=F32):
            return ctx.enter_context(nc.sbuf_tensor("c_" + name, shape, dt))

        s_tok = sb("s_tok", [P, T, E])
        n_tok = sb("n_tok", [P, T, E])
        nT = sb("nT", [P, SEQS, TAPS - 1 + L])
        w_in = sb("w_in", [P, 2, INNER_C])
        taps = sb("taps", [P, TAPS, INNER_C])
        w_tap = sb("w_tap", [P, TAPS, INNER_C])
        w_x = sb("w_x", [P, DT, BC + RANK])
        w_dt = sb("w_dt", [BC + RANK, INNER_C])
        w_out = sb("w_out", [P, DT, E])
        a_log = sb("a_log", [P, DT, STATES])
        a_neg = sb("a_neg", [P, DT, STATES])
        cols = sb("cols", [P, 9])
        eye3 = sb("eye3", [3 * BC, BC])
        sel = sb("sel", [3 * BC, BC, P], BF16)
        diag = sb("diag", [P, DT, P])
        u = sb("u", [P, DT, NTOK])
        zs = sb("zs", [P, DT, NTOK])
        dt = sb("dt", [P, DT, NTOK])
        du = sb("du", [P, DT, NTOK])
        bc_parts = sb("bc_parts", [3 * BC, NTOK], BF16)
        rest = [sb(f"rest{k}", [BC, GRP]) for k in range(2)]
        low = sb("low", [BC + RANK, NTOK])
        v_lin = sb("v_lin", [P, GRP])
        v_exp = sb("v_exp", [P, GRP])
        v_ln = sb("v_ln", [P, GRP])
        v_err = sb("v_err", [P, GRP])
        decay = [sb(f"decay{t}", [P, HSEQ, L]) for t in range(DT)]
        drive = [sb(f"drive{t}", [P, HALF]) for t in range(DT)]
        state = [sb(f"state{t}", [P, HALF]) for t in range(DT)]
        yc = [sb(f"yc{t}", [P, HALF]) for t in range(DT)]
        yz = [sb(f"yz{t}", [P, HALF]) for t in range(DT)]
        mb = [moment_buffers(sb, f"m{k}", T // 2) for k in range(2)]
        bank = [ctx.enter_context(nc.psum_tensor(f"c_bank{k}", [P, GRP], F32)) for k in range(2)]
        psB = ctx.enter_context(nc.psum_tensor("c_psB", [P, HALF], F32))
        psY = [ctx.enter_context(nc.psum_tensor(f"c_psY{t}", [P, HALF], F32)) for t in range(DT)]
        psC_lo, psC_hi = bank

        names = ("const_in", "stats_done", "chain", "var_ready", "rstd_ready", "s_ready", "n_ready", "turned",
                 "nT_ready", "prep", "tap_ready", "proj_ready", "u_ready", "z_ready", "xdbl_ready", "bc_ready",
                 "low_ready", "dtlin_ready", "v_ready", "exp_ready", "ln_ready", "dt_ready", "du_ready", "a_ready",
                 "skip_ready", "b_ready", "c_ready", "drive_ready", "decay_ready", "state_ready", "yc_ready",
                 "y_ready", "yz_ready", "out_ready", "sum_ready", "x_ready", "split", "err", "act_order",
                 "pe_order", "nT_zero", "decay_zero")
        s = {n: ctx.enter_context(nc.semaphore("c_" + n)) for n in names}
        H2 = T // 2

        with nc.Block() as block:
            @block.sync
            def _(sp):
                for dst, name in ((w_in, "c_w_in"), (taps, "c_taps"), (w_x, "c_w_x"), (w_out, "c_w_out"),
                                  (a_log, "c_a_log"), (cols, "c_cols"), (eye3, "c_eye3")):
                    sp.dma_start(dst[:], d[name]).then_inc(s["const_in"], 16)
                sp.dma_start(w_dt[BC:BC + RANK, :], d["c_w_dt"]).then_inc(s["const_in"], 16)

            @block.gpsimd
            def _(g):
                g.memset(nT[:, :, 0:TAPS - 1], 0.0).then_inc(s["nT_zero"], 1)
                for t in range(DT):
                    g.memset(decay[t][:, :, 0:1], 0.0).then_inc(s["decay_zero"], 1)
                for k in range(4):
                    b = mb[k % 2]
                    g.wait_ge(s["var_ready"], k + 1)
                    g.tensor_tensor(b["rstd"][:], b["var"][:], minus_half[:, 0:H2], ALU.pow)\
                        .then_inc(s["rstd_ready"], 1)
                g.wait_ge(s["s_ready"], 2)
                g.wait_ge(s["n_ready"], NG)
                g.tensor_tensor(x_tok[:], x_tok[:], s_tok[:], ALU.add).then_inc(s["sum_ready"], 1)

            @block.scalar
            def _(a):
                a.wait_ge(s["const_in"], 128)
                for k in range(NG):
                    a.wait_ge(s["turned"], k + 1)
                    a.activation(nT[:, 2 * k:2 * k + 2, TAPS - 1:], bank[k % 2][:].rearrange("p (q t) -> p q t", q=2),
                                 ACT.Identity, bias=cols[:, 1:2], scale=cols[:, 0:1]).then_inc(s["nT_ready"], 1)
                for k in range(NG):
                    for c in range(2 * DT):
                        i = k * 2 * DT + c
                        a.wait_ge(s["proj_ready"], i + 1)
                        dst = (u if c < DT else zs)[:, c % DT, k * GRP:(k + 1) * GRP]
                        if c < DT:
                            a.activation(dst, bank[i % 2][:], ACT.Silu, bias=cols[:, 2 + c:3 + c])\
                                .then_inc(s["u_ready"], 1)
                        else:
                            a.activation(dst, bank[i % 2][:], ACT.Silu).then_inc(s["u_ready"], 1)
                a.activation(a_neg[:], a_log[:], ACT.Exp).then_inc(s["a_ready"], 1)
                for k in range(NG):
                    for t in range(DT):
                        i = k * DT + t
                        a.wait_ge(s["dtlin_ready"], i + 1)
                        if i:
                            a.wait_ge(s["dt_ready"], i)
                        a.activation(v_lin[:], psB[:, (i % 2) * GRP:(i % 2 + 1) * GRP], ACT.Identity,
                                     bias=cols[:, 4 + t:5 + t]).then_inc(s["v_ready"], 1)
                        a.wait_ge(s["v_ready"], 3 * i + 1)
                        a.activation(v_exp[:], v_lin[:], ACT.Abs).then_inc(s["v_ready"], 1)
                        a.wait_ge(s["v_ready"], 3 * i + 2)
                        a.activation(v_exp[:], v_exp[:], ACT.Exp, scale=-1.0).then_inc(s["v_ready"], 1)
                        a.wait_ge(s["v_ready"], 3 * i + 3)
                        a.activation(v_ln[:], v_exp[:], ACT.Ln, bias=1.0).then_inc(s["ln_ready"], 1)
                a.wait_ge(s["dt_ready"], NG * DT)
                a.wait_ge(s["a_ready"], 2)
                a.wait_ge(s["decay_zero"], DT)
                for h in range(2):
                    with a.Fori(0, STATES) as i:
                        for t in range(DT):
                            a.wait_ge(s["state_ready"], (i + h * STATES) * DT + t + 1)
                            a.sem_inc(s["act_order"], 1)
                            a.activation(decay[t][:, :, 1:],
                                         dt[:, t, h * HALF:(h + 1) * HALF]
                                         .rearrange("p (q l) -> p q l", l=L)[:, :, 1:],
                                         ACT.Exp, scale=a_neg[:, t, bass.ds(i, 1)]).then_inc(s["decay_ready"], 1)

            @block.vector
            def _(v):
                v.sem_inc(s["state_ready"], DT)
                chain = Chain(v, s["chain"])

                def norm(src, dst, first, signal):
                    for k in range(2):
                        for t in range(H2):
                            ins = v.bn_stats(mb[k]["st"][:, t, :], src[:, k * H2 + t, :])
                        chain.link(ins)
                        moments(v, chain, mb[k], H2).then_inc(s["var_ready"], 1)
                    for k in range(2):
                        v.wait_ge(s["rstd_ready"], first + k + 1)
                        for t in range(H2):
                            ins = v.tensor_scalar(dst[:, k * H2 + t, :], src[:, k * H2 + t, :],
                                                  mb[k]["mean"][:, t:t + 1], mb[k]["rstd"][:, t:t + 1],
                                                  ALU.subtract, ALU.mult)
                            signal(ins, k, t)

                norm(x_tok, s_tok, 0, lambda ins, k, t: ins.then_inc(s["s_ready"], 1) if t == H2 - 1 else None)
                v.wait_ge(s["s_ready"], 2)
                norm(s_tok, n_tok, 2, lambda ins, k, t: ins.then_inc(s["n_ready"], 1) if t % TPG == TPG - 1 else None)
                v.wait_ge(s["const_in"], 128)
                for k in range(TAPS):
                    ins = v.tensor_tensor(w_tap[:, k, :], w_in[:, 0, :], taps[:, k, :], ALU.mult)
                ins.then_inc(s["tap_ready"], 1)
                v.tensor_copy(sel[:], eye3[:].unsqueeze(2).broadcast_to([3 * BC, BC, P])).then_inc(s["prep"], 1)
                for t in range(DT):
                    v.tensor_scalar(diag[:, t, :], ident[:], cols[:, 6 + t:7 + t], None, ALU.mult)\
                        .then_inc(s["prep"], 1)
                for k in range(NG):
                    v.wait_ge(s["xdbl_ready"], k + 1)
                    src = psY[0][0:BC, (k % 2) * GRP:(k % 2 + 1) * GRP]
                    cs = slice(k * GRP, (k + 1) * GRP)
                    v.tensor_copy(low[BC:BC + RANK, cs], psY[0][BC:BC + RANK, (k % 2) * GRP:(k % 2 + 1) * GRP])\
                        .then_inc(s["low_ready"], 1)
                    chain.link(v.tensor_copy(bc_parts[0:BC, cs], src))
                    chain.link(v.tensor_tensor(rest[0][:], src, bc_parts[0:BC, cs], ALU.subtract))
                    chain.link(v.tensor_copy(bc_parts[BC:2 * BC, cs], rest[0][:]))
                    chain.link(v.tensor_copy(rest[1][:], bc_parts[BC:2 * BC, cs]))
                    chain.link(v.tensor_tensor(rest[0][:], rest[0][:], rest[1][:], ALU.subtract))
                    chain.link(v.tensor_copy(bc_parts[2 * BC:3 * BC, cs], rest[0][:]))
                    v.sem_inc(s["bc_ready"], 1)
                v.wait_ge(s["a_ready"], 1)
                v.tensor_scalar(a_neg[:], a_neg[:], -1.0, None, ALU.mult).then_inc(s["a_ready"], 1)
                v.wait_ge(s["u_ready"], NG * 2 * DT)
                for k in range(NG):
                    for t in range(DT):
                        i = k * DT + t
                        cs = slice(k * GRP, (k + 1) * GRP)
                        v.wait_ge(s["v_ready"], 3 * i + 3)
                        chain.link(v.tensor_scalar(v_err[:], v_exp[:], 1.0, -1.0, ALU.add, ALU.add))
                        chain.link(v.tensor_tensor(v_err[:], v_exp[:], v_err[:], ALU.subtract))
                        v.wait_ge(s["ln_ready"], i + 1)
                        chain.link(v.tensor_tensor(v_err[:], v_err[:], v_ln[:], ALU.add))
                        v.scalar_tensor_tensor(dt[:, t, cs], v_lin[:], 0.0, v_err[:], ALU.max, ALU.add)\
                            .then_inc(s["dt_ready"], 1)
                        v.wait_ge(s["dt_ready"], i + 1)
                        v.tensor_tensor(du[:, t, cs], dt[:, t, cs], u[:, t, cs], ALU.mult)\
                            .then_inc(s["du_ready"], 1)
                v.wait_ge(s["du_ready"], NG * DT)
                for h in range(2):
                    hs = slice(h * HALF, (h + 1) * HALF)
                    with v.Fori(0, STATES) as i:
                        n = i + h * STATES
                        v.wait_ge(s["b_ready"], n + 1)
                        for t in range(DT):
                            v.wait_ge(s["state_ready"], n * DT + t + 1)
                            v.tensor_tensor(drive[t][:], du[:, t, hs], psB[:], ALU.mult)\
                                .then_inc(s["drive_ready"], 1)
                        for t in range(DT):
                            v.wait_ge(s["drive_ready"], n * DT + t + 1)
                            v.wait_ge(s["decay_ready"], n * DT + t + 1)
                            v.tensor_tensor_scan(state[t][:], decay[t][:].rearrange("p q l -> p (q l)"), drive[t][:],
                                                 0.0, ALU.mult, ALU.add).then_inc(s["state_ready"], 1)
                        v.wait_ge(s["c_ready"], n + 1)
                        for t in range(DT):
                            v.wait_ge(s["state_ready"], (n + 1) * DT + t + 1)
                            v.wait_ge(s["y_ready"], n * DT + t + 1)
                            for b in range(BANKS):
                                bs = slice(b * GRP, (b + 1) * GRP)
                                ins = v.tensor_tensor(yc[t][:, bs], state[t][:, bs], bank[b][:], ALU.mult)
                            ins.then_inc(s["yc_ready"], 1)
                    for t in range(DT):
                        v.wait_ge(s["y_ready"], (h + 1) * STATES * DT + t + 1)
                        if h:
                            v.wait_ge(s["out_ready"], 2)
                        v.tensor_tensor(yz[t][:], psY[t][:], zs[:, t, hs], ALU.mult).then_inc(s["yz_ready"], 1)
                    v.wait_ge(s["sum_ready"], 1)
                    for k in range(BANKS):
                        v.wait_ge(s["out_ready"], h * BANKS + k + 1)
                        xs = x_tok[:, (h * BANKS + k) * TPG:(h * BANKS + k + 1) * TPG, :]\
                            .rearrange("p t e -> p (t e)")
                        v.scalar_tensor_tensor(xs, psB[:, k * GRP:(k + 1) * GRP], cols[:, 8:9], xs,
                                               ALU.mult, ALU.add).then_inc(s["x_ready"], 1)
                v.wait_ge(s["x_ready"], NG)

            @block.tensor
            def _(p):
                for k in range(NG):
                    p.wait_ge(s["n_ready"], k + 1)
                    if k >= 2:
                        p.wait_ge(s["nT_ready"], k - 1)
                    for t in range(TPG):
                        ins = p.transpose(bank[k % 2][:, t * P:(t + 1) * P], n_tok[:, k * TPG + t, :], ident[:])
                    ins.then_inc(s["turned"], 1)
                p.wait_ge(s["tap_ready"], 1)
                p.wait_ge(s["nT_zero"], 1)
                p.wait_ge(s["nT_ready"], NG)
                for k in range(NG):
                    for c in range(2 * DT):
                        i = k * 2 * DT + c
                        if i >= 2:
                            p.wait_ge(s["u_ready"], i - 1)
                        cs = slice((c % DT) * P, (c % DT + 1) * P)
                        if c < DT:
                            for j in range(TAPS):
                                ins = p.matmul(bank[i % 2][:], w_tap[:, j, cs], nT[:, 2 * k:2 * k + 2, j:j + L],
                                               start=(j == 0), stop=(j == TAPS - 1))
                        else:
                            ins = p.matmul(bank[i % 2][:], w_in[:, 1, cs], nT[:, 2 * k:2 * k + 2, TAPS - 1:],
                                           start=True, stop=True)
                        ins.then_inc(s["proj_ready"], 1)
                for k in range(NG):
                    if k >= 2:
                        p.wait_ge(s["bc_ready"], k - 1)
                    p.wait_ge(s["u_ready"], (k + 1) * 2 * DT)
                    for t in range(DT):
                        ins = p.matmul(psY[0][0:BC + RANK, (k % 2) * GRP:(k % 2 + 1) * GRP], w_x[:, t, :],
                                       u[:, t, k * GRP:(k + 1) * GRP], start=(t == 0), stop=(t == DT - 1))
                    ins.then_inc(s["xdbl_ready"], 1)
                for k in range(NG):
                    for t in range(DT):
                        i = k * DT + t
                        p.wait_ge(s["low_ready"], k + 1)
                        if i >= 2:
                            p.wait_ge(s["v_ready"], 3 * (i - 2) + 1)
                        p.matmul(psB[:, (i % 2) * GRP:(i % 2 + 1) * GRP], w_dt[BC:BC + RANK, t * P:(t + 1) * P],
                                 low[BC:BC + RANK, k * GRP:(k + 1) * GRP], start=True, stop=True)\
                            .then_inc(s["dtlin_ready"], 1)
                p.wait_ge(s["prep"], 1 + DT)
                p.wait_ge(s["bc_ready"], NG)
                p.wait_ge(s["v_ready"], 3 * NG * DT)

                def spread(h, row, dst, done):
                    for b in range(BANKS):
                        cs = slice((h * BANKS + b) * GRP, (h * BANKS + b + 1) * GRP)
                        ins = p.matmul(dst[b], row, bc_parts[:, cs], start=True, stop=True)
                    ins.then_inc(done, 1)

                def add_y(t):
                    for b in range(BANKS):
                        bs = slice(b * GRP, (b + 1) * GRP)
                        ins = p.matmul(psY[t][:, bs], ident[:], yc[t][:, bs], start=False, stop=True,
                                       skip_group_check=True)
                    ins.then_inc(s["y_ready"], 1)

                b_dst = [psB[:, b * GRP:(b + 1) * GRP] for b in range(BANKS)]
                c_dst = [bank[b][:] for b in range(BANKS)]
                for h in range(2):
                    if h:
                        p.wait_ge(s["x_ready"], BANKS)
                    spread(h, sel[:, 0, :], b_dst, s["b_ready"])
                    spread(h, sel[:, STATES, :], c_dst, s["c_ready"])
                    for t in range(DT):
                        if h:
                            p.wait_ge(s["yz_ready"], t + 1)
                        for b in range(BANKS):
                            bs = slice(b * GRP, (b + 1) * GRP)
                            ins = p.matmul(psY[t][:, bs], diag[:, t, :],
                                           u[:, t, h * HALF + b * GRP:h * HALF + (b + 1) * GRP],
                                           start=True, stop=True)
                        if not h:
                            ins.then_inc(s["y_ready"], 1)
                    with p.Fori(0, STATES - 1) as i:
                        n = i + h * STATES
                        p.wait_ge(s["drive_ready"], (n + 1) * DT)
                        p.sem_inc(s["pe_order"], 1)
                        spread(h, sel[:, bass.ds(i + 1, 1), :].rearrange("k r m -> k (r m)"), b_dst, s["b_ready"])
                        p.wait_ge(s["yc_ready"], n * DT + 1)
                        add_y(0)
                        p.wait_ge(s["yc_ready"], (n + 1) * DT)
                        p.sem_inc(s["pe_order"], 1)
                        spread(h, sel[:, bass.ds(i + 1 + STATES, 1), :].rearrange("k r m -> k (r m)"), c_dst,
                               s["c_ready"])
                        add_y(1)
                    for t in range(DT):
                        p.wait_ge(s["yc_ready"], ((h + 1) * STATES - 1) * DT + t + 1)
                        add_y(t)
                    p.wait_ge(s["yz_ready"], (h + 1) * DT)
                    for k in range(BANKS):
                        for t in range(TPG):
                            for c in range(DT):
                                q = k * TPG + t
                                ins = p.matmul(psB[:, q * P:(q + 1) * P], yz[c][:, q * P:(q + 1) * P], w_out[:, c, :],
                                               start=(c == 0), stop=(c == DT - 1))
                        ins.then_inc(s["out_ready"], 1)


def layout_c(i, a):
    w = i["L1_attn_in_proj_w"]
    a["c_w_in"] = np.ascontiguousarray(w.T.reshape(E, 2, INNER_C))
    a["c_taps"] = np.ascontiguousarray(np.broadcast_to(i["L1_attn_conv_w"].T, (P, TAPS, INNER_C)))
    xp = i["L1_attn_x_proj_w"]
    xp = np.concatenate([xp[RANK:], xp[:RANK]])
    a["c_w_x"] = np.ascontiguousarray(xp.T.reshape(DT, P, BC + RANK).transpose(1, 0, 2))
    a["c_w_dt"] = np.ascontiguousarray(i["L1_attn_dt_proj_w"].T)
    a["c_w_out"] = np.ascontiguousarray(i["L1_attn_out_proj_w"].T.reshape(DT, P, E).transpose(1, 0, 2))
    a["c_a_log"] = np.ascontiguousarray(i["L1_attn_A_log"].reshape(DT, P, STATES).transpose(1, 0, 2))
    col = [i["L1_attn_ln_g"][:, None], i["L1_attn_ln_b"][:, None]]
    col += [i["L1_attn_" + n].reshape(DT, P).T for n in ("conv_b", "dt_proj_b", "D")]
    col += [np.broadcast_to(i["L1_attn_res_scale"], (P, 1))]
    a["c_cols"] = np.ascontiguousarray(np.concatenate(col, axis=1))
    a["c_eye3"] = np.ascontiguousarray(np.tile(np.eye(BC, dtype=np.float32), (3, 1)))


DEPTH, HEADS_D, DHD, WINDOW = 2, 8, 64, 64
INNER_D = HEADS_D * DHD
HID_D = E * 4 * 2 // 3
CD = INNER_D // P
FD = [(f, min(P, HID_D - f)) for f in range(0, HID_D, P)]
NFD = len(FD)
QK_SCALE = 8.0
NORM_MIN = 1e-12
MASKED = -1e25
D_LG, D_LB, D_BA, D_BG, D_NCOL = 0, 1, 2, 2 + NFD, 2 + 2 * NFD


def schedule_d():
    slots = {}

    def place(slot, *items):
        slots.setdefault(slot, []).extend(items)

    for q in range(SEQS):
        at = 8 * q
        for g in range(8):
            place(at + g, ("score", q, g))
            place(at + g + 1, ("exp", q, g))
            place(at + g + 2, ("turn_p", q, g))
            place(at + g + 3, ("pv", q, g))
    for q in range(SEQS):
        at = 8 * q
        for t in range(TPS):
            last = at + 4 * t + 3
            place(last + 3, ("norm_o", q, t))
            place(last + 4, ("turn_o", q, t))
            place(last + 5, ("out_o", q, t))
        place(at + 13, ("shift", q))
        place(at + 14, ("rstd_f", q))
        place(at + 15, ("norm_f", q))
        place(at + 16, ("turn_f", q))
        place(at + 17, *[("hidden", q, f) for f in range(NFD)])
        place(at + 18, ("out_f", q))
    for q in range(SEQS):
        at = 8 * (q - 1)
        place(at, ("turn_h", q))
        for t in range(TPS):
            for part in range(3):
                place(at + 1 + 3 * t + part, ("project", q, t, part))
            for part in range(2):
                place(at + 3 + 3 * t + 2 * part, ("turn_qk", q, t, part))
    rank = ("score", "exp", "turn_p", "pv")
    order = []
    for n in sorted(slots):
        order += sorted(slots[n], key=lambda i: rank.index(i[0]) if i[0] in rank else len(rank))
    return order


def stage_d(nc, d, x_tok, ident, minus_half):
    with ExitStack() as ctx:
        def sb(name, shape, dt=F32):
            return ctx.enter_context(nc.sbuf_tensor("d_" + name, shape, dt))

        y_tok = sb("y_tok", [P, T, E])
        wqkv = sb("wqkv", [P, 3, INNER_D])
        wo = sb("wo", [P, CD, E])
        w1 = sb("w1", [P, 2, HID_D])
        w2 = sb("w2", [P, NFD, E])
        cols = sb("cols", [P, D_NCOL])
        b2row = sb("b2row", [1, E])
        ones_row = sb("ones_row", [1, P])
        gains = sb("gains", [P, 4, DHD])
        tables = sb("tables", [P, 4, TPS, DHD])
        rot = sb("rot", [P, 4, TPS, DHD])
        maskf = sb("maskf", [P, L + P])
        mask = sb("mask", [P, L + P], BF16)
        identb = sb("identb", [P, P], BF16)
        down = sb("down", [P, 2, P])
        hT = [sb(f"hT{u}", [P, L + 1]) for u in range(2)]
        sq = [sb(f"sq{u}", [P, INNER_D]) for u in range(2)]
        direct = [sb(f"direct{u}", [P, INNER_D]) for u in range(2)]
        cross = [sb(f"cross{u}", [P, INNER_D]) for u in range(2)]
        qk = [sb(f"qk{u}", [P, INNER_D]) for u in range(2)]
        ss = [sb(f"ss{u}", [P, 2, HEADS_D]) for u in range(2)]
        inv = [[sb(f"inv{u}{t}", [P, 2, HEADS_D]) for t in range(TPS)] for u in range(2)]
        val = [sb(f"val{u}", [P, TPS, INNER_D]) for u in range(2)]
        qkT = [sb(f"qkT{u}", [P, 2, CD, L]) for u in range(2)]
        negmax = [sb(f"negmax{u}", [P, 2]) for u in range(2)]
        bias = [sb(f"bias{u}", [P, 2]) for u in range(2)]
        prob = [[sb(f"prob{t}{u}", [P, 2, (t + 1) * P]) for u in range(2)] for t in range(TPS)]
        probT = [sb(f"probT{u}", [P, 2, 2, P]) for u in range(2)]
        rowsum = [sb(f"rowsum{t}", [P, HEADS_D]) for t in range(TPS)]
        rowinv = [sb(f"rowinv{t}", [P, HEADS_D]) for t in range(TPS)]
        o_n = sb("o_n", [P, INNER_D])
        oT = sb("oT", [P, CD, P])
        hs = sb("hs", [P, TPS, E])
        hn = sb("hn", [P, TPS, E])
        fT = sb("fT", [P, L])
        gel = [sb(f"gel{u}", [P, L]) for u in range(2)]
        mid = sb("mid", [P, NFD, L])
        mb = [moment_buffers(sb, f"m{k}", T // 2) for k in range(2)]
        psQ = [ctx.enter_context(nc.psum_tensor(f"d_psQ{k}", [P, GRP], F32)) for k in range(2)]
        psS = [ctx.enter_context(nc.psum_tensor(f"d_psS{k}", [P, 2, L], F32)) for k in range(2)]
        psT = [ctx.enter_context(nc.psum_tensor(f"d_psT{k}", [P, GRP], F32)) for k in range(2)]
        psO = ctx.enter_context(nc.psum_tensor("d_psO", [P, GRP], F32))
        psW = ctx.enter_context(nc.psum_tensor("d_psW", [P, GRP], F32))

        names = ("const_in", "weights_in", "row_in", "chain", "var_ready", "rstd_ready", "y_ready", "set_up",
                 "rot_ready", "q_full", "q_free", "s_full", "s_free", "t_full", "t_free", "w_full", "w_free",
                 "o_full", "o_free", "square_ready", "rope_ready", "ss_ready", "inv_ready", "qk_ready", "pool_step",
                 "max_step", "bias_ready", "prob_ready", "rowinv_ready", "stats_done", "hs_ready", "hn_ready",
                 "gelu_ready", "mid_ready", "x_ready", "shift_half", "reduce_done")
        s = {n: ctx.enter_context(nc.semaphore("d_" + n)) for n in names}
        H2 = T // 2
        items = schedule_d()

        def order(*kinds):
            found = [i for i in items if i[0] in kinds]
            return {i: n for n, i in enumerate(found)}, len(found)

        Q, NQ = order("project", "hidden")
        S, NS = order("score")
        TT = [("turn_h",), ("turn_qk",), ("turn_p",), ("turn_o",), ("turn_f",)]
        TI, NT = order(*[k for (k,) in TT])
        W, NW = order("out_o", "shift", "out_f")
        O, NO = order("norm_o")
        PR, NPR = {}, 0
        for i in items:
            if i[0] == "project" and i[3] < 2:
                PR[i] = NPR
                NPR += 1
        F, NF = order("hidden")
        SH, NSH = order("shift")
        SL = 2

        def keys(t):
            return (0, P) if t == 0 else (WINDOW, L)

        def heads(g):
            t, r = divmod(g, 4)
            cp, a = divmod(r, 2)
            return t, a, [(2 * cp + j, 2 * (2 * cp + j) + a) for j in range(2)]

        mh16 = minus_half[:, 0:2 * HEADS_D].rearrange("p (k h) -> p k h", k=2)

        def turned(n, l):
            ks = sorted(PR, key=PR.get)
            if n >= 2:
                _, q, t, part = ks[n - 2]
                return l * NT + TI[("turn_qk", q, t, part)] + 1 + SL
            return l * NT + SL

        def prev(q, g):
            t, r = divmod(g, 4)
            if r >= 2:
                return q, g - 2
            return (q - 1, 4 * t + r + 2) if q else None

        CHAIN_D = SEQS * 8

        def last_turn_o(it):
            n = O[it]
            before = [i for i in O if O[i] == n - 1]
            return TI[("turn_o",) + before[0][1:]] + 1 if before else 0

        with nc.Block() as block:
            @block.sync
            def _(sp):
                for dst, name in ((tables, "d_tables"), (maskf, "d_mask"), (down, "d_down")):
                    sp.dma_start(dst[:], d[name]).then_inc(s["const_in"], 16)

                def load(l):
                    for dst, name in ((wqkv, "d_wqkv"), (wo, "d_wo"), (w1, "d_w1"), (w2, "d_w2"), (cols, "d_cols"),
                                      (gains, "d_gains"), (b2row, "d_b2")):
                        sp.dma_start(dst[:], d[name][l]).then_inc(s["weights_in"], 16)

                load(0)
                for l in range(1, DEPTH):
                    sp.wait_ge(s["w_free"], l * NW + 1)
                    load(l)

            @block.gpsimd
            def _(g):
                g.sem_inc(s["qk_ready"], SL)
                g.memset(ones_row[:], 1.0).then_inc(s["set_up"], 1)
                for u in range(2):
                    g.wait_ge(s["set_up"], 2 * u + 1)
                    g.memset(hT[u][P // 2:P, 0:1], 0.0).then_inc(s["set_up"], 1)
                    g.wait_ge(s["set_up"], 2 * u + 2)
                    g.memset(prob[1][u][:, :, 0:WINDOW], 0.0).then_inc(s["set_up"], 1)
                for k in range(2):
                    g.wait_ge(s["var_ready"], k + 1)
                    g.tensor_tensor(mb[k]["rstd"][:], mb[k]["var"][:], minus_half[:, 0:H2], ALU.pow)\
                        .then_inc(s["rstd_ready"], 1)
                g.wait_ge(s["set_up"], 5)
                g.wait_ge(s["const_in"], 48)
                with g.Fori(0, DEPTH) as l:
                    g.wait_ge(s["weights_in"], (l + 1) * 7 * 16)
                    for k in range(4):
                        g.tensor_tensor(rot[:, k], tables[:, k], gains[:, k:k + 1, :].broadcast_to([P, TPS, DHD]),
                                        ALU.mult).then_inc(s["rot_ready"], 1)
                    steps = [0]

                    def step(ins):
                        steps[0] += 1
                        ins.then_inc(s["pool_step"], 1)
                        return l * STEPS + steps[0]

                    STEPS = NPR
                    for it in items:
                        if it[0] == "project" and it[3] < 2:
                            _, q, t, part = it
                            n = PR[it]
                            b = n % 2
                            g.wait_ge(s["rope_ready"], l * NPR + n + 1)
                            if part == 0:
                                g.wait_ge(s["t_full"], turned(n, l))
                                g.tensor_tensor(qk[b][:], direct[b][:], cross[b][:], ALU.add)\
                                    .then_inc(s["qk_ready"], 1)
                            else:
                                at = step(g.tensor_tensor(direct[b][:], direct[b][:], cross[b][:], ALU.add))
                                g.wait_ge(s["ss_ready"], l * (NPR // 2) + n // 2 + 1)
                                at = step(g.tensor_tensor(inv[q % 2][t][:], ss[t][:], mh16, ALU.pow))
                                g.wait_ge(s["pool_step"], at)
                                g.sem_inc(s["inv_ready"], 1)
                                g.wait_ge(s["t_full"], turned(n, l))
                                g.tensor_tensor(qk[b][:].rearrange("p (h e) -> p h e", e=DHD),
                                                direct[b][:].rearrange("p (h e) -> p h e", e=DHD),
                                                inv[q % 2][t][:, 1, :].unsqueeze(2)
                                                .broadcast_to([P, HEADS_D, DHD]), ALU.mult)\
                                    .then_inc(s["qk_ready"], 1)
                        elif it[0] == "rstd_f":
                            n = it[1]
                            g.wait_ge(s["var_ready"], l * SEQS + n + 1 + 2)
                            g.tensor_tensor(mb[0]["rstd"][:, 0:TPS], mb[0]["var"][:, 0:TPS], minus_half[:, 0:TPS],
                                            ALU.pow).then_inc(s["rstd_ready"], 1)

            @block.scalar
            def _(a):
                a.sem_inc(s["t_free"], SL)
                a.sem_inc(s["s_free"], SL)
                a.sem_inc(s["prob_ready"], 1)
                with a.Fori(0, DEPTH) as l:
                    a.wait_ge(s["set_up"], 5)
                    a.wait_ge(s["weights_in"], (l + 1) * 7 * 16)

                    def full(it):
                        n = TI[it]
                        a.wait_ge(s["t_full"], l * NT + n + 1 + SL)
                        return psT[n % 2]

                    def square(it):
                        n, i = PR[it], Q[it]
                        a.wait_ge(s["q_full"], l * NQ + i + 1)
                        a.wait_ge(s["reduce_done"], l * NPR + n - 1 + SL)
                        a.activation(sq[n % 2][:], psQ[i % 2][:], ACT.Square).then_inc(s["square_ready"], 1)

                    def exps(it):
                        _, q, g = it
                        n = S[("score", q, g)]
                        t, _, hh = heads(g)
                        k0, k1 = keys(t)
                        a.wait_ge(s["bias_ready"], l * NS + n + 1)
                        a.wait_ge(s["rowinv_ready"], l * NO + 2 * q + t + 1)
                        a.wait_ge(s["t_full"], l * NT + (TI[("turn_p",) + prev(q, g)] + 1 if prev(q, g) else 0) + SL)
                        for j, (_, h) in enumerate(hh):
                            ins = a.activation(prob[t][g % 2][:, j, k0:k1], psS[n % 2][:, j, k0:k1], ACT.Exp,
                                               bias=bias[n % 2][:, j:j + 1], scale=inv[q % 2][t][:, 0, h:h + 1],
                                               accum_out=rowsum[t][:, h:h + 1])
                        ins.then_inc(s["s_free"], 1)

                    for it in items:
                        kind, q = it[0], it[1]
                        if kind == "turn_h":
                            ps = full(it)
                            a.activation(hT[q % 2][0:P // 2, 0:L], ps[0:P // 2, 0:L], ACT.Copy)\
                                .then_inc(s["shift_half"], 1)
                            a.activation(hT[q % 2][P // 2:P, 1:L + 1], ps[P // 2:P, 0:L], ACT.Copy)\
                                .then_inc(s["t_free"], 1)
                        elif kind == "project" and it[3] < 2:
                            square(it)
                        elif kind == "turn_qk":
                            _, q, t, part = it
                            ps = full(it)
                            a.activation(qkT[q % 2][:, part, :, t * P:(t + 1) * P],
                                         ps[:].rearrange("p (c n) -> p c n", c=CD), ACT.Copy)\
                                .then_inc(s["t_free"], 1)
                        elif kind == "exp":
                            exps(it)
                        elif kind == "turn_p":
                            t = heads(it[2])[0]
                            ps = full(it)
                            a.activation(probT[it[2] % 2][:, :, 0:t + 1, :],
                                         ps[:].rearrange("p (j b n) -> p j b n", j=2, b=2)[:, :, 0:t + 1, :],
                                         ACT.Copy).then_inc(s["t_free"], 1)
                        elif kind == "turn_o":
                            ps = full(it)
                            a.activation(oT[:].rearrange("p c n -> p (c n)"), ps[:], ACT.Copy)\
                                .then_inc(s["t_free"], 1)
                        elif kind == "turn_f":
                            ps = full(it)
                            a.activation(fT[:], ps[:, 0:L], ACT.Identity, bias=cols[:, D_LB:D_LB + 1],
                                         scale=cols[:, D_LG:D_LG + 1]).then_inc(s["t_free"], 1)
                        elif kind == "hidden":
                            f = it[2]
                            w = FD[f][1]
                            a.wait_ge(s["q_full"], l * NQ + Q[it] + 1)
                            a.wait_ge(s["mid_ready"], l * NF + F[it] + 1)
                            a.activation(gel[F[it] % 2][0:w, :], psQ[Q[it] % 2][0:w, L:2 * L], ACT.Gelu,
                                         bias=cols[0:w, D_BG + f:D_BG + f + 1]).then_inc(s["gelu_ready"], 1)

            @block.vector
            def _(v):
                v.sem_inc(s["q_free"], SL)
                v.sem_inc(s["w_free"], 1)
                v.sem_inc(s["o_free"], 1)
                v.sem_inc(s["reduce_done"], SL)
                v.sem_inc(s["rowinv_ready"], SL)
                v.sem_inc(s["mid_ready"], SL)
                chain = Chain(v, s["chain"])
                for k in range(2):
                    for t in range(H2):
                        ins = v.bn_stats(mb[k]["st"][:, t, :], x_tok[:, k * H2 + t, :])
                    chain.link(ins)
                    moments(v, chain, mb[k], H2).then_inc(s["var_ready"], 1)
                for k in range(2):
                    v.wait_ge(s["rstd_ready"], k + 1)
                    for t in range(H2):
                        ins = v.tensor_scalar(y_tok[:, k * H2 + t, :], x_tok[:, k * H2 + t, :],
                                              mb[k]["mean"][:, t:t + 1], mb[k]["rstd"][:, t:t + 1],
                                              ALU.subtract, ALU.mult)
                chain.link(ins)
                v.sem_inc(s["y_ready"], 1)
                v.wait_ge(s["const_in"], 48)
                chain.link(v.tensor_copy(mask[:], maskf[:]))
                chain.link(v.tensor_copy(identb[:], ident[:]))
                v.sem_inc(s["y_ready"], 1)
                first_chain = chain.n
                with v.Fori(0, DEPTH) as l:
                    chain = Chain(v, s["chain"], l * CHAIN_D + first_chain)
                    v.wait_ge(s["rot_ready"], (l + 1) * 4)

                    def heads3(ap):
                        return ap.rearrange("p (h e) -> p h e", e=DHD)

                    for it in items:
                        kind, q = it[0], it[1]
                        if kind == "project":
                            _, q, t, part = it
                            i = Q[it]
                            ps = psQ[i % 2]
                            v.wait_ge(s["q_full"], l * NQ + i + 1)
                            if part == 2:
                                v.tensor_copy(val[q % 2][:, t, :], ps[:]).then_inc(s["q_free"], 1)
                                continue
                            n = PR[it]
                            b = n % 2
                            v.wait_ge(s["square_ready"], l * NPR + n + 1)
                            v.wait_ge(s["qk_ready"], l * NPR + n - 1 + SL)
                            bc = [P, HEADS_D, DHD]
                            v.tensor_tensor(heads3(direct[b][:]), heads3(ps[:]),
                                            rot[:, 2 * part, t:t + 1, :].broadcast_to(bc), ALU.mult)
                            hf = DHD // 2
                            for x0, x1 in ((0, hf), (hf, 0)):
                                ins = v.tensor_tensor(heads3(cross[b][:])[:, :, x0:x0 + hf],
                                                      heads3(ps[:])[:, :, x1:x1 + hf],
                                                      rot[:, 2 * part + 1, t:t + 1, x0:x0 + hf]
                                                      .broadcast_to([P, HEADS_D, hf]), ALU.mult)
                            ins.then_inc(s["rope_ready"], 1)
                            v.tensor_reduce(ss[t][:, part, :], heads3(sq[b][:]), AX.X, ALU.add)\
                                .then_inc(s["reduce_done"], 1)
                            v.wait_ge(s["reduce_done"], l * NPR + n + 1 + SL)
                            v.sem_inc(s["q_free"], 1)
                            if part == 1:
                                v.tensor_scalar(ss[t][:], ss[t][:], NORM_MIN ** 2, None, ALU.max)\
                                    .then_inc(s["ss_ready"], 1)
                                v.wait_ge(s["ss_ready"], l * (NPR // 2) + n // 2 + 1)
                        elif kind == "score":
                            g = it[2]
                            n = S[it]
                            t, _, hh = heads(g)
                            k0, k1 = keys(t)
                            v.wait_ge(s["s_full"], l * NS + n + 1)
                            v.wait_ge(s["s_free"], l * NS + n + 1)
                            v.tensor_reduce(negmax[n % 2][:], psS[n % 2][:, :, k0:k1], AX.X, ALU.max, negate=True)\
                                .then_inc(s["max_step"], 1)
                            v.wait_ge(s["max_step"], l * NS + n + 1)
                            v.wait_ge(s["inv_ready"], l * SEQS * 2 + 2 * q + t + 1)
                            h0, h1 = hh[0][1], hh[1][1]
                            v.tensor_tensor(bias[n % 2][:], negmax[n % 2][:],
                                            inv[q % 2][t][:, 0, h0:h1 + 1:h1 - h0], ALU.mult)\
                                .then_inc(s["bias_ready"], 1)
                        elif kind == "norm_o":
                            _, q, t = it
                            n = O[it]
                            v.wait_ge(s["s_free"], l * NS + S[("score", q, 4 * t + 3)] + 1 + SL)
                            v.reciprocal(rowinv[t][:], rowsum[t][:]).then_inc(s["rowinv_ready"], 1)
                            v.wait_ge(s["rowinv_ready"], l * NO + n + 1 + SL)
                            v.wait_ge(s["o_full"], l * NO + n + 1)
                            v.wait_ge(s["t_full"], l * NT + SL + last_turn_o(it))
                            v.tensor_tensor(heads3(o_n[:]), heads3(psO[:]),
                                            rowinv[t][:].unsqueeze(2).broadcast_to([P, HEADS_D, DHD]), ALU.mult)\
                                .then_inc(s["o_free"], 1)
                        elif kind == "out_o":
                            _, q, t = it
                            v.wait_ge(s["w_full"], l * NW + W[it] + 1)
                            yt = y_tok[:, q * TPS + t, :]
                            v.tensor_tensor(yt, yt, psW[:, 0:E], ALU.add).then_inc(s["w_free"], 1)
                        elif kind == "shift":
                            v.wait_ge(s["w_full"], l * NW + W[it] + 1)
                            chain.link(v.tensor_copy(hs[:, :, E // 2:], psW[:, 0:E].rearrange("p (t e) -> p t e", t=TPS)))
                            v.sem_inc(s["w_free"], 1)
                            v.wait_ge(s["w_free"], l * NW + W[("out_o", q, 1)] + 2)
                            chain.link(v.tensor_copy(hs[:, :, 0:E // 2], y_tok[:, q * TPS:(q + 1) * TPS, 0:E // 2]))
                            b = mb[0]
                            for t in range(TPS):
                                ins = v.bn_stats(b["st"][:, t, :], hs[:, t, :])
                            chain.link(ins)
                            moments(v, chain, b, TPS).then_inc(s["var_ready"], 1)
                        elif kind == "norm_f":
                            v.wait_ge(s["rstd_ready"], l * SEQS + q + 1 + 2)
                            for t in range(TPS):
                                ins = v.tensor_scalar(hn[:, t, :], hs[:, t, :], mb[0]["mean"][:, t:t + 1],
                                                      mb[0]["rstd"][:, t:t + 1], ALU.subtract, ALU.mult)
                            ins.then_inc(s["hn_ready"], 1)
                            v.wait_ge(s["hn_ready"], l * SEQS + q + 1)
                        elif kind == "hidden":
                            f = it[2]
                            w = FD[f][1]
                            n, i = F[it], Q[it]
                            v.wait_ge(s["gelu_ready"], l * NF + n + 1)
                            v.scalar_tensor_tensor(mid[0:w, f, :], psQ[i % 2][0:w, 0:L], cols[0:w, D_BA + f:D_BA + f + 1],
                                                   gel[n % 2][0:w, :], ALU.add, ALU.mult).then_inc(s["mid_ready"], 1)
                            v.wait_ge(s["mid_ready"], l * NF + n + 1 + SL)
                            v.sem_inc(s["q_free"], 1)
                        elif kind == "out_f":
                            v.wait_ge(s["w_full"], l * NW + W[it] + 1)
                            yt = y_tok[:, q * TPS:(q + 1) * TPS, :].rearrange("p t e -> p (t e)")
                            v.tensor_tensor(yt, yt, psW[:, 0:2 * E], ALU.add).then_inc(s["w_free"], 1)
                    assert chain.n == CHAIN_D, chain.n
                v.wait_ge(s["w_free"], DEPTH * NW + 1)
                v.tensor_tensor(x_tok[:], x_tok[:], y_tok[:], ALU.add).then_inc(s["x_ready"], 1)
                v.wait_ge(s["x_ready"], 1)

            @block.tensor
            def _(p):
                p.sem_inc(s["t_full"], SL)
                p.wait_ge(s["y_ready"], 2)
                p.wait_ge(s["const_in"], 48)
                p.wait_ge(s["set_up"], 5)
                with p.Fori(0, DEPTH) as l:
                    p.wait_ge(s["weights_in"], (l + 1) * 7 * 16)
                    p.wait_ge(s["w_free"], l * NW + 1)

                    def bank(it):
                        n = TI[it]
                        p.wait_ge(s["t_free"], l * NT + n + 1)
                        return psT[n % 2]

                    def turned_in(it):
                        p.wait_ge(s["t_free"], l * NT + TI[it] + 1 + SL)

                    for it in items:
                        kind, q = it[0], it[1]
                        if kind == "turn_h":
                            ps = bank(it)
                            for t in range(TPS):
                                ins = p.transpose(ps[:, t * P:(t + 1) * P], y_tok[:, q * TPS + t, :], ident[:])
                            ins.then_inc(s["t_full"], 1)
                        elif kind == "project":
                            _, q, t, part = it
                            i = Q[it]
                            turned_in(("turn_h", q))
                            p.wait_ge(s["q_free"], l * NQ + i + 1)
                            p.matmul(psQ[i % 2][:], hT[q % 2][:, t * P:(t + 1) * P], wqkv[:, part, :],
                                     start=True, stop=True).then_inc(s["q_full"], 1)
                        elif kind == "turn_qk":
                            _, q, t, part = it
                            n = PR[("project", q, t, part)]
                            p.wait_ge(s["qk_ready"], l * NPR + n + 1 + SL)
                            ps = bank(it)
                            for c in range(CD):
                                ins = p.transpose(ps[:, c * P:(c + 1) * P], qk[n % 2][:, c * P:(c + 1) * P], ident[:])
                            ins.then_inc(s["t_full"], 1)
                        elif kind == "score":
                            g = it[2]
                            n = S[it]
                            t, a, hh = heads(g)
                            k0, k1 = keys(t)
                            turned_in(("turn_qk", q, t, 1))
                            p.wait_ge(s["s_free"], l * NS + n + 1)
                            out = psS[n % 2][:, :, k0:k1]
                            m0 = P * t
                            p.matmul(out, identb[:], mask[:, m0 + k0:m0 + k1].unsqueeze(1)
                                     .broadcast_to([P, 2, k1 - k0]), start=True, stop=True)
                            for j, (c, _) in enumerate(hh):
                                rows = slice(a * DHD, (a + 1) * DHD)
                                ins = p.matmul(psS[n % 2][:, j, k0:k1], qkT[q % 2][rows, 0, c, t * P:(t + 1) * P],
                                               qkT[q % 2][rows, 1, c, k0:k1], start=False, stop=True,
                                               skip_group_check=True)
                            ins.then_inc(s["s_full"], 1)
                        elif kind == "turn_p":
                            g = it[2]
                            t = heads(g)[0]
                            p.wait_ge(s["s_free"], l * NS + S[("score", q, g)] + 1 + SL)
                            ps = bank(it)
                            for j in range(2):
                                for b in range(t + 1):
                                    ins = p.transpose(ps[:, (2 * j + b) * P:(2 * j + b + 1) * P],
                                                      prob[t][g % 2][:, j, b * P:(b + 1) * P], ident[:])
                            ins.then_inc(s["t_full"], 1)
                        elif kind == "pv":
                            g = it[2]
                            t, a, hh = heads(g)
                            turned_in(("turn_p", q, g))
                            if g % 4 == 0:
                                p.wait_ge(s["o_free"], l * NO + O[("norm_o", q, t)] + 1)
                            for j, (_, h) in enumerate(hh):
                                for b in range(t + 1):
                                    ins = p.matmul(psO[:, h * DHD:(h + 1) * DHD], probT[g % 2][:, j, b, :],
                                                   val[q % 2][:, b, h * DHD:(h + 1) * DHD], start=(b == 0),
                                                   stop=(b == t))
                            if g % 4 == 3:
                                ins.then_inc(s["o_full"], 1)
                        elif kind == "turn_o":
                            _, q, t = it
                            p.wait_ge(s["o_free"], l * NO + O[("norm_o", q, t)] + 2)
                            ps = bank(it)
                            for c in range(CD):
                                ins = p.transpose(ps[:, c * P:(c + 1) * P], o_n[:, c * P:(c + 1) * P], ident[:])
                            ins.then_inc(s["t_full"], 1)
                        elif kind == "out_o":
                            _, q, t = it
                            turned_in(("turn_o", q, t))
                            p.wait_ge(s["w_free"], l * NW + W[it] + 1)
                            for c in range(CD):
                                ins = p.matmul(psW[:, 0:E], oT[:, c, :], wo[:, c, :], start=(c == 0),
                                               stop=(c == CD - 1))
                            ins.then_inc(s["w_full"], 1)
                        elif kind == "shift":
                            p.wait_ge(s["w_free"], l * NW + W[it] + 1)
                            p.matmul(psW[:, 0:E], down[:, 0, :], y_tok[:, q * TPS:(q + 1) * TPS, E // 2:],
                                     start=True, stop=True)
                            p.matmul(psW[:, E // 2:E], down[:, 1, :], y_tok[:, q * TPS, E // 2:],
                                     start=False, stop=True, skip_group_check=True).then_inc(s["w_full"], 1)
                        elif kind == "turn_f":
                            p.wait_ge(s["hn_ready"], l * SEQS + q + 1)
                            ps = bank(it)
                            for t in range(TPS):
                                ins = p.transpose(ps[:, t * P:(t + 1) * P], hn[:, t, :], ident[:])
                            ins.then_inc(s["t_full"], 1)
                        elif kind == "hidden":
                            f = it[2]
                            f0, w = FD[f]
                            i = Q[it]
                            turned_in(("turn_f", q))
                            p.wait_ge(s["q_free"], l * NQ + i + 1)
                            for k in range(2):
                                ins = p.matmul(psQ[i % 2][0:w, k * L:(k + 1) * L], w1[:, k, f0:f0 + w], fT[:],
                                               start=True, stop=True)
                            ins.then_inc(s["q_full"], 1)
                        elif kind == "out_f":
                            p.wait_ge(s["mid_ready"], l * NF + F[("hidden", q, NFD - 1)] + 1 + SL)
                            p.wait_ge(s["w_free"], l * NW + W[it] + 1)
                            for t in range(TPS):
                                out = psW[:, t * E:(t + 1) * E]
                                p.matmul(out, ones_row[:], b2row[:], start=True, stop=False)
                                for f, (_, w) in enumerate(FD):
                                    ins = p.matmul(out, mid[0:w, f, t * P:(t + 1) * P], w2[0:w, f, :], start=False,
                                                   stop=(f == NFD - 1))
                            ins.then_inc(s["w_full"], 1)


def layout_d(i, a):
    g = {n: i["L1_ffn_" + n] for n in ("wqkv", "q_scale", "k_scale", "wo", "ln_g", "ln_b", "w1", "b1", "w2", "b2")}
    a["d_wqkv"] = np.ascontiguousarray(g["wqkv"].reshape(DEPTH, E, 3, INNER_D))
    a["d_wo"] = np.ascontiguousarray(g["wo"].reshape(DEPTH, CD, P, E).transpose(0, 2, 1, 3))
    a["d_w1"] = np.ascontiguousarray(g["w1"].reshape(DEPTH, E, 2, HID_D))

    def pad(w):
        o = np.zeros((DEPTH, NFD * P) + w.shape[2:], np.float32)
        o[:, :HID_D] = w
        return o.reshape((DEPTH, NFD, P) + w.shape[2:])

    a["d_w2"] = np.ascontiguousarray(pad(g["w2"]).transpose(0, 2, 1, 3))
    ba, bg = (pad(g["b1"][:, k * HID_D:(k + 1) * HID_D]).transpose(0, 2, 1) for k in range(2))
    a["d_cols"] = np.ascontiguousarray(np.concatenate([g["ln_g"][:, :, None], g["ln_b"][:, :, None], ba, bg], axis=2))
    a["d_b2"] = np.ascontiguousarray(g["b2"][:, None])
    swap = np.concatenate([np.arange(DHD // 2, DHD), np.arange(DHD // 2)])
    gains = np.stack([g["q_scale"], g["q_scale"][:, swap], g["k_scale"], g["k_scale"][:, swap]], axis=1)
    a["d_gains"] = np.ascontiguousarray(np.broadcast_to(gains[:, None], (DEPTH, P, 4, DHD)))
    half = np.arange(0, DHD, 2, dtype=np.float32)
    pos = np.arange(L, dtype=np.float32)
    freq = pos[:, None] * (1.0 / np.float32(10000.0) ** (half / DHD))[None]
    freq = np.concatenate([freq, freq], axis=1)
    base = (half + 0.4 * DHD) / (1.4 * DHD)
    scale = base[None] ** ((pos - L // 2) / float(WINDOW // 2))[:, None]
    scale = np.concatenate([scale, scale], axis=1)
    sign = np.where(np.arange(DHD) < DHD // 2, -1.0, 1.0)
    cos, sin = np.cos(freq), np.sin(freq) * sign
    tab = np.stack([QK_SCALE * cos * scale, QK_SCALE * sin * scale, cos / scale, sin / scale])
    a["d_tables"] = np.ascontiguousarray(tab.reshape(4, TPS, P, DHD).transpose(2, 0, 1, 3)).astype(np.float32)
    q, k = np.arange(P)[:, None], np.arange(P)[None]
    keys, q1 = np.arange(L)[None], q + P
    second = np.where((keys <= q1) & (keys >= q1 - WINDOW), 0.0, MASKED)
    first = np.where((k <= q) & (k >= q - WINDOW), 0.0, MASKED)
    a["d_mask"] = np.concatenate([first, second], axis=1).astype(np.float32)
    down = np.zeros((P, 2, P), np.float32)
    down[np.arange(P - 1), 0, np.arange(1, P)] = 1.0
    down[P - 1, 1, 0] = 1.0
    a["d_down"] = down


def layout_a(i, a):
    a["a_wq"] = np.ascontiguousarray(i["L0_attn_Wq"].transpose(0, 2, 1))
    a["a_wk"] = np.ascontiguousarray(i["L0_attn_Wk"].transpose(0, 2, 1))
    a["a_w1"] = np.ascontiguousarray(i["L0_attn_W1"].transpose(0, 2, 1))
    a["a_w2"] = np.ascontiguousarray(i["L0_attn_W2"].transpose(0, 2, 1).reshape(LAYERS, FC, P, E).transpose(0, 2, 1, 3))
    b1 = i["L0_attn_b1"].reshape(LAYERS, FC, P).transpose(0, 2, 1)
    col = lambda *names: [i["L0_attn_" + n][:, :, None] for n in names]
    a["a_cols"] = np.ascontiguousarray(np.concatenate(col("bq", "bk") + [b1] + col("b2", "ln2_w", "ln2_b", "ln3_w", "ln3_b"), axis=2))
    rows = np.stack([i["L0_attn_" + n] for n in ("ln1_w", "ln1_b", "ln3_w", "ln3_b")], axis=1)
    a["a_rows"] = np.ascontiguousarray(np.broadcast_to(rows[:, None], (LAYERS, P, 4, E)))
    a["a_heads"] = (np.arange(P)[:, None] // DH == np.arange(HEADS)[None]).astype(np.float32)
    pos = np.arange(L)
    a["rel"] = (HEADS * np.exp(-np.abs(pos[:, None] - pos[None, :]) / DECAY)).astype(np.float32)


def layout(i):
    a = {"x": np.ascontiguousarray(i["L0_attn_x"].reshape(NTOK, E)), "ident": np.eye(P, dtype=np.float32)}
    for f in LAYOUTS:
        f(i, a)
    return a


STAGES = [stage_a, stage_b, stage_c, stage_d]
LAYOUTS = [layout_a, layout_b, layout_c, layout_d]


def build(nc, d, out):
    with ExitStack() as ctx:
        x_tok = ctx.enter_context(nc.sbuf_tensor("x_tok", [P, T, E], F32))
        ident = ctx.enter_context(nc.sbuf_tensor("ident", [P, P], F32))
        minus_half = ctx.enter_context(nc.sbuf_tensor("minus_half", [P, T], F32))
        x_in = ctx.enter_context(nc.semaphore("x_in"))
        exponent_set = ctx.enter_context(nc.semaphore("exponent_set"))
        x_out = ctx.enter_context(nc.semaphore("x_out"))
        with nc.Block() as block:
            @block.sync
            def _(sp):
                sp.dma_start(x_tok[:], d["x"].rearrange("(t p) e -> p t e", p=P)).then_inc(x_in, 16)
                sp.dma_start(ident[:], d["ident"]).then_inc(x_in, 16)
                sp.wait_ge(x_in, 32)

            @block.gpsimd
            def _(g):
                g.memset(minus_half[:], -0.5).then_inc(exponent_set, 1)
                g.wait_ge(exponent_set, 1)

        for stage in STAGES:
            stage(nc, d, x_tok, ident, minus_half)
        with nc.Block() as block:
            @block.sync
            def _(sp):
                sp.dma_start(out.rearrange("(t p) e -> p t e", p=P), x_tok[:]).then_inc(x_out, 16)
                sp.wait_ge(x_out, 16)


def kernel(**inputs):
    import concourse.bacc as _bacc
    from concourse.bass_utils import run_bass_kernel_spmd as _run

    nc = _bacc.Bacc("TRN2", target_bir_lowering=False, num_devices=1)
    arrays = layout({k: np.asarray(v) for k, v in inputs.items()})
    aps = {k: nc.dram_tensor("in_" + k, v.shape, F32, kind="ExternalInput").ap() for k, v in arrays.items()}
    out = nc.dram_tensor("out", (NTOK, E), F32, kind="ExternalOutput").ap()
    build(nc, aps, out)
    r = _run(nc, [{"in_" + k: v for k, v in arrays.items()}], core_ids=[0])
    return r.results[0]["out"].reshape(SEQS, L, E)
```

```python
from contextlib import ExitStack

import numpy as np
import concourse.bass as bass
from concourse import mybir

ALU = mybir.AluOpType
ACT = mybir.ActivationFunctionType
AX = mybir.AxisListType
F32 = mybir.dt.float32
BF16 = mybir.dt.bfloat16

P = 128
SEQS, L, E = 8, 256, 128
T = SEQS * L // P
TPS = L // P
NTOK = SEQS * L
EPS = 1e-5
GRP = 512
NG = NTOK // GRP
TPG = GRP // P

LAYERS, HEADS, HID_A = 6, 16, 512
DH = E // HEADS
CH = 4
BH = 2
HALVES = CH // BH
HG = HEADS // CH
FC = HID_A // P
DECAY = 16.0
QSLOTS = 2 * HG
LSLOTS = SEQS * QSLOTS
STEADY = 2


class Chain:

    def __init__(self, eng, sem, base=0):
        self.eng, self.sem, self.base, self.n = eng, sem, base, 0

    def link(self, ins):
        self.n += 1
        ins.then_inc(self.sem, 1)
        self.eng.wait_ge(self.sem, self.base + self.n)


def moments(v, chain, b, n):
    st = b["st"][:, 0:n, :]
    sm = b["sm"][:, 0:n, :]
    chain.link(v.tensor_tensor(sm, st[:, :, 1:3], st[:, :, 4:6], ALU.add))
    chain.link(v.tensor_tensor(b["d"][:, 0:n], st[:, :, 1], st[:, :, 4], ALU.subtract))
    chain.link(v.scalar_tensor_tensor(b["dd"][:, 0:n], b["d"][:, 0:n], E / 4.0, b["d"][:, 0:n], ALU.mult, ALU.mult))
    chain.link(v.tensor_tensor(b["dd"][:, 0:n], b["dd"][:, 0:n], sm[:, :, 1], ALU.add))
    chain.link(v.tensor_scalar(b["mean"][:, 0:n], sm[:, :, 0], 0.5, None, ALU.mult))
    return v.tensor_scalar(b["var"][:, 0:n], b["dd"][:, 0:n], 1.0 / E, EPS, ALU.mult, ALU.add)


def moment_buffers(sb, name, n):
    return {k: sb(f"{name}_{k}", [P, n] + ([w] if w else []))
            for k, w in (("st", 6), ("sm", 2), ("d", 0), ("dd", 0), ("mean", 0), ("var", 0), ("rstd", 0))}


def slots_a(layers):
    slots = {}

    def place(slot, *item):
        slots.setdefault(slot, []).append(item)

    for l in layers:
        for q in range(SEQS):
            at = l * LSLOTS + q * QSLOTS
            if q == 0:
                place(at - 6, "scale_bq", l, q, 0)
            place(at - 5, "project", l, q, 0)
            for j, slot in enumerate((-4, -2, -1, 1)):
                place(at + slot, "mask", l, q, j)
            for k in range(QSLOTS):
                place(at + k, "score", l, q, k)
                place(at + k + 1, "exp", l, q, k)
                place(at + k + 2, "invert", l, q, k)
                place(at + k + 2, "sum", l, q, k)
                place(at + k + (4 if k % HG == 0 else 3), "head_sum", l, q, k)
            for t in range(TPS):
                place(at + 4 * t + 6, "join", l, q, t)
                place(at + 4 * t + 7, "fold", l, q, t)
            for slot, kind, part in ((13, "mix", 0), (14, "turn_mix", 0), (15, "attend", 0), (16, "stats", 0),
                                     (16, "rstd", 0), (18, "norm", 0), (19, "affine", 0), (21, "stats", 1),
                                     (21, "rstd", 1), (23, "norm", 1), (25, "turn_n2", 0), (28, "hidden", 0),
                                     (30, "hidden", 1), (33, "mlp_half", 0), (34, "mlp_out", 0),
                                     (36, "turn_ffr", 0), (36, "stats", 2), (36, "rstd", 2), (37, "norm", 2),
                                     (40, "turn_n3", 0), (42, "affine", 1)):
                place(at + slot, kind, l, q, part)
    return slots


def in_order(items, first=(), last=()):
    rank = {k: n - len(first) for n, k in enumerate(first)} | {k: n + 1 for n, k in enumerate(last)}
    return sorted(items, key=lambda item: rank.get(item[0], 0))


class Fills:

    def __init__(self, slots, *kinds):
        found = [i for n in sorted(slots) for i in slots[n] if i[0] in kinds]
        self.at = {i: n for n, i in enumerate(found)}
        self.per_layer = len(found) // LAYERS
        for n in range(STEADY * LSLOTS, (STEADY + 1) * LSLOTS):
            for kind, lay, q, part in slots[n]:
                for l in range(1, LAYERS - 1) if kind in kinds else ():
                    assert (self.at[kind, lay + l - STEADY, q, part]
                            == self.at[kind, lay, q, part] + self.per_layer * (l - STEADY))
        assert self.per_layer % 2 == 0

    def index(self, kind, layer, steady, q, part):
        if isinstance(layer, int):
            return self.at[kind, layer, q, part]
        return layer * self.per_layer + self.at[kind, steady, q, part] - steady * self.per_layer

    def slot(self, kind, steady, q, part):
        return self.at[kind, steady, q, part] % 2


def stage_a(nc, d, x_tok, ident, minus_half):
    with ExitStack() as ctx:
        def sb(name, shape):
            return ctx.enter_context(nc.sbuf_tensor("a_" + name, shape, F32))

        def two(name, shape):
            return [sb(f"{name}{u}", shape) for u in range(2)]

        def ps(name, shape):
            return ctx.enter_context(nc.psum_tensor("a_" + name, shape, F32))

        h_tok = sb("h_tok", [P, T, E])
        hT = sb("hT", [P, NTOK])
        qT = sb("qT", [P, L])
        kT = two("kT", [P, L])
        qm = two("qm", [P, HEADS, L])
        head_mask = sb("head_mask", [P, HEADS])
        RING = 4
        prob = [sb(f"prob{u}", [P, CH, L]) for u in range(RING)]
        rowsum = [sb(f"rowsum{u}", [P, CH]) for u in range(RING)]
        rowinv = [sb(f"rowinv{u}", [P, CH]) for u in range(RING)]
        negmax = two("negmax", [P, CH])
        diag = [sb(f"diag{u}", [P, P]) for u in range(RING)]
        acc = two("acc", [P, TPS, L])
        odd = sb("odd", [P, TPS, L])
        mix = sb("mix", [P, TPS, L])
        mixT = sb("mixT", [P, TPS, L])
        mixsum = sb("mixsum", [P, TPS])
        mixinv = sb("mixinv", [P, TPS])
        r = two("r", [P, TPS, E])
        n1 = two("n1", [P, TPS, E])
        h2T = two("h2T", [P, L])
        act = sb("act", [P, FC, L])
        ffr = sb("ffr", [P, L])
        n3 = two("n3", [P, TPS, E])
        rel = sb("rel", [P, TPS, L])
        wq = sb("wq", [P, P])
        wk = sb("wk", [P, P])
        qk_cols = sb("qk_cols", [P, 2])
        bqs = sb("bqs", [P, 1])
        qscale = sb("qscale", [P, 1])
        rows1 = sb("rows1", [P, 2, E])
        w1 = sb("w1", [P, HID_A])
        cols2 = sb("cols2", [P, 2])
        b1 = sb("b1", [P, FC])
        w2 = sb("w2", [P, FC, E])
        b2 = sb("b2", [P, 1])
        rows3 = sb("rows3", [P, 2, E])
        cols3 = sb("cols3", [P, 2])
        mb = [[{k: sb(f"{k}{n}_{u}", w) for k, w in (("st", [P, TPS, 6]), ("f", [P, TPS, 3]), ("mv", [P, 3, TPS]))}
               for u in range(2)] for n in range(3)]
        parts = sb("parts", [P, TPS, 3])
        eps = sb("eps", [P, TPS])
        minus_one = sb("minus_one", [P, TPS])
        mb0 = [moment_buffers(sb, f"x{k}", TPG) for k in range(2)]

        psS = [ps(f"scores{u}", [P, CH, L]) for u in range(2)]
        psT = [ps(f"turn{u}", [P, TPS, L]) for u in range(2)]
        psH = ps("heads", [P, TPS, L])
        psW = ps("work", [P, 2 * L])

        names = ("const_in", "qk_in", "norm1_in", "hidden_in", "out_in", "norm3_in", "q_scale", "bqs_ready",
                 "qk_ready", "qm_ready", "scores_ready", "negmax_ready", "exp_done", "recip_done", "acc_step",
                 "sum_done", "diag_ready", "head_done", "join_done", "fold_done", "mix_ready", "mixinv_done",
                 "t_full", "t_free", "w_full", "w_free", "r_ready", "stats0", "stats1", "stats2", "step0", "step1",
                 "step2", "rstd0", "rstd1", "rstd2", "norm0", "norm1", "norm2", "gain1",
                 "gain3", "n1_ready", "h2T_ready", "act_ready", "ffr_ready", "hT_ready", "h_tok_ready", "h_turned", "x_chain",
                 "x_var", "x_rstd", "x_ready")
        s = {n: ctx.enter_context(nc.semaphore("a_" + n)) for n in names}
        G8 = QSLOTS

        slots = slots_a(range(LAYERS))
        TF = Fills(slots, "project", "turn_mix", "turn_n2", "hidden", "turn_n3")
        WF = Fills(slots, "attend", "mlp_out", "turn_ffr")

        def run(eng, do, first=(), last=()):
            def span(low, high):
                for n in range(low, high):
                    yield from in_order(slots.get(n, []), first, last)

            for kind, lay, q, part in span(min(slots), LSLOTS):
                do(kind, lay, lay, q, part)
            with eng.Fori(1, LAYERS - 1) as l:
                for kind, lay, q, part in span(STEADY * LSLOTS, (STEADY + 1) * LSLOTS):
                    do(kind, l + (lay - STEADY), lay, q, part)
            for kind, lay, q, part in span((LAYERS - 1) * LSLOTS, max(slots) + 1):
                do(kind, lay, lay, q, part)

        with nc.Block() as block:
            @block.sync
            def _(sp):
                sp.dma_start(rel[:], d["rel"].rearrange("(t p) m -> p t m", p=P)).then_inc(s["const_in"], 16)
                sp.dma_start(head_mask[:], d["a_heads"]).then_inc(s["const_in"], 16)

                def load(l, signal, *pairs):
                    for dst, name in pairs:
                        sp.dma_start(dst[:], d[name][l]).then_inc(s[signal], 16)

                qk = ("qk_in", (wq, "a_wq"), (wk, "a_wk"), (qk_cols, "a_qk_cols"))
                norm1 = ("norm1_in", (rows1, "a_rows1"))
                hidden = ("hidden_in", (cols2, "a_cols2"), (w1, "a_w1"), (b1, "a_b1"))
                out = ("out_in", (w2, "a_w2"), (b2, "a_b2"))
                norm3 = ("norm3_in", (rows3, "a_rows3"), (cols3, "a_cols3"))
                for group in (qk, norm1, hidden, out, norm3):
                    load(0, *group)
                with sp.Fori(0, LAYERS - 1) as l:
                    n = (l + 1) * SEQS
                    sp.wait_ge(s["qk_ready"], n * 2)
                    load(l + 1, *qk)
                    sp.wait_ge(s["n1_ready"], n)
                    load(l + 1, *norm1)
                    sp.wait_ge(s["act_ready"], n * FC)
                    load(l + 1, *hidden)
                    sp.wait_ge(s["ffr_ready"], n)
                    load(l + 1, *out)
                    sp.wait_ge(s["hT_ready"], n + SEQS)
                    sp.wait_ge(s["h_tok_ready"], n + SEQS)
                    load(l + 1, *norm3)

            @block.gpsimd
            def _(g):
                g.sem_inc(s["diag_ready"], RING)
                g.sem_inc(s["qm_ready"], HG)
                g.sem_inc(s["fold_done"], TPS)
                g.memset(qscale[:], float(DH) ** -0.5)
                g.memset(eps[:], EPS)
                g.memset(minus_one[:], -1.0)
                g.memset(parts[:, :, 0], 0.5)
                g.memset(parts[:, :, 2], 0.5)
                g.memset(parts[:, :, 1], 1.0 / E).then_inc(s["q_scale"], 1)
                for k in range(NG):
                    g.wait_ge(s["x_var"], k + 1)
                    g.tensor_tensor(mb0[k % 2]["rstd"][:], mb0[k % 2]["var"][:], minus_half[:, 0:TPG],
                                    ALU.pow).then_inc(s["x_rstd"], 1)
                g.wait_ge(s["q_scale"], 1)
                g.wait_ge(s["const_in"], 32)

                def do(kind, lay, steady, q, part):
                    m = lay * SEQS + q
                    u = q % 2
                    if kind == "scale_bq":
                        g.wait_ge(s["qk_in"], (lay + 1) * 48)
                        g.tensor_tensor(bqs[:], qk_cols[:, 0:1], qscale[:], ALU.mult).then_inc(s["bqs_ready"], 1)
                    elif kind == "mask":
                        if part == 0:
                            g.wait_ge(s["qk_ready"], m * 2 + 1)
                        g.wait_ge(s["scores_ready"], ((m - 2) * G8 + HG + part + 1 + 2 * G8) * HALVES)
                        hs = slice(part * CH, (part + 1) * CH)
                        g.tensor_tensor(qm[u][:, hs, :], qT[:].unsqueeze(1).broadcast_to([P, CH, L]),
                                        head_mask[:, hs].unsqueeze(2).broadcast_to([P, CH, L]), ALU.mult)\
                            .then_inc(s["qm_ready"], 1)
                    elif kind == "sum":
                        n = m * G8 + part
                        g.wait_ge(s["recip_done"], n + 1)
                        g.wait_ge(s["head_done"], n - RING + 1 + RING)
                        g.tensor_tensor(diag[part % RING][:], ident[:],
                                        rowinv[part % RING][:, CH - 1:CH].broadcast_to([P, P]), ALU.mult)\
                            .then_inc(s["diag_ready"], 1)
                    elif kind == "fold":
                        g.wait_ge(s["join_done"], m * TPS + part + 1 + TPS)
                        g.tensor_tensor(acc[u][:, part, :], acc[u][:, part, :], odd[:, part, :], ALU.add)\
                            .then_inc(s["fold_done"], 1)
                    elif kind == "rstd":
                        f, mv = mb[part][u]["f"], mb[part][u]["mv"]
                        st, step, steps = mb[part][u]["st"], s[f"step{part}"], 5 if part == 2 else 7
                        g.wait_ge(s[f"stats{part}"], m + 1)
                        g.tensor_tensor(f[:, :, 0:2], st[:, :, 1:3], st[:, :, 4:6], ALU.add).then_inc(step, 1)
                        g.tensor_tensor(f[:, :, 2], st[:, :, 1], st[:, :, 4], ALU.subtract).then_inc(step, 1)
                        g.wait_ge(step, m * steps + 2)
                        g.tensor_tensor(f[:], f[:], parts[:], ALU.mult).then_inc(step, 1)
                        g.wait_ge(step, m * steps + 3)
                        g.tensor_tensor(mv[:, 0, :], f[:, :, 2], f[:, :, 2], ALU.mult)
                        g.tensor_tensor(mv[:, 1, :], f[:, :, 1], eps[:], ALU.add).then_inc(step, 1)
                        g.wait_ge(step, m * steps + 4)
                        g.tensor_tensor(mv[:, 0, :], mv[:, 0, :], mv[:, 1, :], ALU.add).then_inc(step, 1)
                        g.wait_ge(step, m * steps + 5)
                        pow_ = g.tensor_tensor(mv[:, 1, :], mv[:, 0, :], minus_half[:, 0:TPS], ALU.pow)
                        if part == 2:
                            pow_.then_inc(s["rstd2"], 1)
                        else:
                            pow_.then_inc(step, 1)
                            g.tensor_tensor(mv[:, 2, :], f[:, :, 0], minus_one[:], ALU.mult).then_inc(step, 1)
                            g.wait_ge(step, m * steps + 7)
                            g.tensor_tensor(mv[:, 0, :], mv[:, 2, :], mv[:, 1, :], ALU.mult)\
                                .then_inc(s[f"rstd{part}"], 1)
                    elif kind == "affine" and part == 0:
                        g.wait_ge(s["norm1_in"], (lay + 1) * 16)
                        g.wait_ge(s["norm0"], m + 1)
                        g.tensor_tensor(n1[u][:], r[u][:], rows1[:, 0:1, :].broadcast_to([P, TPS, E]), ALU.mult)\
                            .then_inc(s["gain1"], 1)
                        g.wait_ge(s["gain1"], m + 1)
                        g.tensor_tensor(n1[u][:], n1[u][:], rows1[:, 1:2, :].broadcast_to([P, TPS, E]), ALU.add)\
                            .then_inc(s["n1_ready"], 1)
                    elif kind == "affine":
                        ts = slice(q * TPS, (q + 1) * TPS)
                        g.wait_ge(s["norm3_in"], (lay + 1) * 32)
                        g.wait_ge(s["norm2"], m + 1)
                        g.tensor_tensor(h_tok[:, ts, :], n3[u][:], rows3[:, 0:1, :].broadcast_to([P, TPS, E]),
                                        ALU.mult).then_inc(s["gain3"], 1)
                        g.wait_ge(s["gain3"], m + 1)
                        g.tensor_tensor(h_tok[:, ts, :], h_tok[:, ts, :], rows3[:, 1:2, :]
                                        .broadcast_to([P, TPS, E]), ALU.add).then_inc(s["h_tok_ready"], 1)

                run(g, do, first=("sum",), last=("mask",))

            @block.scalar
            def _(a):
                a.sem_inc(s["exp_done"], 2 * HALVES)
                a.sem_inc(s["t_free"], 2)
                a.sem_inc(s["mix_ready"], 2 * TPS)
                for q in range(SEQS):
                    a.wait_ge(s["h_turned"], q + 1)
                    a.activation(hT[:, q * L:(q + 1) * L], psT[q % 2][:, 0, :], ACT.Copy).then_inc(s["hT_ready"], 1)

                def do(kind, lay, steady, q, part):
                    m = lay * SEQS + q
                    u = q % 2
                    if kind in ("project", "turn_mix", "turn_n2", "hidden", "turn_n3"):
                        i = TF.index(kind, lay, steady, q, part)
                        src = psT[TF.slot(kind, steady, q, part)]
                        a.wait_ge(s["t_full"], i + 1)
                    if kind == "project":
                        a.wait_ge(s["bqs_ready"], lay + 1)
                        a.wait_ge(s["qm_ready"], m * HG + HG)
                        a.activation(qT[:], src[:, 0, :], ACT.Identity, bias=bqs[:], scale=float(DH) ** -0.5)\
                            .then_inc(s["qk_ready"], 1)
                        a.activation(kT[u][:], src[:, 1, :], ACT.Identity, bias=qk_cols[:, 1:2])\
                            .then_inc(s["qk_ready"], 1)
                        a.wait_ge(s["qk_ready"], 2 * m + 2)
                        a.sem_inc(s["t_free"], 1)
                    elif kind == "exp":
                        n = m * G8 + part
                        a.wait_ge(s["sum_done"], n - RING + 1 + RING)
                        a.wait_ge(s["head_done"], n - RING + 1 + RING)
                        for c in range(CH):
                            if c % BH == 0:
                                a.wait_ge(s["negmax_ready"], n * HALVES + c // BH + 1)
                            ins = a.activation(prob[part % RING][:, c, :], psS[part % 2][:, c, :], ACT.Exp,
                                               bias=negmax[part % 2][:, c:c + 1],
                                               accum_out=rowsum[part % RING][:, c:c + 1])
                            if c % BH == BH - 1:
                                ins.then_inc(s["exp_done"], 1)
                    elif kind == "mix":
                        a.wait_ge(s["fold_done"], (m + 1) * TPS + TPS)
                        a.wait_ge(s["mixinv_done"], m + 1)
                        for t in range(TPS):
                            a.activation(mix[:, t, :], acc[u][:, t, :], ACT.Exp, scale=1.0 / HEADS,
                                         accum_out=mixsum[:, t:t + 1]).then_inc(s["mix_ready"], 1)
                    elif kind == "norm" and part < 2:
                        a.wait_ge(s[f"rstd{part}"], m + 1)
                        y, mv = (r, n1)[part][u], mb[part][u]["mv"]
                        for t in range(TPS):
                            ins = a.activation(y[:, t, :], y[:, t, :], ACT.Identity, bias=mv[:, 0, t:t + 1],
                                               scale=mv[:, 1, t:t + 1])
                        ins.then_inc(s[f"norm{part}"], 1)
                    elif kind == "turn_mix":
                        a.activation(mixT[:], src[:], ACT.Copy).then_inc(s["t_free"], 1)
                    elif kind == "turn_n2":
                        a.wait_ge(s["hidden_in"], (lay + 1) * 48)
                        a.activation(h2T[u][:], src[:, 0, :], ACT.Identity, bias=cols2[:, 1:2], scale=cols2[:, 0:1])\
                            .then_inc(s["h2T_ready"], 1)
                        a.wait_ge(s["h2T_ready"], m + 1)
                        a.sem_inc(s["t_free"], 1)
                    elif kind == "hidden":
                        a.wait_ge(s["hidden_in"], (lay + 1) * 48)
                        for k in range(2):
                            f = 2 * part + k
                            a.activation(act[:, f, :], src[:, k, :], ACT.Relu, bias=b1[:, f:f + 1])\
                                .then_inc(s["act_ready"], 1)
                        a.wait_ge(s["act_ready"], m * FC + 2 * part + 2)
                        a.sem_inc(s["t_free"], 1)
                    elif kind == "turn_n3":
                        a.wait_ge(s["norm3_in"], (lay + 1) * 32)
                        a.activation(hT[:, q * L:(q + 1) * L], src[:, 0, :], ACT.Identity, bias=cols3[:, 1:2],
                                     scale=cols3[:, 0:1]).then_inc(s["hT_ready"], 1)
                        a.wait_ge(s["hT_ready"], m + 1 + SEQS)
                        a.sem_inc(s["t_free"], 1)

                run(a, do, first=("exp",))

            @block.vector
            def _(v):
                v.sem_inc(s["sum_done"], RING)
                v.sem_inc(s["w_free"], 1)
                v.sem_inc(s["mixinv_done"], 1)
                v.sem_inc(s["join_done"], TPS)
                chain = Chain(v, s["x_chain"])
                for k in range(NG):
                    b = mb0[k % 2]
                    for t in range(TPG):
                        ins = v.bn_stats(b["st"][:, t, :], x_tok[:, k * TPG + t, :])
                    chain.link(ins)
                    moments(v, chain, b, TPG).then_inc(s["x_var"], 1)
                    v.wait_ge(s["x_rstd"], k + 1)
                    for t in range(TPG):
                        ins = v.tensor_scalar(h_tok[:, k * TPG + t, :], x_tok[:, k * TPG + t, :], b["mean"][:, t:t + 1],
                                              b["rstd"][:, t:t + 1], ALU.subtract, ALU.mult)
                        if t % TPS == TPS - 1:
                            ins.then_inc(s["h_tok_ready"], 1)
                v.wait_ge(s["const_in"], 32)

                def sums(m, u, part):
                    n = m * G8 + part
                    t, j = part // HG, part % HG
                    pr, inv = prob[part % RING], rowinv[part % RING]
                    v.wait_ge(s["recip_done"], n + 1)
                    v.wait_ge(s["sum_done"], n - 1 + 1 + RING)
                    if j == 0:
                        v.wait_ge(s["mix_ready"], (m - 2) * TPS + TPS + 2 * TPS)
                        v.scalar_tensor_tensor(acc[u][:, t, :], pr[:, 0, :], inv[:, 0:1], rel[:, t, :],
                                               ALU.mult, ALU.add).then_inc(s["acc_step"], 1)
                        v.wait_ge(s["fold_done"], (m - 1) * TPS + t + 1 + TPS)
                        v.tensor_scalar(odd[:, t, :], pr[:, 1, :], inv[:, 1:2], None, ALU.mult)
                    else:
                        v.scalar_tensor_tensor(acc[u][:, t, :], pr[:, 0, :], inv[:, 0:1], acc[u][:, t, :],
                                               ALU.mult, ALU.add).then_inc(s["acc_step"], 1)
                        v.scalar_tensor_tensor(odd[:, t, :], pr[:, 1, :], inv[:, 1:2], odd[:, t, :],
                                               ALU.mult, ALU.add)
                    v.wait_ge(s["acc_step"], n + 1)
                    v.scalar_tensor_tensor(acc[u][:, t, :], pr[:, 2, :], inv[:, 2:3], acc[u][:, t, :],
                                           ALU.mult, ALU.add).then_inc(s["sum_done"], 1)

                def join(m, u, t):
                    n = m * G8 + t * HG + HG - 1
                    v.wait_ge(s["sum_done"], n + 1 + RING)
                    v.wait_ge(s["head_done"], n + 1 + RING)
                    v.tensor_tensor(acc[u][:, t, :], acc[u][:, t, :], psH[:, t, :], ALU.add)\
                        .then_inc(s["join_done"], 1)

                def stats(m, u, k, src):
                    b = mb[k][u]
                    for t in range(TPS):
                        ins = v.bn_stats(b["st"][:, t, :], src[:, t, :])
                    ins.then_inc(s[f"stats{k}"], 1)

                def norm(m, u, k, src, dst):
                    b = mb[k][u]
                    v.wait_ge(s[f"rstd{k}"], m + 1)
                    for t in range(TPS):
                        ins = v.tensor_scalar(dst[:, t, :], src[:, t, :], b["f"][:, t, 0:1], b["mv"][:, 1, t:t + 1],
                                              ALU.subtract, ALU.mult)
                    ins.then_inc(s[f"norm{k}"], 1)

                psY = psW[:, 0:L].rearrange("p (t e) -> p t e", t=TPS)

                def do(kind, lay, steady, q, part):
                    m = lay * SEQS + q
                    u = q % 2
                    if kind in ("attend", "mlp_out", "turn_ffr"):
                        i = WF.index(kind, lay, steady, q, part)
                        v.wait_ge(s["w_full"], i + 1)
                    if kind == "score":
                        n = m * G8 + part
                        for h in range(HALVES):
                            hs = slice(h * BH, (h + 1) * BH)
                            v.wait_ge(s["scores_ready"], (n + 2 * G8) * HALVES + h + 1)
                            v.wait_ge(s["exp_done"], n * HALVES + h + 1)
                            v.tensor_reduce(negmax[part % 2][:, hs], psS[part % 2][:, hs, :], AX.X, ALU.max,
                                            negate=True).then_inc(s["negmax_ready"], 1)
                    elif kind == "invert":
                        v.wait_ge(s["exp_done"], (m * G8 + part + 1 + 2) * HALVES)
                        v.wait_ge(s["diag_ready"], m * G8 + part - RING + 1 + RING)
                        v.reciprocal(rowinv[part % RING][:], rowsum[part % RING][:]).then_inc(s["recip_done"], 1)
                    elif kind == "sum":
                        sums(m, u, part)
                    elif kind == "join":
                        join(m, u, part)
                    elif kind == "attend":
                        v.wait_ge(s["mix_ready"], (m + 1) * TPS + 2 * TPS)
                        v.reciprocal(mixinv[:], mixsum[:]).then_inc(s["mixinv_done"], 1)
                        v.wait_ge(s["mixinv_done"], m + 1 + 1)
                        for t in range(TPS):
                            v.scalar_tensor_tensor(r[u][:, t, :], psY[:, t, :], mixinv[:, t:t + 1],
                                                   h_tok[:, q * TPS + t, :], ALU.mult, ALU.add)\
                                .then_inc(s["r_ready"], 1)
                        v.wait_ge(s["r_ready"], (m + 1) * TPS)
                        v.sem_inc(s["w_free"], 1)
                    elif kind == "stats":
                        if part == 1:
                            v.wait_ge(s["n1_ready"], m + 1)
                        stats(m, u, part, (r[u], n1[u], psY)[part])
                    elif kind == "norm" and part == 2:
                        norm(m, u, 2, psY, n3[u])
                        v.wait_ge(s["norm2"], m + 1)
                        v.sem_inc(s["w_free"], 1)
                    elif kind == "mlp_out":
                        v.wait_ge(s["out_in"], (lay + 1) * 32)
                        v.scalar_tensor_tensor(ffr[:], psW[:, 0:L], b2[:], h2T[u][:], ALU.add, ALU.add)\
                            .then_inc(s["ffr_ready"], 1)
                        v.wait_ge(s["ffr_ready"], m + 1)
                        v.sem_inc(s["w_free"], 1)

                run(v, do, first=("invert", "score", "sum", "join"))
                v.wait_ge(s["h_tok_ready"], (LAYERS + 1) * SEQS)
                v.tensor_tensor(x_tok[:], x_tok[:], h_tok[:], ALU.add).then_inc(s["x_ready"], 1)
                v.wait_ge(s["x_ready"], 1)

            @block.tensor
            def _(p):
                p.sem_inc(s["scores_ready"], 2 * G8 * HALVES)
                p.sem_inc(s["head_done"], RING)
                for q in range(SEQS):
                    p.wait_ge(s["h_tok_ready"], q + 1)
                    if q >= 2:
                        p.wait_ge(s["hT_ready"], q - 1)
                    for t in range(TPS):
                        ins = p.transpose(psT[q % 2][:, 0, t * P:(t + 1) * P], h_tok[:, q * TPS + t, :], ident[:])
                    ins.then_inc(s["h_turned"], 1)
                p.wait_ge(s["hT_ready"], SEQS)

                def do(kind, lay, steady, q, part):
                    m = lay * SEQS + q
                    u = q % 2
                    if kind in ("project", "turn_mix", "turn_n2", "hidden", "turn_n3"):
                        i = TF.index(kind, lay, steady, q, part)
                        dst = psT[TF.slot(kind, steady, q, part)]
                        p.wait_ge(s["t_free"], i - 2 + 1 + 2)
                    if kind in ("attend", "mlp_half", "turn_ffr"):
                        i = WF.index(kind.replace("half", "out"), lay, steady, q, part)
                        p.wait_ge(s["w_free"], i - 1 + 1 + 1)

                    def evacuated(kind, part=0):
                        p.wait_ge(s["t_free"], TF.index(kind, lay, steady, q, part) + 1 + 2)

                    if kind == "project":
                        p.wait_ge(s["qk_in"], (lay + 1) * 48)
                        p.wait_ge(s["hT_ready"], m + 1)
                        for k, w in enumerate((wq, wk)):
                            ins = p.matmul(dst[:, k, :], w[:], hT[:, q * L:(q + 1) * L], start=True, stop=True)
                        ins.then_inc(s["t_full"], 1)
                    elif kind == "score":
                        n = m * G8 + part
                        t, j = part // HG, part % HG
                        evacuated("project")
                        p.wait_ge(s["qm_ready"], m * HG + j + 1 + HG)
                        for c in range(CH):
                            if c % BH == 0:
                                p.wait_ge(s["exp_done"], n * HALVES + c // BH + 1)
                            ins = p.matmul(psS[part % 2][:, c, :], qm[u][:, j * CH + c, t * P:(t + 1) * P], kT[u][:],
                                           start=True, stop=True)
                            if c % BH == BH - 1:
                                ins.then_inc(s["scores_ready"], 1)
                    elif kind == "head_sum":
                        n = m * G8 + part
                        t, j = part // HG, part % HG
                        p.wait_ge(s["diag_ready"], n + 1 + RING)
                        if j == 0:
                            p.wait_ge(s["join_done"], m * TPS + t + TPS)
                        p.matmul(psH[:, t, :], diag[part % RING][:], prob[part % RING][:, CH - 1, :], start=(j == 0),
                                 stop=(j == HG - 1)).then_inc(s["head_done"], 1)
                    elif kind == "turn_mix":
                        p.wait_ge(s["mix_ready"], (m + 1) * TPS + 2 * TPS)
                        for t in range(TPS):
                            for k in range(TPS):
                                ins = p.transpose(dst[:, k, t * P:(t + 1) * P], mix[:, t, k * P:(k + 1) * P], ident[:])
                        ins.then_inc(s["t_full"], 1)
                    elif kind == "attend":
                        evacuated("turn_mix")
                        p.wait_ge(s["h_tok_ready"], m + 1)
                        for t in range(TPS):
                            for k in range(TPS):
                                ins = p.matmul(psW[:, t * E:(t + 1) * E], mixT[:, k, t * P:(t + 1) * P],
                                               h_tok[:, q * TPS + k, :], start=(k == 0), stop=(k == TPS - 1))
                        ins.then_inc(s["w_full"], 1)
                    elif kind == "turn_n2":
                        p.wait_ge(s["norm1"], m + 1)
                        for t in range(TPS):
                            ins = p.transpose(dst[:, 0, t * P:(t + 1) * P], n1[u][:, t, :], ident[:])
                        ins.then_inc(s["t_full"], 1)
                    elif kind == "hidden":
                        p.wait_ge(s["h2T_ready"], m + 1)
                        p.wait_ge(s["hidden_in"], (lay + 1) * 48)
                        for k in range(2):
                            f = 2 * part + k
                            ins = p.matmul(dst[:, k, :], w1[:, f * P:(f + 1) * P], h2T[u][:], start=True, stop=True)
                        ins.then_inc(s["t_full"], 1)
                    elif kind in ("mlp_half", "mlp_out"):
                        h = FC // 2 * (kind == "mlp_out")
                        if h == 0:
                            evacuated("hidden", 1)
                            p.wait_ge(s["out_in"], (lay + 1) * 32)
                        for f in range(h, h + FC // 2):
                            ins = p.matmul(psW[:, 0:L], w2[:, f, :], act[:, f, :], start=(f == 0), stop=(f == FC - 1))
                        if h:
                            ins.then_inc(s["w_full"], 1)
                    elif kind == "turn_ffr":
                        p.wait_ge(s["ffr_ready"], m + 1)
                        for t in range(TPS):
                            ins = p.transpose(psW[:, t * P:(t + 1) * P], ffr[:, t * P:(t + 1) * P], ident[:])
                        ins.then_inc(s["w_full"], 1)
                    elif kind == "turn_n3":
                        p.wait_ge(s["norm2"], m + 1)
                        for t in range(TPS):
                            ins = p.transpose(dst[:, 0, t * P:(t + 1) * P], n3[u][:, t, :], ident[:])
                        ins.then_inc(s["t_full"], 1)

                run(p, do, last=("score", "head_sum"))


EXPERTS, HID_B = 8, 352
FB = [(f, min(P, HID_B - f)) for f in range(0, HID_B, P)]
NFB = len(FB)


def stage_b(nc, d, x_tok, ident, minus_half):
    with ExitStack() as ctx:
        def sb(name, shape):
            return ctx.enter_context(nc.sbuf_tensor("b_" + name, shape, F32))

        def ps(name, shape):
            return ctx.enter_context(nc.psum_tensor("b_" + name, shape, F32))

        xn = sb("xn", [P, T, E])
        xg = sb("xg", [P, T, E])
        xnT = sb("xnT", [P, NTOK])
        xgT = sb("xgT", [P, NTOK])
        router = sb("router", [P, EXPERTS])
        rank = sb("rank", [P, EXPERTS])
        top = sb("top", [P, T])
        gate = sb("gate", [P, T])
        score = sb("score", [P, T, EXPERTS])
        ranked = sb("ranked", [P, T, EXPERTS])
        best = sb("best", [P, T])
        own = sb("own", [P, EXPERTS, T])
        mask = [sb(f"mask{u}", [P, T]) for u in range(2)]
        w13 = [sb(f"w13_{u}", [P, 2, HID_B]) for u in range(2)]
        w2 = [sb(f"w2_{u}", [P, NFB, E]) for u in range(2)]
        silu = [sb(f"silu{u}", [P, GRP]) for u in range(2)]
        mid = [sb(f"mid{u}", [P, NFB, GRP]) for u in range(2)]
        mb = [moment_buffers(sb, f"m{u}", T // 2) for u in range(2)]
        psH = [ps(f"h1_{u}", [P, GRP]) for u in range(2)]
        psG = [ps(f"h3_{u}", [P, GRP]) for u in range(2)]
        psO = [ps(f"o{u}", [P, GRP]) for u in range(2)]
        psX = [ps(f"x{u}", [P, GRP]) for u in range(2)]

        names = ("const_in", "weights0_in", "weights1_in", "chain", "var_ready", "rstd_ready", "xn_ready", "turned",
                 "xnT_ready", "xgT_ready", "scores_ready", "top_ready", "gate_ready", "xg_ready", "hidden_ready",
                 "silu_ready", "mid_ready", "out_ready", "acc_done", "mask_ready")
        s = {n: ctx.enter_context(nc.semaphore("b_" + n)) for n in names}
        H2 = T // 2
        SL = 2
        CPS = NG * NFB

        with nc.Block() as block:
            @block.sync
            def _(sp):
                sp.dma_start(router[:], d["b_router"]).then_inc(s["const_in"], 16)
                sp.dma_start(rank[:], d["b_rank"]).then_inc(s["const_in"], 16)

                def load(e, u):
                    sp.dma_start(w13[u][:], d["b_w13"][e]).then_inc(s[f"weights{u}_in"], 16)
                    sp.dma_start(w2[u][:], d["b_w2"][e]).then_inc(s[f"weights{u}_in"], 16)

                load(0, 1)
                load(1, 0)
                with sp.Fori(0, EXPERTS // 2 - 1) as i:
                    for u in range(2):
                        sp.wait_ge(s["out_ready"], (2 * i + u + 1) * NG + SL)
                        load(2 * i + u + 2, 1 - u)
                sp.wait_ge(s["out_ready"], (EXPERTS - 1) * NG + SL)
                load(EXPERTS, 1)

            @block.gpsimd
            def _(g):
                for k in range(2):
                    g.wait_ge(s["var_ready"], k + 1)
                    g.tensor_tensor(mb[k]["rstd"][:], mb[k]["var"][:], minus_half[:, 0:H2], ALU.pow)\
                        .then_inc(s["rstd_ready"], 1)

            @block.scalar
            def _(a):
                for k in range(NG):
                    a.wait_ge(s["turned"], k + 1)
                    a.activation(xnT[:, k * GRP:(k + 1) * GRP], psX[k % 2][:], ACT.Copy).then_inc(s["xnT_ready"], 1)
                a.wait_ge(s["top_ready"], 1)
                a.activation(gate[:], top[:], ACT.Sigmoid).then_inc(s["gate_ready"], 1)
                def step(n):
                    for k in range(NG):
                        for f, (_, w) in enumerate(FB):
                            i = k * NFB + f
                            a.wait_ge(s["hidden_ready"], n * CPS + i + 1)
                            a.wait_ge(s["mid_ready"], n * CPS + i + 1)
                            a.activation(silu[i % 2][0:w, :], psH[i % 2][0:w, :], ACT.Silu)\
                                .then_inc(s["silu_ready"], 1)

                step(0)
                for k in range(NG):
                    a.wait_ge(s["turned"], NG + k + 1)
                    a.activation(xgT[:, k * GRP:(k + 1) * GRP], psX[k % 2][:], ACT.Copy).then_inc(s["xgT_ready"], 1)
                with a.Fori(0, EXPERTS) as e:
                    step(e + 1)

            @block.vector
            def _(v):
                v.sem_inc(s["mid_ready"], SL)
                v.sem_inc(s["acc_done"], SL)
                chain = Chain(v, s["chain"])
                for k in range(2):
                    for t in range(H2):
                        ins = v.bn_stats(mb[k]["st"][:, t, :], x_tok[:, k * H2 + t, :])
                    chain.link(ins)
                    moments(v, chain, mb[k], H2).then_inc(s["var_ready"], 1)
                for k in range(2):
                    v.wait_ge(s["rstd_ready"], k + 1)
                    for t in range(H2):
                        ins = v.tensor_scalar(xn[:, k * H2 + t, :], x_tok[:, k * H2 + t, :], mb[k]["mean"][:, t:t + 1],
                                              mb[k]["rstd"][:, t:t + 1], ALU.subtract, ALU.mult)
                        if t % TPG == TPG - 1:
                            ins.then_inc(s["xn_ready"], 1)
                v.wait_ge(s["const_in"], 32)
                v.wait_ge(s["scores_ready"], 1)
                sc = psO[0][:, 0:T * EXPERTS].rearrange("p (t e) -> p t e", e=EXPERTS)
                chain.link(v.tensor_copy(score[:], sc))
                v.tensor_reduce(top[:], score[:], AX.X, ALU.max).then_inc(s["top_ready"], 1)
                v.wait_ge(s["top_ready"], 1)
                chain.link(v.tensor_tensor(ranked[:], score[:], top[:].unsqueeze(2).broadcast_to([P, T, EXPERTS]),
                                           ALU.is_equal))
                chain.link(v.tensor_tensor(ranked[:], ranked[:],
                                           rank[:].unsqueeze(1).broadcast_to([P, T, EXPERTS]), ALU.mult))
                chain.link(v.tensor_reduce(best[:], ranked[:], AX.X, ALU.max))
                chain.link(v.tensor_tensor(own[:].rearrange("p e t -> p t e"), ranked[:],
                                           best[:].unsqueeze(2).broadcast_to([P, T, EXPERTS]), ALU.is_equal))
                chain.link(v.memset(mask[1][:], 1.0))
                v.wait_ge(s["gate_ready"], 1)
                for t in range(T):
                    ins = v.tensor_scalar(xg[:, t, :], xn[:, t, :], gate[:, t:t + 1], None, ALU.mult)
                    if t % TPG == TPG - 1:
                        ins.then_inc(s["xg_ready"], 1)

                def product(n, k, f):
                    i = k * NFB + f
                    w = FB[f][1]
                    v.wait_ge(s["silu_ready"], n * CPS + i + 1)
                    v.wait_ge(s["out_ready"], n * NG + k - 1 + SL)
                    v.tensor_tensor(mid[k % 2][0:w, f, :], silu[i % 2][0:w, :], psG[i % 2][0:w, :], ALU.mult)\
                        .then_inc(s["mid_ready"], 1)

                def add_out(n, u, k):
                    v.wait_ge(s["out_ready"], n * NG + k + 1 + SL)
                    if not isinstance(n, int) or n:
                        v.wait_ge(s["acc_done"], n * NG + k - NG + 1 + SL)
                    for t in range(TPG):
                        x1 = x_tok[:, k * TPG + t, :]
                        ins = v.scalar_tensor_tensor(x1, psO[k % 2][:, t * E:(t + 1) * E],
                                                     mask[u][:, k * TPG + t:k * TPG + t + 1], x1, ALU.mult, ALU.add)
                    ins.then_inc(s["acc_done"], 1)

                for k in range(NG):
                    for f in range(NFB):
                        product(0, k, f)
                    if k:
                        add_out(0, 1, k - 1)
                with v.Fori(0, EXPERTS // 2) as i:
                    for u in range(2):
                        n = 2 * i + u + 1
                        for k in range(NG):
                            for f in range(NFB):
                                product(n, k, f)
                                if k == 0 and f == 0:
                                    add_out(n - 1, 1 - u, NG - 1)
                                    v.tensor_copy(mask[u][:], own[:, bass.ds(2 * i + u, 1), :]
                                                  .rearrange("p o t -> p (o t)")).then_inc(s["mask_ready"], 1)
                                    v.wait_ge(s["mask_ready"], n)
                            if k:
                                add_out(n, u, k - 1)
                add_out(EXPERTS, 1, NG - 1)
                v.wait_ge(s["acc_done"], (EXPERTS + 1) * NG + SL)

            @block.tensor
            def _(p):
                p.sem_inc(s["out_ready"], SL)

                def turn(src, k, ready, free):
                    p.wait_ge(s[ready], k + 1)
                    if free:
                        p.wait_ge(*free)
                    for t in range(TPG):
                        ins = p.transpose(psX[k % 2][:, t * P:(t + 1) * P], src[:, k * TPG + t, :], ident[:])
                    ins.then_inc(s["turned"], 1)

                for k in range(NG):
                    turn(xn, k, "xn_ready", (s["xnT_ready"], k - 1) if k >= 2 else None)
                p.wait_ge(s["const_in"], 32)
                p.wait_ge(s["xnT_ready"], NG)
                for t in range(T):
                    ins = p.matmul(psO[0][:, t * EXPERTS:(t + 1) * EXPERTS], xnT[:, t * P:(t + 1) * P], router[:],
                                   start=True, stop=True)
                ins.then_inc(s["scores_ready"], 1)

                def hidden(n, u, x, k, f):
                    i = k * NFB + f
                    f0, w = FB[f]
                    p.wait_ge(s["mid_ready"], n * CPS + i + 1)
                    p.matmul(psH[i % 2][0:w, :], w13[u][:, 0, f0:f0 + w], x[:, k * GRP:(k + 1) * GRP],
                             start=True, stop=True)
                    p.matmul(psG[i % 2][0:w, :], w13[u][:, 1, f0:f0 + w], x[:, k * GRP:(k + 1) * GRP],
                             start=True, stop=True).then_inc(s["hidden_ready"], 1)

                def output(n, u, k):
                    p.wait_ge(s["mid_ready"], n * CPS + (k + 1) * NFB + SL)
                    p.wait_ge(s["acc_done"], n * NG + k + 1)
                    for t in range(TPG):
                        for f, (_, w) in enumerate(FB):
                            ins = p.matmul(psO[k % 2][:, t * E:(t + 1) * E], mid[k % 2][0:w, f, t * P:(t + 1) * P],
                                           w2[u][0:w, f, :], start=(f == 0), stop=(f == NFB - 1))
                    ins.then_inc(s["out_ready"], 1)

                def step(n, u, x, loads):
                    p.wait_ge(s[f"weights{u}_in"], loads * 32)
                    for k in range(NG):
                        for f in range(NFB):
                            hidden(n, u, x, k, f)
                            if f == 1 and k:
                                output(n, u, k - 1)
                            if f == 1 and not k and not isinstance(n, int):
                                output(n - 1, 1 - u, NG - 1)

                step(0, 1, xnT, 1)
                for k in range(NG):
                    turn(xg, k, "xg_ready", (s["xgT_ready"], k - 1) if k >= 2 else (s["xnT_ready"], NG))
                p.wait_ge(s["xgT_ready"], NG)
                with p.Fori(0, EXPERTS // 2) as i:
                    for u in range(2):
                        step(2 * i + u + 1, u, xgT, i + 1 + u)
                output(EXPERTS, 1, NG - 1)


def layout_b(i, a):
    w1 = np.concatenate([i["L0_ffn_ws1_DF"][None], i["L0_ffn_w1_eDF"]])
    w3 = np.concatenate([i["L0_ffn_ws3_DF"][None], i["L0_ffn_w3_eDF"]])
    a["b_w13"] = np.ascontiguousarray(np.stack([w1, w3], axis=2))
    w2 = np.zeros((EXPERTS + 1, NFB * P, E), np.float32)
    w2[:, :HID_B] = np.concatenate([i["L0_ffn_ws2_FD"][None], i["L0_ffn_w2_eFD"]])
    a["b_w2"] = np.ascontiguousarray(w2.reshape(EXPERTS + 1, NFB, P, E).transpose(0, 2, 1, 3))
    a["b_router"] = np.ascontiguousarray(i["L0_ffn_router_DE"])
    a["b_rank"] = np.ascontiguousarray(np.broadcast_to(np.arange(EXPERTS, 0, -1, dtype=np.float32), (P, EXPERTS)))


STATES, TAPS, RANK = 16, 4, 8
DT = 2
INNER_C = DT * P
BC = 2 * STATES
HALF = NTOK // 2
HSEQ = SEQS // 2
BANKS = HALF // GRP


def stage_c(nc, d, x_tok, ident, minus_half):
    with ExitStack() as ctx:
        def sb(name, shape, dt=F32):
            return ctx.enter_context(nc.sbuf_tensor("c_" + name, shape, dt))

        s_tok = sb("s_tok", [P, T, E])
        n_tok = sb("n_tok", [P, T, E])
        nT = sb("nT", [P, SEQS, TAPS - 1 + L])
        w_in = sb("w_in", [P, 2, INNER_C])
        taps = sb("taps", [P, TAPS, INNER_C])
        w_tap = sb("w_tap", [P, TAPS, INNER_C])
        w_x = sb("w_x", [P, DT, BC + RANK])
        w_dt = sb("w_dt", [BC + RANK, INNER_C])
        w_out = sb("w_out", [P, DT, E])
        a_log = sb("a_log", [P, DT, STATES])
        a_neg = sb("a_neg", [P, DT, STATES])
        cols = sb("cols", [P, 9])
        eye3 = sb("eye3", [3 * BC, BC])
        sel = sb("sel", [3 * BC, BC, P], BF16)
        diag = sb("diag", [P, DT, P])
        u = sb("u", [P, DT, NTOK])
        zs = sb("zs", [P, DT, NTOK])
        dt = sb("dt", [P, DT, NTOK])
        du = sb("du", [P, DT, NTOK])
        bc_parts = sb("bc_parts", [3 * BC, NTOK], BF16)
        rest = [sb(f"rest{k}", [BC, GRP]) for k in range(2)]
        low = sb("low", [BC + RANK, NTOK])
        v_ln = [sb(f"v_ln{k}", [P, GRP]) for k in range(2)]
        b_row = [sb(f"b_row{k}", [P, GRP]) for k in range(BANKS)]
        decay = [sb(f"decay{t}", [P, HSEQ, L]) for t in range(DT)]
        n_flat = n_tok[:].rearrange("p t e -> p (t e)")
        drive = [[sb(f"drive{t}", [P, HALF])[:] for t in range(DT)],
                 [n_flat[:, t * HALF:(t + 1) * HALF] for t in range(DT)]]
        state = [sb(f"state{t}", [P, HALF]) for t in range(DT)]
        yc = [sb(f"yc{t}", [P, HALF]) for t in range(DT)]
        yz = [sb(f"yz{t}", [P, HALF]) for t in range(DT)]
        v_err = [b[:, k * GRP:(k + 1) * GRP] for b in (*state, *yc) for k in range(BANKS)]
        mb = [moment_buffers(sb, f"m{k}", T // 2) for k in range(2)]
        bank = [ctx.enter_context(nc.psum_tensor(f"c_bank{k}", [P, GRP], F32)) for k in range(2)]
        psB = ctx.enter_context(nc.psum_tensor("c_psB", [P, HALF], F32))
        psY = [ctx.enter_context(nc.psum_tensor(f"c_psY{t}", [P, HALF], F32)) for t in range(DT)]
        psC_lo, psC_hi = bank

        names = ("const_in", "chain", "var_ready", "rstd_ready", "s_ready", "n_ready", "turned",
                 "nT_ready", "prep", "tap_ready", "proj_ready", "u_ready", "xdbl_ready", "bc_ready",
                 "low_ready", "dtlin_ready", "v_ready", "exp_ready", "ln_ready", "dt_ready", "du_ready", "a_ready",
                 "b_ready", "c_ready", "drive_ready", "decay_ready", "state_ready", "yc_ready",
                 "y_ready", "yz_ready", "out_ready", "sum_ready", "x_ready", "err_ready", "b_copied", "act_order",
                 "pe_order", "nT_zero", "decay_zero")
        s = {n: ctx.enter_context(nc.semaphore("c_" + n)) for n in names}
        H2 = T // 2

        with nc.Block() as block:
            @block.sync
            def _(sp):
                for dst, name in ((w_in, "c_w_in"), (taps, "c_taps"), (w_x, "c_w_x"), (w_out, "c_w_out"),
                                  (a_log, "c_a_log"), (cols, "c_cols"), (eye3, "c_eye3")):
                    sp.dma_start(dst[:], d[name]).then_inc(s["const_in"], 16)
                sp.dma_start(w_dt[BC:BC + RANK, :], d["c_w_dt"]).then_inc(s["const_in"], 16)

            @block.gpsimd
            def _(g):
                g.sem_inc(s["drive_ready"], BANKS * DT)
                g.memset(nT[:, :, 0:TAPS - 1], 0.0).then_inc(s["nT_zero"], 1)
                for t in range(DT):
                    g.memset(decay[t][:, :, 0:1], 0.0).then_inc(s["decay_zero"], 1)
                for k in range(4):
                    b = mb[k % 2]
                    g.wait_ge(s["var_ready"], k + 1)
                    g.tensor_tensor(b["rstd"][:], b["var"][:], minus_half[:, 0:H2], ALU.pow)\
                        .then_inc(s["rstd_ready"], 1)
                g.wait_ge(s["s_ready"], 2)
                g.wait_ge(s["n_ready"], NG)
                g.tensor_tensor(x_tok[:], x_tok[:], s_tok[:], ALU.add).then_inc(s["sum_ready"], 1)
                for k in range(NG):
                    for t in range(DT):
                        g.wait_ge(s["dt_ready"], k * DT + t + 1)
                        cs = slice(k * GRP, (k + 1) * GRP)
                        g.tensor_tensor(du[:, t, cs], dt[:, t, cs], u[:, t, cs], ALU.mult).then_inc(s["du_ready"], 1)
                g.wait_ge(s["du_ready"], NG * DT)
                for h in range(2):
                    with g.Fori(0, STATES // 2) as pair:
                        for odd in range(2):
                            n = pair * 2 + odd + h * STATES
                            for b in range(BANKS):
                                g.wait_ge(s["b_copied"], n * BANKS + b + 1)
                                for t in range(DT):
                                    if b == 0:
                                        g.wait_ge(s["state_ready"], n * DT + t + 1)
                                    at = h * HALF + b * GRP
                                    g.tensor_tensor(drive[odd][t][:, b * GRP:(b + 1) * GRP],
                                                    du[:, t, at:at + GRP], b_row[b][:], ALU.mult)\
                                        .then_inc(s["drive_ready"], 1)

            @block.scalar
            def _(a):
                a.wait_ge(s["const_in"], 128)
                for k in range(NG):
                    a.wait_ge(s["turned"], k + 1)
                    a.activation(nT[:, 2 * k:2 * k + 2, TAPS - 1:], bank[k % 2][:].rearrange("p (q t) -> p q t", q=2),
                                 ACT.Identity, bias=cols[:, 1:2], scale=cols[:, 0:1]).then_inc(s["nT_ready"], 1)
                for k in range(NG):
                    for c in range(2 * DT):
                        i = k * 2 * DT + c
                        a.wait_ge(s["proj_ready"], i + 1)
                        dst = (u if c < DT else zs)[:, c % DT, k * GRP:(k + 1) * GRP]
                        if c < DT:
                            a.activation(dst, bank[i % 2][:], ACT.Silu, bias=cols[:, 2 + c:3 + c])\
                                .then_inc(s["u_ready"], 1)
                        else:
                            a.activation(dst, bank[i % 2][:], ACT.Silu).then_inc(s["u_ready"], 1)
                pieces = [(t, slice(k * GRP, (k + 1) * GRP)) for k in range(NG) for t in range(DT)]
                for i, (t, cs) in enumerate(pieces):
                    a.wait_ge(s["dtlin_ready"], i + 1)
                    a.activation(dt[:, t, cs], psB[:, (i % 2) * GRP:(i % 2 + 1) * GRP], ACT.Identity,
                                 bias=cols[:, 4 + t:5 + t]).then_inc(s["v_ready"], 1)
                    a.wait_ge(s["v_ready"], 2 * i + 1)
                    a.activation(du[:, t, cs], dt[:, t, cs], ACT.Abs).then_inc(s["v_ready"], 1)
                    a.wait_ge(s["v_ready"], 2 * i + 2)
                    a.activation(du[:, t, cs], du[:, t, cs], ACT.Exp, scale=-1.0).then_inc(s["exp_ready"], 1)
                for i, (t, cs) in enumerate(pieces):
                    a.wait_ge(s["exp_ready"], i + 1)
                    if i >= 2:
                        a.wait_ge(s["dt_ready"], i - 1)
                    a.activation(v_ln[i % 2][:], du[:, t, cs], ACT.Ln, bias=1.0).then_inc(s["ln_ready"], 1)
                a.wait_ge(s["dt_ready"], NG * DT)
                a.activation(a_neg[:], a_log[:], ACT.Exp).then_inc(s["a_ready"], 1)
                a.wait_ge(s["a_ready"], 2)
                a.wait_ge(s["decay_zero"], DT)

                def copy_b(n, b):
                    a.wait_ge(s["b_ready"], n + 1)
                    a.wait_ge(s["drive_ready"], n * BANKS * DT + (b + 1) * DT)
                    a.activation(b_row[b][:], psB[:, b * GRP:(b + 1) * GRP], ACT.Copy).then_inc(s["b_copied"], 1)

                def decays(h, i, t):
                    a.wait_ge(s["state_ready"], (i + h * STATES + 1) * DT + t + 1)
                    a.sem_inc(s["act_order"], 1)
                    a.activation(decay[t][:, :, 1:],
                                 dt[:, t, h * HALF:(h + 1) * HALF].rearrange("p (q l) -> p q l", l=L)[:, :, 1:],
                                 ACT.Exp, scale=a_neg[:, t, bass.ds(i, 1)]).then_inc(s["decay_ready"], 1)

                for h in range(2):
                    for b in range(BANKS):
                        copy_b(h * STATES, b)
                    with a.Fori(0, STATES - 1) as i:
                        for k in range(2):
                            copy_b(i + h * STATES + 1, k)
                            decays(h, i, k)
                    for t in range(DT):
                        decays(h, STATES - 1, t)

            @block.vector
            def _(v):
                v.sem_inc(s["state_ready"], 2 * DT)
                v.sem_inc(s["yc_ready"], DT)
                chain = Chain(v, s["chain"])

                def norm(src, dst, first, signal):
                    for k in range(2):
                        for t in range(H2):
                            ins = v.bn_stats(mb[k]["st"][:, t, :], src[:, k * H2 + t, :])
                        chain.link(ins)
                        moments(v, chain, mb[k], H2).then_inc(s["var_ready"], 1)
                    for k in range(2):
                        v.wait_ge(s["rstd_ready"], first + k + 1)
                        for t in range(H2):
                            ins = v.tensor_scalar(dst[:, k * H2 + t, :], src[:, k * H2 + t, :],
                                                  mb[k]["mean"][:, t:t + 1], mb[k]["rstd"][:, t:t + 1],
                                                  ALU.subtract, ALU.mult)
                            signal(ins, k, t)

                norm(x_tok, s_tok, 0, lambda ins, k, t: ins.then_inc(s["s_ready"], 1) if t == H2 - 1 else None)
                v.wait_ge(s["s_ready"], 2)
                norm(s_tok, n_tok, 2, lambda ins, k, t: ins.then_inc(s["n_ready"], 1) if t % TPG == TPG - 1 else None)
                v.wait_ge(s["const_in"], 128)
                for k in range(TAPS):
                    ins = v.tensor_tensor(w_tap[:, k, :], w_in[:, 0, :], taps[:, k, :], ALU.mult)
                ins.then_inc(s["tap_ready"], 1)
                v.tensor_copy(sel[:], eye3[:].unsqueeze(2).broadcast_to([3 * BC, BC, P])).then_inc(s["prep"], 1)
                for t in range(DT):
                    v.tensor_scalar(diag[:, t, :], ident[:], cols[:, 6 + t:7 + t], None, ALU.mult)\
                        .then_inc(s["prep"], 1)
                for k in range(NG):
                    v.wait_ge(s["xdbl_ready"], k + 1)
                    src = psY[0][0:BC, (k % 2) * GRP:(k % 2 + 1) * GRP]
                    cs = slice(k * GRP, (k + 1) * GRP)
                    v.tensor_copy(low[BC:BC + RANK, cs], psY[0][BC:BC + RANK, (k % 2) * GRP:(k % 2 + 1) * GRP])\
                        .then_inc(s["low_ready"], 1)
                    chain.link(v.tensor_copy(bc_parts[0:BC, cs], src))
                    chain.link(v.tensor_tensor(rest[0][:], src, bc_parts[0:BC, cs], ALU.subtract))
                    chain.link(v.tensor_copy(bc_parts[BC:2 * BC, cs], rest[0][:]))
                    chain.link(v.tensor_copy(rest[1][:], bc_parts[BC:2 * BC, cs]))
                    chain.link(v.tensor_tensor(rest[0][:], rest[0][:], rest[1][:], ALU.subtract))
                    chain.link(v.tensor_copy(bc_parts[2 * BC:3 * BC, cs], rest[0][:]))
                    v.sem_inc(s["bc_ready"], 1)
                v.wait_ge(s["u_ready"], NG * 2 * DT)
                pieces = [(t, slice(k * GRP, (k + 1) * GRP)) for k in range(NG) for t in range(DT)]
                for i, (t, cs) in enumerate(pieces):
                    v.wait_ge(s["exp_ready"], i + 1)
                    v.tensor_scalar(v_err[i], du[:, t, cs], 1.0, -1.0, ALU.add, ALU.add)\
                        .then_inc(s["err_ready"], 1)
                    v.wait_ge(s["err_ready"], 2 * i + 1)
                    v.tensor_tensor(v_err[i], du[:, t, cs], v_err[i], ALU.subtract).then_inc(s["err_ready"], 1)
                for i, (t, cs) in enumerate(pieces):
                    v.wait_ge(s["ln_ready"], i + 1)
                    v.wait_ge(s["err_ready"], 2 * NG * DT + i)
                    v.tensor_tensor(v_err[i], v_err[i], v_ln[i % 2][:], ALU.add).then_inc(s["err_ready"], 1)
                    v.wait_ge(s["err_ready"], 2 * NG * DT + i + 1)
                    v.scalar_tensor_tensor(dt[:, t, cs], dt[:, t, cs], 0.0, v_err[i], ALU.max, ALU.add)\
                        .then_inc(s["dt_ready"], 1)
                v.wait_ge(s["a_ready"], 1)
                v.tensor_scalar(a_neg[:], a_neg[:], -1.0, None, ALU.mult).then_inc(s["a_ready"], 1)
                for h in range(2):
                    hs = slice(h * HALF, (h + 1) * HALF)
                    with v.Fori(0, STATES // 2) as pair:
                        for odd in range(2):
                            n = pair * 2 + odd + h * STATES
                            for t in range(DT):
                                v.wait_ge(s["drive_ready"], (n + 1) * BANKS * DT + (BANKS - 1) * DT + t + 1)
                                v.wait_ge(s["decay_ready"], n * DT + t + 1)
                                v.wait_ge(s["yc_ready"], n * DT + t + 1)
                                v.tensor_tensor_scan(state[t][:], decay[t][:].rearrange("p q l -> p (q l)"),
                                                     drive[odd][t], 0.0, ALU.mult, ALU.add)\
                                    .then_inc(s["state_ready"], 1)
                            v.wait_ge(s["c_ready"], n + 1)
                            for t in range(DT):
                                v.wait_ge(s["state_ready"], (n + 2) * DT + t + 1)
                                v.wait_ge(s["y_ready"], n * DT + t + 1)
                                for b in range(BANKS):
                                    bs = slice(b * GRP, (b + 1) * GRP)
                                    ins = v.tensor_tensor(yc[t][:, bs], state[t][:, bs], bank[b][:], ALU.mult)
                                ins.then_inc(s["yc_ready"], 1)
                    for t in range(DT):
                        v.wait_ge(s["y_ready"], (h + 1) * STATES * DT + t + 1)
                        if h:
                            v.wait_ge(s["out_ready"], 2)
                        v.tensor_tensor(yz[t][:], psY[t][:], zs[:, t, hs], ALU.mult).then_inc(s["yz_ready"], 1)
                    v.wait_ge(s["sum_ready"], 1)
                    for k in range(BANKS):
                        v.wait_ge(s["out_ready"], h * BANKS + k + 1)
                        xs = x_tok[:, (h * BANKS + k) * TPG:(h * BANKS + k + 1) * TPG, :]\
                            .rearrange("p t e -> p (t e)")
                        v.scalar_tensor_tensor(xs, psB[:, k * GRP:(k + 1) * GRP], cols[:, 8:9], xs,
                                               ALU.mult, ALU.add).then_inc(s["x_ready"], 1)
                v.wait_ge(s["x_ready"], NG)

            @block.tensor
            def _(p):
                for k in range(NG):
                    p.wait_ge(s["n_ready"], k + 1)
                    if k >= 2:
                        p.wait_ge(s["nT_ready"], k - 1)
                    for t in range(TPG):
                        ins = p.transpose(bank[k % 2][:, t * P:(t + 1) * P], n_tok[:, k * TPG + t, :], ident[:])
                    ins.then_inc(s["turned"], 1)
                p.wait_ge(s["tap_ready"], 1)
                p.wait_ge(s["nT_zero"], 1)
                p.wait_ge(s["nT_ready"], NG)

                def project(k):
                    for c in range(2 * DT):
                        i = k * 2 * DT + c
                        if i >= 2:
                            p.wait_ge(s["u_ready"], i - 1)
                        cs = slice((c % DT) * P, (c % DT + 1) * P)
                        if c < DT:
                            for j in range(TAPS):
                                ins = p.matmul(bank[i % 2][:], w_tap[:, j, cs], nT[:, 2 * k:2 * k + 2, j:j + L],
                                               start=(j == 0), stop=(j == TAPS - 1))
                        else:
                            ins = p.matmul(bank[i % 2][:], w_in[:, 1, cs], nT[:, 2 * k:2 * k + 2, TAPS - 1:],
                                           start=True, stop=True)
                        ins.then_inc(s["proj_ready"], 1)

                def x_dbl(k):
                    if k >= 2:
                        p.wait_ge(s["bc_ready"], k - 1)
                    p.wait_ge(s["u_ready"], (k + 1) * 2 * DT)
                    for t in range(DT):
                        ins = p.matmul(psY[0][0:BC + RANK, (k % 2) * GRP:(k % 2 + 1) * GRP], w_x[:, t, :],
                                       u[:, t, k * GRP:(k + 1) * GRP], start=(t == 0), stop=(t == DT - 1))
                    ins.then_inc(s["xdbl_ready"], 1)

                project(0)
                for k in range(1, NG):
                    project(k)
                    x_dbl(k - 1)
                x_dbl(NG - 1)
                for k in range(NG):
                    for t in range(DT):
                        i = k * DT + t
                        p.wait_ge(s["low_ready"], k + 1)
                        if i >= 2:
                            p.wait_ge(s["v_ready"], 2 * (i - 2) + 1)
                        p.matmul(psB[:, (i % 2) * GRP:(i % 2 + 1) * GRP], w_dt[BC:BC + RANK, t * P:(t + 1) * P],
                                 low[BC:BC + RANK, k * GRP:(k + 1) * GRP], start=True, stop=True)\
                            .then_inc(s["dtlin_ready"], 1)
                p.wait_ge(s["prep"], 1 + DT)
                p.wait_ge(s["bc_ready"], NG)
                p.wait_ge(s["v_ready"], 2 * NG * DT)

                def spread(h, row, dst, done):
                    for b in range(BANKS):
                        cs = slice((h * BANKS + b) * GRP, (h * BANKS + b + 1) * GRP)
                        ins = p.matmul(dst[b], row, bc_parts[:, cs], start=True, stop=True)
                    ins.then_inc(done, 1)

                def add_y(t):
                    for b in range(BANKS):
                        bs = slice(b * GRP, (b + 1) * GRP)
                        ins = p.matmul(psY[t][:, bs], ident[:], yc[t][:, bs], start=False, stop=True,
                                       skip_group_check=True)
                    ins.then_inc(s["y_ready"], 1)

                b_dst = [psB[:, b * GRP:(b + 1) * GRP] for b in range(BANKS)]
                c_dst = [bank[b][:] for b in range(BANKS)]
                for h in range(2):
                    if h:
                        p.wait_ge(s["x_ready"], BANKS)
                    spread(h, sel[:, 0, :], b_dst, s["b_ready"])
                    spread(h, sel[:, STATES, :], c_dst, s["c_ready"])
                    for t in range(DT):
                        if h:
                            p.wait_ge(s["yz_ready"], t + 1)
                        for b in range(BANKS):
                            bs = slice(b * GRP, (b + 1) * GRP)
                            ins = p.matmul(psY[t][:, bs], diag[:, t, :],
                                           u[:, t, h * HALF + b * GRP:h * HALF + (b + 1) * GRP],
                                           start=True, stop=True)
                        if not h:
                            ins.then_inc(s["y_ready"], 1)
                    p.wait_ge(s["b_copied"], (h * STATES + 1) * BANKS)
                    spread(h, sel[:, 1, :], b_dst, s["b_ready"])

                    def add_state(n, c_row):
                        p.wait_ge(s["yc_ready"], (n + 1) * DT + 1)
                        add_y(0)
                        p.wait_ge(s["yc_ready"], (n + 2) * DT)
                        p.sem_inc(s["pe_order"], 1)
                        spread(h, c_row, c_dst, s["c_ready"])
                        add_y(1)

                    with p.Fori(0, STATES - 2) as i:
                        n = i + h * STATES
                        p.wait_ge(s["b_copied"], (n + 2) * BANKS)
                        p.sem_inc(s["pe_order"], 1)
                        spread(h, sel[:, bass.ds(i + 2, 1), :].rearrange("k r m -> k (r m)"), b_dst, s["b_ready"])
                        add_state(n, sel[:, bass.ds(i + 1 + STATES, 1), :].rearrange("k r m -> k (r m)"))
                    add_state((h + 1) * STATES - 2, sel[:, 2 * STATES - 1, :])
                    for t in range(DT):
                        p.wait_ge(s["yc_ready"], (h + 1) * STATES * DT + t + 1)
                        add_y(t)
                    p.wait_ge(s["yz_ready"], (h + 1) * DT)
                    for k in range(BANKS):
                        for t in range(TPG):
                            for c in range(DT):
                                q = k * TPG + t
                                ins = p.matmul(psB[:, q * P:(q + 1) * P], yz[c][:, q * P:(q + 1) * P], w_out[:, c, :],
                                               start=(c == 0), stop=(c == DT - 1))
                        ins.then_inc(s["out_ready"], 1)


def layout_c(i, a):
    w = i["L1_attn_in_proj_w"]
    a["c_w_in"] = np.ascontiguousarray(w.T.reshape(E, 2, INNER_C))
    a["c_taps"] = np.ascontiguousarray(np.broadcast_to(i["L1_attn_conv_w"].T, (P, TAPS, INNER_C)))
    xp = i["L1_attn_x_proj_w"]
    xp = np.concatenate([xp[RANK:], xp[:RANK]])
    a["c_w_x"] = np.ascontiguousarray(xp.T.reshape(DT, P, BC + RANK).transpose(1, 0, 2))
    a["c_w_dt"] = np.ascontiguousarray(i["L1_attn_dt_proj_w"].T)
    a["c_w_out"] = np.ascontiguousarray(i["L1_attn_out_proj_w"].T.reshape(DT, P, E).transpose(1, 0, 2))
    a["c_a_log"] = np.ascontiguousarray(i["L1_attn_A_log"].reshape(DT, P, STATES).transpose(1, 0, 2))
    col = [i["L1_attn_ln_g"][:, None], i["L1_attn_ln_b"][:, None]]
    col += [i["L1_attn_" + n].reshape(DT, P).T for n in ("conv_b", "dt_proj_b", "D")]
    col += [np.broadcast_to(i["L1_attn_res_scale"], (P, 1))]
    a["c_cols"] = np.ascontiguousarray(np.concatenate(col, axis=1))
    a["c_eye3"] = np.ascontiguousarray(np.tile(np.eye(BC, dtype=np.float32), (3, 1)))


DEPTH, HEADS_D, DHD, WINDOW = 2, 8, 64, 64
INNER_D = HEADS_D * DHD
HID_D = E * 4 * 2 // 3
CD = INNER_D // P
FD = [(f, min(P, HID_D - f)) for f in range(0, HID_D, P)]
NFD = len(FD)
QK_SCALE = 8.0
NORM_MIN = 1e-12
MASKED = -1e25
D_LG, D_LB, D_BA, D_BG, D_NCOL = 0, 1, 2, 2 + NFD, 2 + 2 * NFD


def schedule_d():
    slots = {}

    def place(slot, *items):
        slots.setdefault(slot, []).extend(items)

    for q in range(SEQS):
        at = 8 * q
        for g in range(8):
            place(at + g, ("score", q, g))
            place(at + g + 1, ("exp", q, g))
            place(at + g + 2, ("turn_p", q, g))
            place(at + g + 3, ("pv", q, g))
    for q in range(SEQS):
        at = 8 * q
        for t in range(TPS):
            last = at + 4 * t + 3
            place(last + 3, ("norm_o", q, t))
            place(last + 4, ("turn_o", q, t))
            place(last + 5, ("out_o", q, t))
        place(at + 15, ("shift", q), ("rstd_f", q))
        place(at + 16, ("norm_f", q))
        place(at + 17, ("turn_f", q))
        place(at + 22, *[("hidden", q, f) for f in range(NFD - 1)])
        place(at + 24, ("hidden", q, NFD - 1))
        place(at + 25, ("out_f", q))
    for q in range(SEQS):
        at = 8 * (q - 1)
        place(at, ("turn_h", q))
        for t in range(TPS):
            for part in range(3):
                place(at + 1 + 3 * t + part, ("project", q, t, part))
            for part in range(2):
                place(at + 3 + 3 * t + 2 * part, ("turn_qk", q, t, part))
    rank = ('score', 'exp', 'turn_p', 'pv')
    order = []
    for n in sorted(slots):
        order += sorted(slots[n], key=lambda i: rank.index(i[0]) if i[0] in rank else len(rank))
    return order


def stage_d(nc, d, x_tok, ident, minus_half):
    with ExitStack() as ctx:
        def sb(name, shape, dt=F32):
            return ctx.enter_context(nc.sbuf_tensor("d_" + name, shape, dt))

        y_tok = sb("y_tok", [P, T, E])
        wqkv = sb("wqkv", [P, 3, INNER_D])
        wo = sb("wo", [P, CD, E])
        w1 = sb("w1", [P, 2, HID_D])
        w2 = sb("w2", [P, NFD, E])
        cols = sb("cols", [P, D_NCOL])
        b2row = sb("b2row", [1, E])
        ones_row = sb("ones_row", [1, P])
        gains = sb("gains", [P, 4, DHD])
        tables = sb("tables", [P, 4, TPS, DHD])
        rot = sb("rot", [P, 4, TPS, DHD])
        maskf = sb("maskf", [P, L + P])
        mask = sb("mask", [P, L + P], BF16)
        identb = sb("identb", [P, P], BF16)
        down = sb("down", [P, 2, P])
        hT = [sb(f"hT{u}", [P, L + 1]) for u in range(2)]
        sq = [sb(f"sq{u}", [P, INNER_D]) for u in range(2)]
        direct = [sb(f"direct{u}", [P, INNER_D]) for u in range(2)]
        cross = [sb(f"cross{u}", [P, INNER_D]) for u in range(2)]
        qk = [sb(f"qk{u}", [P, INNER_D]) for u in range(2)]
        ss = [sb(f"ss{u}", [P, 2, HEADS_D]) for u in range(2)]
        inv = [[sb(f"inv{u}{t}", [P, 2, HEADS_D]) for t in range(TPS)] for u in range(2)]
        val = [sb(f"val{u}", [P, TPS, INNER_D]) for u in range(2)]
        qkT = [sb(f"qkT{u}", [P, 2, CD, L]) for u in range(2)]
        negmax = [sb(f"negmax{u}", [P, 2]) for u in range(2)]
        bias = [sb(f"bias{u}", [P, 2]) for u in range(2)]
        prob = [[sb(f"prob{t}{u}", [P, 2, (t + 1) * P]) for u in range(2)] for t in range(TPS)]
        probT = [sb(f"probT{u}", [P, 2, 2, P]) for u in range(2)]
        rowsum = [sb(f"rowsum{t}", [P, HEADS_D]) for t in range(TPS)]
        rowinv = [sb(f"rowinv{t}", [P, HEADS_D]) for t in range(TPS)]
        o_n = sb("o_n", [P, INNER_D])
        oT = sb("oT", [P, CD, P])
        hs = sb("hs", [P, TPS, E])
        hn = sb("hn", [P, TPS, E])
        fT = sb("fT", [P, L])
        gel = [sb(f"gel{u}", [P, L]) for u in range(2)]
        mid = sb("mid", [P, NFD, L])
        mb = [moment_buffers(sb, f"m{k}", T // 2) for k in range(2)]
        psQ = [ctx.enter_context(nc.psum_tensor(f"d_psQ{k}", [P, GRP], F32)) for k in range(2)]
        psS = [ctx.enter_context(nc.psum_tensor(f"d_psS{k}", [P, 2, L], F32)) for k in range(2)]
        psT = [ctx.enter_context(nc.psum_tensor(f"d_psT{k}", [P, GRP], F32)) for k in range(2)]
        psO = ctx.enter_context(nc.psum_tensor("d_psO", [P, GRP], F32))
        psW = ctx.enter_context(nc.psum_tensor("d_psW", [P, GRP], F32))

        names = ("const_in", "weights_in", "chain", "var_ready", "rstd_ready", "y_ready", "set_up",
                 "rot_ready", "q_full", "q_free", "s_full", "s_free", "t_full", "t_free", "w_full", "w_free",
                 "o_full", "o_free", "square_ready", "rope_ready", "ss_ready", "inv_ready", "qk_ready", "pool_step",
                 "max_step", "bias_ready", "prob_ready", "rowinv_ready", "hn_ready",
                 "gelu_ready", "mid_ready", "x_ready", "shift_half", "reduce_done")
        s = {n: ctx.enter_context(nc.semaphore("d_" + n)) for n in names}
        H2 = T // 2
        items = schedule_d()

        def order(*kinds):
            found = [i for i in items if i[0] in kinds]
            return {i: n for n, i in enumerate(found)}, len(found)

        Q, NQ = order("project", "hidden")
        S, NS = order("score")
        TT = [("turn_h",), ("turn_qk",), ("turn_p",), ("turn_o",), ("turn_f",)]
        TI, NT = order(*[k for (k,) in TT])
        W, NW = order("out_o", "shift", "out_f")
        O, NO = order("norm_o")
        PR, NPR = {}, 0
        for i in items:
            if i[0] == "project" and i[3] < 2:
                PR[i] = NPR
                NPR += 1
        F, NF = order("hidden")
        SH, NSH = order("shift")
        SL = 2

        def keys(t):
            return (0, P) if t == 0 else (WINDOW, L)

        def heads(g):
            t, r = divmod(g, 4)
            cp, a = divmod(r, 2)
            return t, a, [(2 * cp + j, 2 * (2 * cp + j) + a) for j in range(2)]

        mh16 = minus_half[:, 0:2 * HEADS_D].rearrange("p (k h) -> p k h", k=2)

        def turned(n, l):
            ks = sorted(PR, key=PR.get)
            if n >= 2:
                _, q, t, part = ks[n - 2]
                return l * NT + TI[("turn_qk", q, t, part)] + 1 + SL
            return l * NT + SL

        def prev(q, g):
            t, r = divmod(g, 4)
            if r >= 2:
                return q, g - 2
            return (q - 1, 4 * t + r + 2) if q else None

        CHAIN_D = SEQS * 8

        def last_turn_o(it):
            n = O[it]
            before = [i for i in O if O[i] == n - 1]
            return TI[("turn_o",) + before[0][1:]] + 1 if before else 0

        with nc.Block() as block:
            @block.sync
            def _(sp):
                for dst, name in ((tables, "d_tables"), (maskf, "d_mask"), (down, "d_down")):
                    sp.dma_start(dst[:], d[name]).then_inc(s["const_in"], 16)

                def load(l):
                    for dst, name in ((wqkv, "d_wqkv"), (wo, "d_wo"), (w1, "d_w1"), (w2, "d_w2"), (cols, "d_cols"),
                                      (gains, "d_gains"), (b2row, "d_b2")):
                        sp.dma_start(dst[:], d[name][l]).then_inc(s["weights_in"], 16)

                load(0)
                for l in range(1, DEPTH):
                    sp.wait_ge(s["w_free"], l * NW + 1)
                    load(l)

            @block.gpsimd
            def _(g):
                g.sem_inc(s["qk_ready"], SL)
                g.memset(ones_row[:], 1.0).then_inc(s["set_up"], 1)
                for u in range(2):
                    g.wait_ge(s["set_up"], 2 * u + 1)
                    g.memset(hT[u][P // 2:P, 0:1], 0.0).then_inc(s["set_up"], 1)
                    g.wait_ge(s["set_up"], 2 * u + 2)
                    g.memset(prob[1][u][:, :, 0:WINDOW], 0.0).then_inc(s["set_up"], 1)
                for k in range(2):
                    g.wait_ge(s["var_ready"], k + 1)
                    g.tensor_tensor(mb[k]["rstd"][:], mb[k]["var"][:], minus_half[:, 0:H2], ALU.pow)\
                        .then_inc(s["rstd_ready"], 1)
                g.wait_ge(s["set_up"], 5)
                g.wait_ge(s["const_in"], 48)
                with g.Fori(0, DEPTH) as l:
                    g.wait_ge(s["weights_in"], (l + 1) * 7 * 16)
                    for k in range(4):
                        g.tensor_tensor(rot[:, k], tables[:, k], gains[:, k:k + 1, :].broadcast_to([P, TPS, DHD]),
                                        ALU.mult).then_inc(s["rot_ready"], 1)
                    steps = [0]

                    def step(ins):
                        steps[0] += 1
                        ins.then_inc(s["pool_step"], 1)
                        return l * STEPS + steps[0]

                    STEPS = NPR
                    for it in items:
                        if it[0] == "project" and it[3] < 2:
                            _, q, t, part = it
                            n = PR[it]
                            b = n % 2
                            g.wait_ge(s["rope_ready"], l * NPR + n + 1)
                            if part == 0:
                                g.wait_ge(s["t_full"], turned(n, l))
                                g.tensor_tensor(qk[b][:], direct[b][:], cross[b][:], ALU.add)\
                                    .then_inc(s["qk_ready"], 1)
                            else:
                                at = step(g.tensor_tensor(direct[b][:], direct[b][:], cross[b][:], ALU.add))
                                g.wait_ge(s["ss_ready"], l * (NPR // 2) + n // 2 + 1)
                                at = step(g.tensor_tensor(inv[q % 2][t][:], ss[t][:], mh16, ALU.pow))
                                g.wait_ge(s["pool_step"], at)
                                g.sem_inc(s["inv_ready"], 1)
                                g.wait_ge(s["t_full"], turned(n, l))
                                g.tensor_tensor(qk[b][:].rearrange("p (h e) -> p h e", e=DHD),
                                                direct[b][:].rearrange("p (h e) -> p h e", e=DHD),
                                                inv[q % 2][t][:, 1, :].unsqueeze(2)
                                                .broadcast_to([P, HEADS_D, DHD]), ALU.mult)\
                                    .then_inc(s["qk_ready"], 1)
                        elif it[0] == "rstd_f":
                            n = it[1]
                            g.wait_ge(s["var_ready"], l * SEQS + n + 1 + 2)
                            g.tensor_tensor(mb[0]["rstd"][:, 0:TPS], mb[0]["var"][:, 0:TPS], minus_half[:, 0:TPS],
                                            ALU.pow).then_inc(s["rstd_ready"], 1)

            @block.scalar
            def _(a):
                a.sem_inc(s["t_free"], SL)
                a.sem_inc(s["s_free"], SL)
                a.sem_inc(s["prob_ready"], 1)
                with a.Fori(0, DEPTH) as l:
                    a.wait_ge(s["set_up"], 5)
                    a.wait_ge(s["weights_in"], (l + 1) * 7 * 16)

                    def full(it):
                        n = TI[it]
                        a.wait_ge(s["t_full"], l * NT + n + 1 + SL)
                        return psT[n % 2]

                    def square(it):
                        n, i = PR[it], Q[it]
                        a.wait_ge(s["q_full"], l * NQ + i + 1)
                        a.wait_ge(s["reduce_done"], l * NPR + n - 1 + SL)
                        a.activation(sq[n % 2][:], psQ[i % 2][:], ACT.Square).then_inc(s["square_ready"], 1)

                    def exps(it):
                        _, q, g = it
                        n = S[("score", q, g)]
                        t, _, hh = heads(g)
                        k0, k1 = keys(t)
                        a.wait_ge(s["bias_ready"], l * NS + n + 1)
                        a.wait_ge(s["rowinv_ready"], l * NO + 2 * q + t + 1)
                        a.wait_ge(s["t_full"], l * NT + (TI[("turn_p",) + prev(q, g)] + 1 if prev(q, g) else 0) + SL)
                        for j, (_, h) in enumerate(hh):
                            ins = a.activation(prob[t][g % 2][:, j, k0:k1], psS[n % 2][:, j, k0:k1], ACT.Exp,
                                               bias=bias[n % 2][:, j:j + 1], scale=inv[q % 2][t][:, 0, h:h + 1],
                                               accum_out=rowsum[t][:, h:h + 1])
                        ins.then_inc(s["s_free"], 1)

                    for it in items:
                        kind, q = it[0], it[1]
                        if kind == "turn_h":
                            ps = full(it)
                            a.activation(hT[q % 2][0:P // 2, 0:L], ps[0:P // 2, 0:L], ACT.Copy)\
                                .then_inc(s["shift_half"], 1)
                            a.activation(hT[q % 2][P // 2:P, 1:L + 1], ps[P // 2:P, 0:L], ACT.Copy)\
                                .then_inc(s["t_free"], 1)
                        elif kind == "project" and it[3] < 2:
                            square(it)
                        elif kind == "turn_qk":
                            _, q, t, part = it
                            ps = full(it)
                            a.activation(qkT[q % 2][:, part, :, t * P:(t + 1) * P],
                                         ps[:].rearrange("p (c n) -> p c n", c=CD), ACT.Copy)\
                                .then_inc(s["t_free"], 1)
                        elif kind == "exp":
                            exps(it)
                        elif kind == "turn_p":
                            t = heads(it[2])[0]
                            ps = full(it)
                            a.activation(probT[it[2] % 2][:, :, 0:t + 1, :],
                                         ps[:].rearrange("p (j b n) -> p j b n", j=2, b=2)[:, :, 0:t + 1, :],
                                         ACT.Copy).then_inc(s["t_free"], 1)
                        elif kind == "turn_o":
                            ps = full(it)
                            a.activation(oT[:].rearrange("p c n -> p (c n)"), ps[:], ACT.Copy)\
                                .then_inc(s["t_free"], 1)
                        elif kind == "turn_f":
                            ps = full(it)
                            a.activation(fT[:], ps[:, 0:L], ACT.Identity, bias=cols[:, D_LB:D_LB + 1],
                                         scale=cols[:, D_LG:D_LG + 1]).then_inc(s["t_free"], 1)
                        elif kind == "hidden":
                            f = it[2]
                            w = FD[f][1]
                            a.wait_ge(s["q_full"], l * NQ + Q[it] + 1)
                            a.wait_ge(s["mid_ready"], l * NF + F[it] + 1)
                            a.activation(gel[F[it] % 2][0:w, :], psQ[Q[it] % 2][0:w, L:2 * L], ACT.Gelu,
                                         bias=cols[0:w, D_BG + f:D_BG + f + 1]).then_inc(s["gelu_ready"], 1)

            @block.vector
            def _(v):
                v.sem_inc(s["q_free"], SL)
                v.sem_inc(s["w_free"], 1)
                v.sem_inc(s["o_free"], 1)
                v.sem_inc(s["reduce_done"], SL)
                v.sem_inc(s["rowinv_ready"], SL)
                v.sem_inc(s["mid_ready"], SL)
                chain = Chain(v, s["chain"])
                for k in range(2):
                    for t in range(H2):
                        ins = v.bn_stats(mb[k]["st"][:, t, :], x_tok[:, k * H2 + t, :])
                    chain.link(ins)
                    moments(v, chain, mb[k], H2).then_inc(s["var_ready"], 1)
                for k in range(2):
                    v.wait_ge(s["rstd_ready"], k + 1)
                    for t in range(H2):
                        ins = v.tensor_scalar(y_tok[:, k * H2 + t, :], x_tok[:, k * H2 + t, :],
                                              mb[k]["mean"][:, t:t + 1], mb[k]["rstd"][:, t:t + 1],
                                              ALU.subtract, ALU.mult)
                chain.link(ins)
                v.sem_inc(s["y_ready"], 1)
                v.wait_ge(s["const_in"], 48)
                chain.link(v.tensor_copy(mask[:], maskf[:]))
                chain.link(v.tensor_copy(identb[:], ident[:]))
                v.sem_inc(s["y_ready"], 1)
                first_chain = chain.n
                with v.Fori(0, DEPTH) as l:
                    chain = Chain(v, s["chain"], l * CHAIN_D + first_chain)
                    v.wait_ge(s["rot_ready"], (l + 1) * 4)

                    def heads3(ap):
                        return ap.rearrange("p (h e) -> p h e", e=DHD)

                    for it in items:
                        kind, q = it[0], it[1]
                        if kind == "project":
                            _, q, t, part = it
                            i = Q[it]
                            ps = psQ[i % 2]
                            v.wait_ge(s["q_full"], l * NQ + i + 1)
                            if part == 2:
                                v.tensor_copy(val[q % 2][:, t, :], ps[:]).then_inc(s["q_free"], 1)
                                continue
                            n = PR[it]
                            b = n % 2
                            v.wait_ge(s["square_ready"], l * NPR + n + 1)
                            v.wait_ge(s["qk_ready"], l * NPR + n - 1 + SL)
                            bc = [P, HEADS_D, DHD]
                            v.tensor_tensor(heads3(direct[b][:]), heads3(ps[:]),
                                            rot[:, 2 * part, t:t + 1, :].broadcast_to(bc), ALU.mult)
                            hf = DHD // 2
                            for x0, x1 in ((0, hf), (hf, 0)):
                                ins = v.tensor_tensor(heads3(cross[b][:])[:, :, x0:x0 + hf],
                                                      heads3(ps[:])[:, :, x1:x1 + hf],
                                                      rot[:, 2 * part + 1, t:t + 1, x0:x0 + hf]
                                                      .broadcast_to([P, HEADS_D, hf]), ALU.mult)
                            ins.then_inc(s["rope_ready"], 1)
                            v.tensor_reduce(ss[t][:, part, :], heads3(sq[b][:]), AX.X, ALU.add)\
                                .then_inc(s["reduce_done"], 1)
                            v.wait_ge(s["reduce_done"], l * NPR + n + 1 + SL)
                            v.sem_inc(s["q_free"], 1)
                            if part == 1:
                                v.tensor_scalar(ss[t][:], ss[t][:], NORM_MIN ** 2, None, ALU.max)\
                                    .then_inc(s["ss_ready"], 1)
                                v.wait_ge(s["ss_ready"], l * (NPR // 2) + n // 2 + 1)
                        elif kind == "score":
                            g = it[2]
                            n = S[it]
                            t, _, hh = heads(g)
                            k0, k1 = keys(t)
                            v.wait_ge(s["s_full"], l * NS + n + 1)
                            v.wait_ge(s["s_free"], l * NS + n + 1)
                            v.tensor_reduce(negmax[n % 2][:], psS[n % 2][:, :, k0:k1], AX.X, ALU.max, negate=True)\
                                .then_inc(s["max_step"], 1)
                            v.wait_ge(s["max_step"], l * NS + n + 1)
                            v.wait_ge(s["inv_ready"], l * SEQS * 2 + 2 * q + t + 1)
                            h0, h1 = hh[0][1], hh[1][1]
                            v.tensor_tensor(bias[n % 2][:], negmax[n % 2][:],
                                            inv[q % 2][t][:, 0, h0:h1 + 1:h1 - h0], ALU.mult)\
                                .then_inc(s["bias_ready"], 1)
                        elif kind == "norm_o":
                            _, q, t = it
                            n = O[it]
                            v.wait_ge(s["s_free"], l * NS + S[("score", q, 4 * t + 3)] + 1 + SL)
                            v.reciprocal(rowinv[t][:], rowsum[t][:]).then_inc(s["rowinv_ready"], 1)
                            v.wait_ge(s["rowinv_ready"], l * NO + n + 1 + SL)
                            v.wait_ge(s["o_full"], l * NO + n + 1)
                            v.wait_ge(s["t_full"], l * NT + SL + last_turn_o(it))
                            v.tensor_tensor(heads3(o_n[:]), heads3(psO[:]),
                                            rowinv[t][:].unsqueeze(2).broadcast_to([P, HEADS_D, DHD]), ALU.mult)\
                                .then_inc(s["o_free"], 1)
                        elif kind == "out_o":
                            _, q, t = it
                            v.wait_ge(s["w_full"], l * NW + W[it] + 1)
                            yt = y_tok[:, q * TPS + t, :]
                            v.tensor_tensor(yt, yt, psW[:, 0:E], ALU.add).then_inc(s["w_free"], 1)
                        elif kind == "shift":
                            v.wait_ge(s["w_full"], l * NW + W[it] + 1)
                            chain.link(v.tensor_copy(hs[:, :, E // 2:], psW[:, 0:E].rearrange("p (t e) -> p t e", t=TPS)))
                            v.sem_inc(s["w_free"], 1)
                            v.wait_ge(s["w_free"], l * NW + W[("out_o", q, 1)] + 2)
                            chain.link(v.tensor_copy(hs[:, :, 0:E // 2], y_tok[:, q * TPS:(q + 1) * TPS, 0:E // 2]))
                            b = mb[0]
                            for t in range(TPS):
                                ins = v.bn_stats(b["st"][:, t, :], hs[:, t, :])
                            chain.link(ins)
                            moments(v, chain, b, TPS).then_inc(s["var_ready"], 1)
                        elif kind == "norm_f":
                            v.wait_ge(s["rstd_ready"], l * SEQS + q + 1 + 2)
                            for t in range(TPS):
                                ins = v.tensor_scalar(hn[:, t, :], hs[:, t, :], mb[0]["mean"][:, t:t + 1],
                                                      mb[0]["rstd"][:, t:t + 1], ALU.subtract, ALU.mult)
                            ins.then_inc(s["hn_ready"], 1)
                            v.wait_ge(s["hn_ready"], l * SEQS + q + 1)
                        elif kind == "hidden":
                            f = it[2]
                            w = FD[f][1]
                            n, i = F[it], Q[it]
                            v.wait_ge(s["gelu_ready"], l * NF + n + 1)
                            v.scalar_tensor_tensor(mid[0:w, f, :], psQ[i % 2][0:w, 0:L], cols[0:w, D_BA + f:D_BA + f + 1],
                                                   gel[n % 2][0:w, :], ALU.add, ALU.mult).then_inc(s["mid_ready"], 1)
                            v.wait_ge(s["mid_ready"], l * NF + n + 1 + SL)
                            v.sem_inc(s["q_free"], 1)
                        elif kind == "out_f":
                            v.wait_ge(s["w_full"], l * NW + W[it] + 1)
                            yt = y_tok[:, q * TPS:(q + 1) * TPS, :].rearrange("p t e -> p (t e)")
                            v.tensor_tensor(yt, yt, psW[:, 0:2 * E], ALU.add).then_inc(s["w_free"], 1)
                    assert chain.n == CHAIN_D, chain.n
                v.wait_ge(s["w_free"], DEPTH * NW + 1)
                v.tensor_tensor(x_tok[:], x_tok[:], y_tok[:], ALU.add).then_inc(s["x_ready"], 1)
                v.wait_ge(s["x_ready"], 1)

            @block.tensor
            def _(p):
                p.sem_inc(s["t_full"], SL)
                p.wait_ge(s["y_ready"], 2)
                p.wait_ge(s["const_in"], 48)
                p.wait_ge(s["set_up"], 5)
                with p.Fori(0, DEPTH) as l:
                    p.wait_ge(s["weights_in"], (l + 1) * 7 * 16)
                    p.wait_ge(s["w_free"], l * NW + 1)

                    def bank(it):
                        n = TI[it]
                        p.wait_ge(s["t_free"], l * NT + n + 1)
                        return psT[n % 2]

                    def turned_in(it):
                        p.wait_ge(s["t_free"], l * NT + TI[it] + 1 + SL)

                    for it in items:
                        kind, q = it[0], it[1]
                        if kind == "turn_h":
                            ps = bank(it)
                            for t in range(TPS):
                                ins = p.transpose(ps[:, t * P:(t + 1) * P], y_tok[:, q * TPS + t, :], ident[:])
                            ins.then_inc(s["t_full"], 1)
                        elif kind == "project":
                            _, q, t, part = it
                            i = Q[it]
                            turned_in(("turn_h", q))
                            p.wait_ge(s["q_free"], l * NQ + i + 1)
                            p.matmul(psQ[i % 2][:], hT[q % 2][:, t * P:(t + 1) * P], wqkv[:, part, :],
                                     start=True, stop=True).then_inc(s["q_full"], 1)
                        elif kind == "turn_qk":
                            _, q, t, part = it
                            n = PR[("project", q, t, part)]
                            p.wait_ge(s["qk_ready"], l * NPR + n + 1 + SL)
                            ps = bank(it)
                            for c in range(CD):
                                ins = p.transpose(ps[:, c * P:(c + 1) * P], qk[n % 2][:, c * P:(c + 1) * P], ident[:])
                            ins.then_inc(s["t_full"], 1)
                        elif kind == "score":
                            g = it[2]
                            n = S[it]
                            t, a, hh = heads(g)
                            k0, k1 = keys(t)
                            turned_in(("turn_qk", q, t, 1))
                            p.wait_ge(s["s_free"], l * NS + n + 1)
                            out = psS[n % 2][:, :, k0:k1]
                            m0 = P * t
                            p.matmul(out, identb[:], mask[:, m0 + k0:m0 + k1].unsqueeze(1)
                                     .broadcast_to([P, 2, k1 - k0]), start=True, stop=True)
                            for j, (c, _) in enumerate(hh):
                                rows = slice(a * DHD, (a + 1) * DHD)
                                ins = p.matmul(psS[n % 2][:, j, k0:k1], qkT[q % 2][rows, 0, c, t * P:(t + 1) * P],
                                               qkT[q % 2][rows, 1, c, k0:k1], start=False, stop=True,
                                               skip_group_check=True)
                            ins.then_inc(s["s_full"], 1)
                        elif kind == "turn_p":
                            g = it[2]
                            t = heads(g)[0]
                            p.wait_ge(s["s_free"], l * NS + S[("score", q, g)] + 1 + SL)
                            ps = bank(it)
                            for j in range(2):
                                for b in range(t + 1):
                                    ins = p.transpose(ps[:, (2 * j + b) * P:(2 * j + b + 1) * P],
                                                      prob[t][g % 2][:, j, b * P:(b + 1) * P], ident[:])
                            ins.then_inc(s["t_full"], 1)
                        elif kind == "pv":
                            g = it[2]
                            t, a, hh = heads(g)
                            turned_in(("turn_p", q, g))
                            if g % 4 == 0:
                                p.wait_ge(s["o_free"], l * NO + O[("norm_o", q, t)] + 1)
                            for j, (_, h) in enumerate(hh):
                                for b in range(t + 1):
                                    ins = p.matmul(psO[:, h * DHD:(h + 1) * DHD], probT[g % 2][:, j, b, :],
                                                   val[q % 2][:, b, h * DHD:(h + 1) * DHD], start=(b == 0),
                                                   stop=(b == t))
                            if g % 4 == 3:
                                ins.then_inc(s["o_full"], 1)
                        elif kind == "turn_o":
                            _, q, t = it
                            p.wait_ge(s["o_free"], l * NO + O[("norm_o", q, t)] + 2)
                            ps = bank(it)
                            for c in range(CD):
                                ins = p.transpose(ps[:, c * P:(c + 1) * P], o_n[:, c * P:(c + 1) * P], ident[:])
                            ins.then_inc(s["t_full"], 1)
                        elif kind == "out_o":
                            _, q, t = it
                            turned_in(("turn_o", q, t))
                            p.wait_ge(s["w_free"], l * NW + W[it] + 1)
                            for c in range(CD):
                                ins = p.matmul(psW[:, 0:E], oT[:, c, :], wo[:, c, :], start=(c == 0),
                                               stop=(c == CD - 1))
                            ins.then_inc(s["w_full"], 1)
                        elif kind == "shift":
                            p.wait_ge(s["w_free"], l * NW + W[it] + 1)
                            p.matmul(psW[:, 0:E], down[:, 0, :], y_tok[:, q * TPS:(q + 1) * TPS, E // 2:],
                                     start=True, stop=True)
                            p.matmul(psW[:, E // 2:E], down[:, 1, :], y_tok[:, q * TPS, E // 2:],
                                     start=False, stop=True, skip_group_check=True).then_inc(s["w_full"], 1)
                        elif kind == "turn_f":
                            p.wait_ge(s["hn_ready"], l * SEQS + q + 1)
                            ps = bank(it)
                            for t in range(TPS):
                                ins = p.transpose(ps[:, t * P:(t + 1) * P], hn[:, t, :], ident[:])
                            ins.then_inc(s["t_full"], 1)
                        elif kind == "hidden":
                            f = it[2]
                            f0, w = FD[f]
                            i = Q[it]
                            turned_in(("turn_f", q))
                            p.wait_ge(s["q_free"], l * NQ + i + 1)
                            for k in range(2):
                                ins = p.matmul(psQ[i % 2][0:w, k * L:(k + 1) * L], w1[:, k, f0:f0 + w], fT[:],
                                               start=True, stop=True)
                            ins.then_inc(s["q_full"], 1)
                        elif kind == "out_f":
                            p.wait_ge(s["mid_ready"], l * NF + F[("hidden", q, NFD - 1)] + 1 + SL)
                            p.wait_ge(s["w_free"], l * NW + W[it] + 1)
                            for t in range(TPS):
                                out = psW[:, t * E:(t + 1) * E]
                                p.matmul(out, ones_row[:], b2row[:], start=True, stop=False)
                                for f, (_, w) in enumerate(FD):
                                    ins = p.matmul(out, mid[0:w, f, t * P:(t + 1) * P], w2[0:w, f, :], start=False,
                                                   stop=(f == NFD - 1))
                            ins.then_inc(s["w_full"], 1)


def layout_d(i, a):
    g = {n: i["L1_ffn_" + n] for n in ("wqkv", "q_scale", "k_scale", "wo", "ln_g", "ln_b", "w1", "b1", "w2", "b2")}
    a["d_wqkv"] = np.ascontiguousarray(g["wqkv"].reshape(DEPTH, E, 3, INNER_D))
    a["d_wo"] = np.ascontiguousarray(g["wo"].reshape(DEPTH, CD, P, E).transpose(0, 2, 1, 3))
    a["d_w1"] = np.ascontiguousarray(g["w1"].reshape(DEPTH, E, 2, HID_D))

    def pad(w):
        o = np.zeros((DEPTH, NFD * P) + w.shape[2:], np.float32)
        o[:, :HID_D] = w
        return o.reshape((DEPTH, NFD, P) + w.shape[2:])

    a["d_w2"] = np.ascontiguousarray(pad(g["w2"]).transpose(0, 2, 1, 3))
    ba, bg = (pad(g["b1"][:, k * HID_D:(k + 1) * HID_D]).transpose(0, 2, 1) for k in range(2))
    a["d_cols"] = np.ascontiguousarray(np.concatenate([g["ln_g"][:, :, None], g["ln_b"][:, :, None], ba, bg], axis=2))
    a["d_b2"] = np.ascontiguousarray(g["b2"][:, None])
    swap = np.concatenate([np.arange(DHD // 2, DHD), np.arange(DHD // 2)])
    gains = np.stack([g["q_scale"], g["q_scale"][:, swap], g["k_scale"], g["k_scale"][:, swap]], axis=1)
    a["d_gains"] = np.ascontiguousarray(np.broadcast_to(gains[:, None], (DEPTH, P, 4, DHD)))
    half = np.arange(0, DHD, 2, dtype=np.float32)
    pos = np.arange(L, dtype=np.float32)
    freq = pos[:, None] * (1.0 / np.float32(10000.0) ** (half / DHD))[None]
    freq = np.concatenate([freq, freq], axis=1)
    base = (half + 0.4 * DHD) / (1.4 * DHD)
    scale = base[None] ** ((pos - L // 2) / float(WINDOW // 2))[:, None]
    scale = np.concatenate([scale, scale], axis=1)
    sign = np.where(np.arange(DHD) < DHD // 2, -1.0, 1.0)
    cos, sin = np.cos(freq), np.sin(freq) * sign
    tab = np.stack([QK_SCALE * cos * scale, QK_SCALE * sin * scale, cos / scale, sin / scale])
    a["d_tables"] = np.ascontiguousarray(tab.reshape(4, TPS, P, DHD).transpose(2, 0, 1, 3)).astype(np.float32)
    q, k = np.arange(P)[:, None], np.arange(P)[None]
    keys, q1 = np.arange(L)[None], q + P
    second = np.where((keys <= q1) & (keys >= q1 - WINDOW), 0.0, MASKED)
    first = np.where((k <= q) & (k >= q - WINDOW), 0.0, MASKED)
    a["d_mask"] = np.concatenate([first, second], axis=1).astype(np.float32)
    down = np.zeros((P, 2, P), np.float32)
    down[np.arange(P - 1), 0, np.arange(1, P)] = 1.0
    down[P - 1, 1, 0] = 1.0
    a["d_down"] = down


def layout_a(i, a):
    a["a_wq"] = np.ascontiguousarray(i["L0_attn_Wq"].transpose(0, 2, 1))
    a["a_wk"] = np.ascontiguousarray(i["L0_attn_Wk"].transpose(0, 2, 1))
    a["a_w1"] = np.ascontiguousarray(i["L0_attn_W1"].transpose(0, 2, 1))
    a["a_w2"] = np.ascontiguousarray(i["L0_attn_W2"].transpose(0, 2, 1).reshape(LAYERS, FC, P, E).transpose(0, 2, 1, 3))
    b1 = i["L0_attn_b1"].reshape(LAYERS, FC, P).transpose(0, 2, 1)
    col = lambda *names: [i["L0_attn_" + n][:, :, None] for n in names]
    a["a_qk_cols"] = np.ascontiguousarray(np.concatenate(col("bq", "bk"), axis=2))
    a["a_cols2"] = np.ascontiguousarray(np.concatenate(col("ln2_w", "ln2_b"), axis=2))
    a["a_b1"] = np.ascontiguousarray(b1)
    a["a_b2"] = np.ascontiguousarray(col("b2")[0])
    a["a_cols3"] = np.ascontiguousarray(np.concatenate(col("ln3_w", "ln3_b"), axis=2))
    for k in (1, 3):
        rows = np.stack([i[f"L0_attn_ln{k}_w"], i[f"L0_attn_ln{k}_b"]], axis=1)
        a[f"a_rows{k}"] = np.ascontiguousarray(np.broadcast_to(rows[:, None], (LAYERS, P, 2, E)))
    a["a_heads"] = (np.arange(P)[:, None] // DH == np.arange(HEADS)[None]).astype(np.float32)
    pos = np.arange(L)
    a["rel"] = (HEADS * np.exp(-np.abs(pos[:, None] - pos[None, :]) / DECAY)).astype(np.float32)


def layout(i):
    a = {"x": np.ascontiguousarray(i["L0_attn_x"].reshape(NTOK, E)), "ident": np.eye(P, dtype=np.float32)}
    for f in LAYOUTS:
        f(i, a)
    return a


STAGES = [stage_a, stage_b, stage_c, stage_d]
LAYOUTS = [layout_a, layout_b, layout_c, layout_d]


def build(nc, d, out):
    with ExitStack() as ctx:
        x_tok = ctx.enter_context(nc.sbuf_tensor("x_tok", [P, T, E], F32))
        ident = ctx.enter_context(nc.sbuf_tensor("ident", [P, P], F32))
        minus_half = ctx.enter_context(nc.sbuf_tensor("minus_half", [P, T], F32))
        x_in = ctx.enter_context(nc.semaphore("x_in"))
        exponent_set = ctx.enter_context(nc.semaphore("exponent_set"))
        x_out = ctx.enter_context(nc.semaphore("x_out"))
        with nc.Block() as block:
            @block.sync
            def _(sp):
                sp.dma_start(x_tok[:], d["x"].rearrange("(t p) e -> p t e", p=P)).then_inc(x_in, 16)
                sp.dma_start(ident[:], d["ident"]).then_inc(x_in, 16)
                sp.wait_ge(x_in, 32)

            @block.gpsimd
            def _(g):
                g.memset(minus_half[:], -0.5).then_inc(exponent_set, 1)
                g.wait_ge(exponent_set, 1)

        for stage in STAGES:
            stage(nc, d, x_tok, ident, minus_half)
        with nc.Block() as block:
            @block.sync
            def _(sp):
                sp.dma_start(out.rearrange("(t p) e -> p t e", p=P), x_tok[:]).then_inc(x_out, 16)
                sp.wait_ge(x_out, 16)


def kernel(**inputs):
    import concourse.bacc as _bacc
    from concourse.bass_utils import run_bass_kernel_spmd as _run

    nc = _bacc.Bacc("TRN2", target_bir_lowering=False, num_devices=1)
    arrays = layout({k: np.asarray(v) for k, v in inputs.items()})
    aps = {k: nc.dram_tensor("in_" + k, v.shape, F32, kind="ExternalInput").ap() for k, v in arrays.items()}
    out = nc.dram_tensor("out", (NTOK, E), F32, kind="ExternalOutput").ap()
    build(nc, aps, out)
    r = _run(nc, [{"in_" + k: v for k, v in arrays.items()}], core_ids=[0])
    return r.results[0]["out"].reshape(SEQS, L, E)
```
